# Optimizing a Trainium2 kernel written in Bass

```python
import numpy as np
import jax
import jax.numpy as jnp

def _softmax(x, axis=-1):
    return jax.nn.softmax(x, axis=axis)

def _gelu(x):
    return jax.nn.gelu(x, approximate=True)

def _silu(x):
    return jax.nn.silu(x)

def _sigmoid(x):
    return jax.nn.sigmoid(x)

def _layernorm(x, axis=-1, eps=1e-05):
    m = jnp.mean(x, axis=axis, keepdims=True)
    v = jnp.var(x, axis=axis, keepdims=True)
    return (x - m) / jnp.sqrt(v + eps)

def _scatter_add(tgt, idx, src, axis=0):
    return tgt.at[idx].add(src)

def _segment_sum(src, seg, n):
    return jax.ops.segment_sum(src, seg, n)
kernel_name = 'mk_adaln_d2_jaxref_r8_89d2e4'

def setup_inputs(seed: int=0):
    np.random.seed(seed)
    _w = jnp.asarray

    def _L0_attn_setup():
        import jax, jax.numpy as jnp
        import numpy as np
        ATT_WIDTH = 64

        def _band_mask(T, width, dtype):
            lower = width // 2
            upper = (width - 1) // 2
            i = jnp.arange(T)[:, None]
            j = jnp.arange(T)[None, :]
            keep = (i - j <= lower) & (j - i <= upper)
            return keep.astype(dtype)
        key = jax.random.key(seed)
        k1, k2, k3, k4 = jax.random.split(key, 4)
        B, T, H, D = (8, 256, 128, 128)
        scale = 1.0 / np.sqrt(H)
        return {'inputs': jax.random.normal(k1, (B, T, H), dtype=jnp.float32), 'WQ': jax.random.normal(k2, (H, D), dtype=jnp.float32) * scale, 'WK': jax.random.normal(k3, (H, D), dtype=jnp.float32) * scale, 'WV': jax.random.normal(k4, (H, D), dtype=jnp.float32) * scale}
    _L0_attn_in = _L0_attn_setup()

    def _L0_ffn_setup():
        import jax, jax.numpy as jnp
        import numpy as np
        D_MODEL = 128
        D_HIDDEN = 512
        NUM_BANKS = 16
        NUM_SELECTED = 2
        key = jax.random.key(seed)
        ks = jax.random.split(key, 7)
        s = 0.02
        return {'tensor': jax.random.normal(ks[0], (4, 128, D_MODEL), dtype=jnp.float32), 'Wr': jax.random.normal(ks[1], (D_MODEL, NUM_BANKS), dtype=jnp.float32) * s, 'br': jnp.zeros((NUM_BANKS,), dtype=jnp.float32), 'W1': jax.random.normal(ks[2], (NUM_BANKS, D_MODEL, D_HIDDEN), dtype=jnp.float32) * s, 'b1': jnp.zeros((NUM_BANKS, D_HIDDEN), dtype=jnp.float32), 'W2': jax.random.normal(ks[3], (NUM_BANKS, D_HIDDEN, D_MODEL), dtype=jnp.float32) * s, 'b2': jnp.zeros((NUM_BANKS, D_MODEL), dtype=jnp.float32)}
    _L0_ffn_in = _L0_ffn_setup()
    _L0_c = _w((lambda *s: np.random.randn(*s).astype(np.float32) * 0.05)(1, 128))
    _L0_wmod = _w((lambda *s: np.random.randn(*s).astype(np.float32) * 0.05)(128, 6 * 128) * 128 ** (-0.5))

    def _L1_attn_setup():
        import jax, jax.numpy as jnp
        import numpy as np
        from jax import lax
        N_HEAD, D_HEAD, D_MODEL = (16, 64, 128)
        LN_EPS = 1e-05

        def _layer_norm(x, g, b):
            mu = jnp.mean(x, -1, keepdims=True)
            var = jnp.mean((x - mu) ** 2, -1, keepdims=True)
            return (x - mu) * lax.rsqrt(var + LN_EPS) * g + b
        key = jax.random.key(seed)
        ks = jax.random.split(key, 3)
        slen, bsz = (128, 16)
        h = jax.random.normal(ks[0], (slen, bsz, D_MODEL), dtype=jnp.float32)
        W_qkvb = jax.random.normal(ks[1], (N_HEAD * (3 * D_HEAD + 1), D_MODEL), dtype=jnp.float32) * D_MODEL ** (-0.5)
        W_o = jax.random.normal(ks[2], (D_MODEL, N_HEAD * D_HEAD), dtype=jnp.float32) * (N_HEAD * D_HEAD) ** (-0.5)
        ln_g = jnp.ones((D_MODEL,), dtype=jnp.float32)
        ln_b = jnp.zeros((D_MODEL,), dtype=jnp.float32)
        return {'h': h, 'W_qkvb': W_qkvb, 'W_o': W_o, 'ln_g': ln_g, 'ln_b': ln_b}
    _L1_attn_in = _L1_attn_setup()

    def _L1_ffn_setup():
        import jax, jax.numpy as jnp
        import numpy as np
        DIM = 128
        INTER = 176
        N_EXPERTS = 16
        TOPK = 2
        N_SHARED = 2
        SHARED_INTER = N_SHARED * INTER
        ROUTE_SCALE = 1.0
        key = jax.random.key(seed)
        ks = jax.random.split(key, 16)
        s = 0.02
        return {'x': jax.random.normal(ks[0], (2, 256, DIM), dtype=jnp.float32), 'gate_w': jax.random.normal(ks[1], (DIM, N_EXPERTS), dtype=jnp.float32) * s, 'gate_b': jnp.zeros((N_EXPERTS,), dtype=jnp.float32), 'w1': jax.random.normal(ks[2], (N_EXPERTS, DIM, INTER), dtype=jnp.float32) * s, 'b1': jnp.zeros((N_EXPERTS, INTER), dtype=jnp.float32), 'w3': jax.random.normal(ks[3], (N_EXPERTS, DIM, INTER), dtype=jnp.float32) * s, 'b3': jnp.zeros((N_EXPERTS, INTER), dtype=jnp.float32), 'w2': jax.random.normal(ks[4], (N_EXPERTS, INTER, DIM), dtype=jnp.float32) * s, 'b2': jnp.zeros((N_EXPERTS, DIM), dtype=jnp.float32), 'sw1': jax.random.normal(ks[5], (DIM, SHARED_INTER), dtype=jnp.float32) * s, 'sb1': jax.random.normal(ks[6], (SHARED_INTER,), dtype=jnp.float32) * s, 'sw3': jax.random.normal(ks[7], (DIM, SHARED_INTER), dtype=jnp.float32) * s, 'sb3': jax.random.normal(ks[8], (SHARED_INTER,), dtype=jnp.float32) * s, 'sw2': jax.random.normal(ks[9], (SHARED_INTER, DIM), dtype=jnp.float32) * s, 'sb2': jax.random.normal(ks[10], (DIM,), dtype=jnp.float32) * s}
    _L1_ffn_in = _L1_ffn_setup()
    _L1_c = _w((lambda *s: np.random.randn(*s).astype(np.float32) * 0.05)(1, 128))
    _L1_wmod = _w((lambda *s: np.random.randn(*s).astype(np.float32) * 0.05)(128, 6 * 128) * 128 ** (-0.5))
    _d = {'L0_attn_inputs': _L0_attn_in['inputs'], 'L0_attn_WQ': _L0_attn_in['WQ'], 'L0_attn_WK': _L0_attn_in['WK'], 'L0_attn_WV': _L0_attn_in['WV'], 'L0_ffn_Wr': _L0_ffn_in['Wr'], 'L0_ffn_br': _L0_ffn_in['br'], 'L0_ffn_W1': _L0_ffn_in['W1'], 'L0_ffn_b1': _L0_ffn_in['b1'], 'L0_ffn_W2': _L0_ffn_in['W2'], 'L0_ffn_b2': _L0_ffn_in['b2'], 'L0_c': _L0_c, 'L0_wmod': _L0_wmod, 'L1_attn_W_qkvb': _L1_attn_in['W_qkvb'], 'L1_attn_W_o': _L1_attn_in['W_o'], 'L1_attn_ln_g': _L1_attn_in['ln_g'], 'L1_attn_ln_b': _L1_attn_in['ln_b'], 'L1_ffn_gate_w': _L1_ffn_in['gate_w'], 'L1_ffn_gate_b': _L1_ffn_in['gate_b'], 'L1_ffn_w1': _L1_ffn_in['w1'], 'L1_ffn_b1': _L1_ffn_in['b1'], 'L1_ffn_w3': _L1_ffn_in['w3'], 'L1_ffn_b3': _L1_ffn_in['b3'], 'L1_ffn_w2': _L1_ffn_in['w2'], 'L1_ffn_b2': _L1_ffn_in['b2'], 'L1_ffn_sw1': _L1_ffn_in['sw1'], 'L1_ffn_sb1': _L1_ffn_in['sb1'], 'L1_ffn_sw3': _L1_ffn_in['sw3'], 'L1_ffn_sb3': _L1_ffn_in['sb3'], 'L1_ffn_sw2': _L1_ffn_in['sw2'], 'L1_ffn_sb2': _L1_ffn_in['sb2'], 'L1_c': _L1_c, 'L1_wmod': _L1_wmod}
    _x0 = _d['L0_attn_inputs']
    _d['L0_attn_inputs'] = jax.random.normal(jax.random.fold_in(jax.random.key(seed), 1), (1, 2048, 128), dtype=_x0.dtype)
    del _x0
    return _d

def reference(L0_attn_inputs, L0_attn_WQ, L0_attn_WK, L0_attn_WV, L0_ffn_Wr, L0_ffn_br, L0_ffn_W1, L0_ffn_b1, L0_ffn_W2, L0_ffn_b2, L0_c, L0_wmod, L1_attn_W_qkvb, L1_attn_W_o, L1_attn_ln_g, L1_attn_ln_b, L1_ffn_gate_w, L1_ffn_gate_b, L1_ffn_w1, L1_ffn_b1, L1_ffn_w3, L1_ffn_b3, L1_ffn_w2, L1_ffn_b2, L1_ffn_sw1, L1_ffn_sb1, L1_ffn_sw3, L1_ffn_sb3, L1_ffn_sw2, L1_ffn_sb2, L1_c, L1_wmod):

    def _L0_attn_ref(inputs, WQ, WK, WV):
        import jax, jax.numpy as jnp
        import numpy as np
        ATT_WIDTH = 64

        def _band_mask(T, width, dtype):
            lower = width // 2
            upper = (width - 1) // 2
            i = jnp.arange(T)[:, None]
            j = jnp.arange(T)[None, :]
            keep = (i - j <= lower) & (j - i <= upper)
            return keep.astype(dtype)
        B, T, H = inputs.shape
        D = WQ.shape[1]
        scale = jnp.asarray(D, inputs.dtype) ** 0.5
        q = jnp.einsum('bth,hd->btd', inputs, WQ)
        k = jnp.einsum('bth,hd->btd', inputs, WK)
        v = jnp.einsum('bth,hd->btd', inputs, WV)
        score = jnp.einsum('bqd,bkd->bqk', q, k) / scale
        local = _band_mask(T, ATT_WIDTH, score.dtype)
        score = score * local[None, :, :]
        attn = jax.nn.softmax(score, axis=-1)
        return jnp.einsum('bqk,bkd->bqd', attn, v)

    def _L0_ffn_ref(tensor, Wr, br, W1, b1, W2, b2):
        import jax, jax.numpy as jnp
        import numpy as np
        D_MODEL = 128
        D_HIDDEN = 512
        NUM_BANKS = 16
        NUM_SELECTED = 2
        logits = jnp.einsum('bsd,de->bse', tensor, Wr) + br
        probs = jax.nn.softmax(logits, axis=-1)
        topv, topi = jax.lax.top_k(probs, NUM_SELECTED)
        gate = jnp.sum(jax.nn.one_hot(topi, NUM_BANKS, dtype=tensor.dtype) * topv[..., None], axis=-2)
        h = jax.nn.relu(jnp.einsum('bsd,edh->bseh', tensor, W1) + b1)
        y = jnp.einsum('bseh,ehm->bsem', h, W2) + b2
        out = jnp.einsum('bse,bsem->bsm', gate, y)
        return out

    def _L1_attn_ref(h, W_qkvb, W_o, ln_g, ln_b):
        import jax, jax.numpy as jnp
        import numpy as np
        from jax import lax
        N_HEAD, D_HEAD, D_MODEL = (16, 64, 128)
        LN_EPS = 1e-05

        def _layer_norm(x, g, b):
            mu = jnp.mean(x, -1, keepdims=True)
            var = jnp.mean((x - mu) ** 2, -1, keepdims=True)
            return (x - mu) * lax.rsqrt(var + LN_EPS) * g + b
        slen, bsz, _ = h.shape
        BH = bsz * N_HEAD
        qkvb = jnp.einsum('sbd,ed->sbe', h, W_qkvb).reshape(slen, BH, 3 * D_HEAD + 1)
        q, k, v, beta = jnp.split(qkvb, [D_HEAD, 2 * D_HEAD, 3 * D_HEAD], axis=-1)
        beta = jax.nn.sigmoid(beta)
        q = jax.nn.elu(q) + 1.0
        k = jax.nn.elu(k) + 1.0
        q = q / jnp.sum(q, -1, keepdims=True)
        k = k / jnp.sum(k, -1, keepdims=True)

        def step(W, inp):
            k_t, v_t, q_t, b_t = inp
            v_old = jnp.einsum('bij,bj->bi', W, k_t)
            v_ins = b_t * (v_t - v_old)
            W = W + v_ins[:, :, None] * k_t[:, None, :]
            out = jnp.einsum('bij,bj->bi', W, q_t)
            return (W, out)
        W0 = jnp.zeros((BH, D_HEAD, D_HEAD), dtype=h.dtype)
        _, outs = lax.scan(step, W0, (k, v, q, beta))
        scale = 1.0 / D_HEAD ** 0.5
        layer_out = (scale * outs).reshape(slen, bsz, N_HEAD * D_HEAD)
        attn_out = jnp.einsum('sbe,de->sbd', layer_out, W_o)
        return _layer_norm(h + attn_out, ln_g, ln_b)

    def _L1_ffn_ref(x, gate_w, gate_b, w1, b1, w3, b3, w2, b2, sw1, sb1, sw3, sb3, sw2, sb2):
        import jax, jax.numpy as jnp
        import numpy as np
        DIM = 128
        INTER = 176
        N_EXPERTS = 16
        TOPK = 2
        N_SHARED = 2
        SHARED_INTER = N_SHARED * INTER
        ROUTE_SCALE = 1.0
        shape = x.shape
        xf = x.reshape(-1, DIM)
        logits = xf @ gate_w + gate_b
        scores = jax.nn.softmax(logits.astype(jnp.float32), axis=-1)
        top_vals, top_idx = jax.lax.top_k(scores, TOPK)
        weights = (top_vals * ROUTE_SCALE).astype(x.dtype)
        cw = (jax.nn.one_hot(top_idx, N_EXPERTS, dtype=x.dtype) * weights[..., None]).sum(axis=1)
        h = jnp.einsum('td,edh->teh', xf, w1) + b1
        g = jnp.einsum('td,edh->teh', xf, w3) + b3
        a = jax.nn.silu(h) * g
        y = jnp.einsum('teh,ehd,te->td', a, w2, cw) + cw @ b2
        z = jax.nn.silu(xf @ sw1 + sb1) * (xf @ sw3 + sb3) @ sw2 + sb2
        return (y + z).reshape(shape)
    x = L0_attn_inputs
    mod = (_silu(L0_c) @ L0_wmod).reshape(L0_c.shape[0], 6, 1, -1)
    sa, ca, ga, sb, cb, gb = (mod[:, 0], mod[:, 1], mod[:, 2], mod[:, 3], mod[:, 4], mod[:, 5])
    ga = (2 * (ga >= 0) - 1) * jnp.maximum(jnp.abs(ga), 0.25)
    gb = (2 * (gb >= 0) - 1) * jnp.maximum(jnp.abs(gb), 0.25)
    h = _layernorm(x, axis=-1) * (1 + ca) + sa
    x = x + ga * _L0_attn_ref(h, L0_attn_WQ, L0_attn_WK, L0_attn_WV)
    h = _layernorm(x, axis=-1) * (1 + cb) + sb
    x = x + gb * _L0_ffn_ref(h, L0_ffn_Wr, L0_ffn_br, L0_ffn_W1, L0_ffn_b1, L0_ffn_W2, L0_ffn_b2)
    mod = (_silu(L1_c) @ L1_wmod).reshape(L1_c.shape[0], 6, 1, -1)
    sa, ca, ga, sb, cb, gb = (mod[:, 0], mod[:, 1], mod[:, 2], mod[:, 3], mod[:, 4], mod[:, 5])
    ga = (2 * (ga >= 0) - 1) * jnp.maximum(jnp.abs(ga), 0.25)
    gb = (2 * (gb >= 0) - 1) * jnp.maximum(jnp.abs(gb), 0.25)
    h = _layernorm(x, axis=-1) * (1 + ca) + sa
    x = x + ga * _L1_attn_ref(h, L1_attn_W_qkvb, L1_attn_W_o, L1_attn_ln_g, L1_attn_ln_b)
    h = _layernorm(x, axis=-1) * (1 + cb) + sb
    x = x + gb * _L1_ffn_ref(h, L1_ffn_gate_w, L1_ffn_gate_b, L1_ffn_w1, L1_ffn_b1, L1_ffn_w3, L1_ffn_b3, L1_ffn_w2, L1_ffn_b2, L1_ffn_sw1, L1_ffn_sb1, L1_ffn_sw3, L1_ffn_sb3, L1_ffn_sw2, L1_ffn_sb2)
    return x

_drawn_inputs = setup_inputs


def setup_inputs(seed=0):
    import zlib

    import numpy as np

    out = dict(_drawn_inputs(seed))
    spreads = {'L0_ffn_br': (0.0, 0.8),
     'L0_ffn_b1': (0.0, 0.8),
     'L0_ffn_b2': (0.0, 0.8),
     'L1_attn_ln_g': (1.0, 0.2),
     'L1_attn_ln_b': (0.0, 0.345),
     'L1_ffn_gate_b': (0.0, 0.8),
     'L1_ffn_b1': (0.0, 0.8),
     'L1_ffn_b3': (0.0, 0.8),
     'L1_ffn_b2': (0.0, 0.8)}
    factors = {'L0_attn_WQ': 8.0,
     'L0_attn_WK': 8.0,
     'L0_attn_WV': 8.0,
     'L0_ffn_Wr': 8.0,
     'L0_ffn_W1': 8.0,
     'L0_ffn_W2': 8.0,
     'L0_c': 7.294,
     'L0_wmod': 7.706,
     'L1_attn_W_qkvb': 30.808,
     'L1_attn_W_o': 31.311,
     'L1_ffn_gate_w': 8.0,
     'L1_ffn_w1': 8.0,
     'L1_ffn_w3': 8.0,
     'L1_ffn_w2': 8.0,
     'L1_ffn_sw1': 8.0,
     'L1_ffn_sb1': 8.0,
     'L1_ffn_sw3': 8.0,
     'L1_ffn_sb3': 8.0,
     'L1_ffn_sw2': 8.0,
     'L1_ffn_sb2': 29.335}
    for name, (base, spread) in spreads.items():
        noise = np.random.default_rng([zlib.crc32(name.encode()), seed]).standard_normal(out[name].shape)
        drawn = base * np.exp(spread * noise) if base else spread * noise
        out[name] = jnp.asarray(drawn.astype(out[name].dtype))
    for name, factor in factors.items():
        out[name] = (out[name] * factor).astype(out[name].dtype)
    return out
```

```python
from contextlib import ExitStack

import concourse.bass as bass
from concourse import mybir

ALU = mybir.AluOpType
ACT = mybir.ActivationFunctionType
AX_X = mybir.AxisListType.X
F32 = mybir.dt.float32
BF16 = mybir.dt.bfloat16
I32 = mybir.dt.int32
U32 = mybir.dt.uint32

P = 128
EPS = 1e-5


def after(eng, sem, n):
    if isinstance(n, int) and n <= 0:
        return
    eng.wait_ge(sem, n)


def settle(eng, passed):
    eng.sem_inc(passed, 1)


def run_tiles(eng, n, unroll, work):
    deepest = max(lag for lag, _ in work)
    head = (-(-deepest // unroll) + 1) * unroll
    for s in range(head):
        for lag, stage in work:
            if 0 <= s - lag:
                stage(s - lag, (s - lag) % unroll)
    with eng.Fori(head // unroll, n // unroll) as j:
        for u in range(unroll):
            for lag, stage in work:
                stage(unroll * j + (u - lag), (u - lag) % unroll)
    for s in range(n, n + deepest):
        for lag, stage in work:
            if s - lag < n:
                stage(s - lag, (s - lag) % unroll)


def build(nc, x, WQ, WK, WV, Wr0, br0, W1, b1, W2, b2, c01, wmod0, wmod1,
          WqkvbT, WoT, ln_g, ln_b, Wr1, br1, w1, b1e, w3, b3e, w2, b2e,
          sw1, sb1, sw3, sb3, sw2, sb2, out):
    T, D = x.shape
    NT = T // P
    E = Wr0.shape[1]
    H0 = W1.shape[2]
    C0 = H0 // P
    H1 = w1.shape[2]
    K1 = H1 // 2
    HS = sw1.shape[1]
    SC = [(a, min(P, HS - a)) for a in range(0, HS, P)]
    NH = 16
    DH = (WqkvbT.shape[1] - NH) // (3 * NH)
    HD = NH * DH
    BAND = 32
    WIN = P + 2 * BAND
    PADT = T + 2 * BAND
    TOPK = 2
    SLOTS = -(-(TOPK * T // P + E - 1) // 4) * 4
    REGION = T + P
    SPARE = SLOTS - TOPK * T // P
    DUMMY = E * REGION
    ROWS = DUMMY + SPARE * P
    NB = 4
    assert D == P and T % (2 * P) == 0 and SLOTS <= P

    xs = [nc.dram_tensor(f"sorted_tokens_{l}", [ROWS, D], F32, kind="Internal").ap() for l in range(2)]
    ys = [nc.dram_tensor(f"slot_results_{l}", [SLOTS * P, D], F32, kind="Internal").ap() for l in range(2)]

    with ExitStack() as ctx:
        def sb(name, shape, dt=F32):
            return ctx.enter_context(nc.sbuf_tensor(name, shape, dt))

        def sem(name):
            return ctx.enter_context(nc.semaphore(name))

        bank = ctx.enter_context(nc.psum_tensor("bank", [P, 8, 512], F32))

        xres = sb("xres", [P, NT * D])
        hT = sb("hT", [P, PADT])
        big = sb("big", [P, 2 * E * H0])
        W1s = big[:, 0:E * H0]
        W2s = big[:, E * H0:2 * E * H0]
        o13, o2, ob = 0, 2 * E * H1, 2 * E * H1 + 2 * E * D
        w13s = big[:, o13:o13 + 2 * E * H1]
        w2s = big[0:K1, o2:o2 + 2 * E * D]
        bias_big = sb("bias_big", [P, E * H0])
        b2B = sb("b2B", [P, E * D])
        Wa = sb("Wa", [P, 3, D])
        Wqkvb = sb("Wqkvb", [P, 3 * HD + NH])
        Wo = sb("Wo", [P, HD // P, D])
        Wr = sb("Wr", [P, 2, E])
        brB = sb("brB", [P, 2, E])
        sw13 = sb("sw13", [P, 2, HS])
        sw2s = sb("sw2s", [P, len(SC), D])
        sb13 = sb("sb13", [P, 2, len(SC)])
        sb2r = sb("sb2r", [1, D])
        lnB = sb("lnB", [P, 2, D])
        cT = sb("cT", [P, 2])

        ident = sb("ident", [P, P])
        band = sb("band", [P, WIN])
        before = sb("before", [P, P], BF16)
        ones = sb("ones", [P, P], BF16)
        onerow = sb("onerow", [1, P])
        zeros = sb("zeros", [P, D])
        expert_id = sb("expert_id", [P, E])
        region_at = sb("region_at", [P, E])
        upto = sb("upto", [E, E])
        slot_id = sb("slot_id", [P, 1])
        eps = sb("eps", [P, 1])

        sc = sb("sc", [P, 6, 2])
        siluB = sb("siluB", [P, 2, P])
        mcol = sb("mcol", [P, 2, 4])
        gB = sb("gB", [P, 2, 2, D])
        gtmp = sb("gtmp", [P, 3, D])
        lnG = sb("lnG", [P, 2, D])

        hsum = sb("hsum", [P, NT])
        hsumB = sb("hsumB", [P, P])
        vtot = sb("vtot", [P, D])
        hwin = sb("hwin", [P, 2, P])
        qT = sb("qT", [P, 2, P])
        sm = sb("sm", [P, 2, WIN])
        pr = sb("pr", [P, 2, WIN])
        pT = sb("pT", [P, 2, 2 * P])
        ao = sb("ao", [P, D])
        st6 = sb("st6", [P, 8, 2])
        gates = sb("gates", [P, 2, NT, 2])
        chosen = sb("chosen", [P, 2, NT, 2])
        where = sb("where", [P, 2, NT, 2])
        result_at = sb("result_at", [P, 2, NT, 2], I32)
        slot_shift = sb("slot_shift", [P, 3, E])
        shifts = sb("shifts", [P, 2 * NT])
        match = sb("match", [P, 2 * NT, E])
        posb = sb("posb", [P, 4], I32)
        gidx = sb("gidx", [P, 4], I32)
        macc = sb("macc", [P, 2, E], BF16)
        slot_vals = sb("slot_vals", [P, 2])
        tbl = sb("tbl", [1, 2 * P + E], I32)
        tiles_per = sb("tiles_per", [E, P])
        tiles_int = sb("tiles_int", [E, 2, P], I32)
        cumt = sb("cumt", [P, 3, E])
        sl = sb("sl", [P, 3])
        sums = sb("sums", [P, 6, NH])
        qk_sums = sb("qk_sums", [P, 2, NH])
        eb = sb("eb", [P, 4, NH])
        mix = sb("mix", [P, 3, D])

        work = sb("work", [P, 7168])
        wmod = work[:, 4352:4352 + 12 * D].rearrange("p (l n) -> p l n", l=2)
        kT = work[:, 0:PADT]
        V = work[:, PADT:PADT + (NT + 1) * D]
        ef = work[:, 0:2 * HD]
        rf = work[:, 2 * HD:4 * HD]
        vc = work[:, 4 * HD:5 * HD]
        vT = work[:, 5 * HD:6 * HD]
        h3T = [work[:, 6 * HD + P * b:6 * HD + P * b + P] for b in range(2)]
        yg = [work[:, 6 * HD + 2 * P + 2 * D * b:6 * HD + 2 * P + 2 * D * (b + 1)] for b in range(2)]
        ya = [work[:, 6 * HD + 6 * P + D * b:6 * HD + 6 * P + D * (b + 1)] for b in range(2)]
        xg = [work[:, D * b:D * b + D] for b in range(NB)]
        xgT = [work[:, 512 + P * b:512 + P * b + P] for b in range(2)]
        hb = [work[:, 1024 + H0 * b:1024 + H0 * (b + 1)] for b in range(2)]
        hbT = [work[:, 2048 + H0 * b:2048 + H0 * (b + 1)] for b in range(2)]
        yo = [work[:, 3072 + D * b:3072 + D * b + D] for b in range(NB)]
        act1 = [work[:, 3584 + 256 * b:3584 + 256 * b + H1] for b in range(2)]
        shT = [work[:, 4096 + 512 * c:4096 + 512 * (c + 1)] for c in range(2 * len(SC))]

        s_consts = sem("constants_made")
        passed = sem("passed")
        ld_x, ld_c, ld_attn, ld_router = sem("ld_x"), sem("ld_c"), sem("ld_attn"), sem("ld_router")
        ld_w0, ld_w1, ld_l1 = sem("ld_experts0"), sem("ld_experts1"), sem("ld_layer1")
        s_silu_act, s_silu = sem("silu_exp"), sem("silu_steps")
        s_mod, s_mod_used, s_mod_ready = sem("mod_products"), sem("mod_used"), sem("mod_ready")

        def layer_norm(name):
            return {
                "stats": sb(name + "_stats", [P, 2, 6]),
                "mv": sb(name + "_mv", [P, 2, 2]),
                "r": sb(name + "_r", [P, 2, 2]),
                "xn": sb(name + "_xn", [P, 2, D]),
                "moments": sem(name + "_moments"),
                "rstd": sem(name + "_rstd"),
                "normed": sem(name + "_normed"),
            }

        def ln_measure(dve, n, src, t, b):
            settle(dve, passed)
            dve.bn_stats(n["stats"][:, b, :], src).then_inc(n["moments"], 1)
            dve.wait_ge(n["moments"], 2 * t + 1)
            after(dve, n["normed"], t - 1)
            settle(dve, passed)
            dve.bn_aggr(n["mv"][:, b, :], n["stats"][:, b, :]).then_inc(n["moments"], 1)

        def ln_deviation(act, n, t, b):
            act.wait_ge(n["moments"], 2 * t + 2)
            act.activation(n["r"][:, b, 0:1], n["mv"][:, b, 1:2], ACT.Ln, bias=eps[:, :]).then_inc(n["rstd"], 1)
            act.wait_ge(n["rstd"], 2 * t + 1)
            act.activation(n["r"][:, b, 1:2], n["r"][:, b, 0:1], ACT.Exp, scale=-0.5).then_inc(n["rstd"], 1)

        def ln_scale(dve, n, src, t, b):
            dve.wait_ge(n["rstd"], 2 * t + 2)
            dve.tensor_scalar(n["xn"][:, b, :], src, n["mv"][:, b, 0:1], n["r"][:, b, 1:2],
                              ALU.subtract, ALU.mult).then_inc(n["normed"], 1)

        PICK, RANK, GATE = 6, 5, 3

        def router(layer, ln, scale_shift, logits_ps, rank_ps, xT_ps):
            n = f"router{layer}_"
            return {
                "layer": layer, "ln": ln, "ss": scale_shift,
                "logits_ps": logits_ps, "rank_ps": rank_ps, "xT_ps": xT_ps,
                "hb": sb(n + "hT", [P, 2, P]),
                "lg": sb(n + "lg", [P, 2, E]),
                "top": sb(n + "top", [P, 2, 8]),
                "ti": sb(n + "ti", [P, 2, 8], U32),
                "hot": sb(n + "hot", [P, 2, 2, E]),
                "pick": sb(n + "pick", [P, 2, E], BF16),
                "nl": sb(n + "nl", [P, 2, 1]),
                "ex": sb(n + "ex", [P, 2, E]),
                "se": sb(n + "se", [P, 2, 4]),
                "rk": sb(n + "rk", [P, 2, E]),
                "sel": sb(n + "sel", [P, 2, 2, E]),
                "xT": sem(n + "xT"),
                "h": sem(n + "h"),
                "logits": sem(n + "logits"),
                "picked": sem(n + "picked"),
                "exps": sem(n + "exps"),
                "rank": sem(n + "rank"),
                "placed": sem(n + "placed"),
                "gated": sem(n + "gated"),
                "sent": [sem(n + f"sent{b}") for b in range(2)],
            }

        def pe_transpose(pe, r, t, b):
            pe.wait_ge(r["ln"]["normed"], t + 1)
            after(pe, r["h"], t)
            pe.transpose(r["xT_ps"], r["ln"]["xn"][:, b, :], ident[:, :]).then_inc(r["xT"], 1)

        def act_modulate(act, r, t, b):
            act.wait_ge(r["xT"], t + 1)
            after(act, r["logits"], t - 1)
            act.activation(r["hb"][:, b, :], r["xT_ps"], ACT.Identity,
                           bias=r["ss"][0], scale=r["ss"][1]).then_inc(r["h"], 1)

        def pe_logits(pe, r, t, b):
            pe.wait_ge(r["h"], t + 1)
            after(pe, r["placed"], RANK * t - 2)
            pe.matmul(r["logits_ps"], r["hb"][:, b, :], Wr[:, r["layer"], :],
                      start=True, stop=True).then_inc(r["logits"], 1)

        def dve_pick(dve, r, t, b):
            k = PICK * t
            dve.wait_ge(r["logits"], t + 1)
            dve.tensor_tensor(r["lg"][:, b, :], r["logits_ps"], brB[:, r["layer"], :],
                              ALU.add).then_inc(r["picked"], 1)
            dve.wait_ge(r["picked"], k + 1)
            settle(dve, passed)
            dve.max(r["top"][:, b, :], r["lg"][:, b, :]).then_inc(r["picked"], 1)
            dve.wait_ge(r["picked"], k + 2)
            dve.tensor_scalar(r["nl"][:, b, :], r["top"][:, b, 0:1], -1.0, None,
                              ALU.mult).then_inc(r["picked"], 1)
            dve.max_index(r["ti"][:, b, :], r["top"][:, b, :], r["lg"][:, b, :]).then_inc(r["picked"], 1)
            dve.wait_ge(r["picked"], k + 4)
            mine = chosen[:, r["layer"], bass.ds(t, 1), :].rearrange("p a k -> p (a k)")
            dve.tensor_scalar(mine, r["ti"][:, b, 0:2], 1.0, None, ALU.mult).then_inc(r["picked"], 1)
            dve.wait_ge(r["picked"], k + 5)
            dve.tensor_tensor(r["hot"][:, b, :, :], expert_id[:, :].unsqueeze(1).to_broadcast([P, 2, E]),
                              mine.unsqueeze(2).to_broadcast([P, 2, E]),
                              ALU.is_equal).then_inc(r["picked"], 1)
            dve.wait_ge(r["picked"], k + 6)
            after(dve, r["rank"], t - 1)
            dve.tensor_tensor(r["pick"][:, b, :], r["hot"][:, b, 0, :], r["hot"][:, b, 1, :],
                              ALU.add).then_inc(r["placed"], 1)

        def act_exps(act, r, t, b):
            act.wait_ge(r["picked"], PICK * t + 3)
            after(act, r["gated"], GATE * (t - 1))
            act.activation(r["ex"][:, b, :], r["lg"][:, b, :], ACT.Exp, bias=r["nl"][:, b, :],
                           accum_out=r["se"][:, b, 0:1]).then_inc(r["exps"], 1)
            act.activation(r["se"][:, b, 2:4], r["top"][:, b, 0:2], ACT.Exp,
                           bias=r["nl"][:, b, :]).then_inc(r["exps"], 1)

        def pe_rank(pe, r, t, b):
            pe.wait_ge(r["placed"], RANK * t + 1)
            pe.matmul(r["rank_ps"], before[:, :], r["pick"][:, b, :], start=True, stop=False)
            pe.matmul(r["rank_ps"], ones[:, :], macc[:, r["layer"], :], start=False,
                      stop=True).then_inc(r["rank"], 1)

        def dve_place(dve, r, t, b):
            k = RANK * t
            dve.wait_ge(r["rank"], t + 1)
            dve.tensor_tensor(macc[:, r["layer"], :], macc[:, r["layer"], :], r["pick"][:, b, :],
                              ALU.add).then_inc(r["placed"], 1)
            dve.tensor_tensor(r["rk"][:, b, :], r["rank_ps"], region_at[:, :],
                              ALU.add).then_inc(r["placed"], 1)
            dve.wait_ge(r["placed"], k + 3)
            dve.tensor_tensor(r["sel"][:, b, :, :], r["hot"][:, b, :, :],
                              r["rk"][:, b, :].unsqueeze(1).to_broadcast([P, 2, E]),
                              ALU.mult).then_inc(r["placed"], 1)
            dve.wait_ge(r["placed"], k + 4)
            if not (isinstance(t, int) and t < 2):
                dve.wait_ge(r["sent"][b], 16 * (t - b))
            with nc.allow_low_precision("row numbers below 2 ** 24 are exact"):
                rows = where[:, r["layer"], bass.ds(t, 1), :].rearrange("p a k -> p (a k)")
                dve.tensor_reduce(rows, r["sel"][:, b, :, :], AX_X,
                                  ALU.add).then_inc(r["placed"], 1)
            dve.wait_ge(r["placed"], k + 5)
            dve.tensor_scalar(posb[:, 2 * b:2 * b + 2], rows, 1.0, None, ALU.mult).then_inc(r["gated"], 1)
            dve.wait_ge(r["exps"], 2 * t + 2)
            dve.reciprocal(r["se"][:, b, 1:2], r["se"][:, b, 0:1]).then_inc(r["gated"], 1)
            dve.wait_ge(r["gated"], GATE * t + 2)
            dve.tensor_scalar(gates[:, r["layer"], bass.ds(t, 1), :].rearrange("p a k -> p (a k)"),
                              r["se"][:, b, 2:4], r["se"][:, b, 1:2], None, ALU.mult).then_inc(r["gated"], 1)

        def pool_send(pool, r, t, b):
            pool.wait_ge(r["gated"], GATE * t + 1)
            settle(pool, passed)
            for k in range(TOPK):
                pool.indirect_dma_start(xs[r["layer"]], bass.IndirectOffsetOnAxis(posb[:, 2 * b + k:2 * b + k + 1], 0),
                                        r["ln"]["xn"][:, b, :], None).then_inc(r["sent"][b], 16)

        ln1, ln2, ln3, ln4, ln5 = (layer_norm(f"ln{k}") for k in range(1, 6))
        router0 = router(0, ln2, (mcol[:, 0, 2:3], mcol[:, 0, 3:4]), bank[:, 6, 0:E], bank[:, 6, E:2 * E],
                         bank[:, 5, 0:P])
        router1 = router(1, ln5, (mcol[:, 1, 2:3], mcol[:, 1, 3:4]), bank[:, 6, 0:E], bank[:, 6, E:2 * E],
                         bank[:, 6, P:2 * P])
        turned1, beta = bank[:, 7, 0:P], bank[:, 7, P:P + NH]
        attn1 = bank[:, 6, 2 * P:3 * P]
        ends = (0, 7)
        routers = [router0, router1]

        a_xT, a_h, a_win = sem("a_xT"), sem("a_h"), sem("a_window")
        a_kv, a_k, a_v = sem("a_kv"), sem("a_k_copied"), sem("a_v_copied")
        a_hs, a_vt, a_vtc = sem("a_hsum"), sem("a_vtot"), sem("a_vtot_copied")
        b_q, b_qT, b_s, b_sm = sem("b_q"), sem("b_qT"), sem("b_scores"), sem("b_masked")
        b_nm, b_p, b_pp, b_pT, b_pTc = sem("b_negmax"), sem("b_exp"), sem("b_probs"), sem("b_pT"), sem("b_pTc")
        b_o, b_x = sem("b_out"), sem("b_x")
        t_cnt, t_dve, t_cum, t_val, t_ready, t_rows = (sem("t_counts"), sem("t_dve"), sem("t_cumulated"),
                                               sem("t_values"), sem("t_ready"), sem("t_rows"))
        z_sent = sem("zero_rows_sent")
        e_x = [sem(f"e_x{b}") for b in range(NB)]
        e_y = [sem(f"e_y{b}") for b in range(NB)]
        e_xT, e_xTc, e_h, e_hb, e_hT, e_hTc, e_o, e_yo = (
            sem("e_xT"), sem("e_xTc"), sem("e_hidden"), sem("e_hb"), sem("e_hT"), sem("e_hTc"),
            sem("e_out"), sem("e_yo"))
        e_silu, e_act = sem("e_silu"), sem("e_act")
        d_gi, d_x = sem("d_gather_index"), sem("d_x")
        d_g = [sem(f"d_gathered{b}") for b in range(2)]
        d_xT, d_h, d_q, d_k, d_v, d_b = sem("d_xT"), sem("d_h"), sem("d_q"), sem("d_k"), sem("d_v"), sem("d_beta")
        DS = 9
        d_eb = sem("d_exp_beta")
        d_e, d_f, d_qk, d_sum = sem("d_exp"), sem("d_feature"), sem("d_qk"), sem("d_sums")
        d_vT, d_vTc, d_o, d_y = sem("d_vT"), sem("d_vTc"), sem("d_out"), sem("d_y")
        f_in, f_h, f_a, f_g, f_o, f_x = (sem("f_in"), sem("f_hidden"), sem("f_act"), sem("f_gated"), sem("f_out"),
                                        sem("f_x"))
        g_i, g_x, g_st = sem("g_index"), sem("g_x"), sem("g_stored")
        g_g = [sem(f"g_gathered{b}") for b in range(2)]

        def all_row(ap, n):
            return ap.rearrange("(a n) -> a n", a=1).to_broadcast([P, n])

        def xt(t):
            return xres[:, bass.ds(t * D, D)]

        block = ctx.enter_context(nc.Block())

        @block.sync
        def _(sp):
            sp.dma_start(cT[:, :], c01).then_inc(ld_c, 16)
            sp.dma_start(wmod[:, 0, :], wmod0).then_inc(ld_c, 16)
            sp.dma_start(wmod[:, 1, :], wmod1).then_inc(ld_c, 16)
            sp.dma_start(xres[:, :].rearrange("p (t d) -> p t d", d=D),
                         x.rearrange("(t p) d -> p t d", p=P)).then_inc(ld_x, 16)
            for k, w in enumerate((WQ, WK, WV)):
                sp.dma_start(Wa[:, k, :], w).then_inc(ld_attn, 16)
            for k, (w, b) in enumerate(((Wr0, br0), (Wr1, br1))):
                sp.dma_start(Wr[:, k, :], w).then_inc(ld_router, 16)
                sp.dma_start(brB[:, k, :], all_row(b, E)).then_inc(ld_router, 16)
            sp.dma_start(W1s.rearrange("p (e h) -> p e h", e=E), W1.rearrange("e d h -> d e h")).then_inc(ld_w0, 16)
            sp.dma_start(W2s.rearrange("p (e c d) -> p e c d", e=E, c=C0),
                         W2.rearrange("e (c p) d -> p e c d", p=P)).then_inc(ld_w0, 16)
            sp.dma_start(bias_big[:, :], all_row(b1.rearrange("e h -> (e h)"), E * H0)).then_inc(ld_w0, 16)
            sp.dma_start(b2B[:, :], all_row(b2.rearrange("e d -> (e d)"), E * D)).then_inc(ld_w0, 16)
            sp.dma_start(Wqkvb[:, :], WqkvbT).then_inc(ld_l1, 16)
            sp.dma_start(Wo[:, :, :], WoT.rearrange("(c p) d -> p c d", p=P)).then_inc(ld_l1, 16)
            for k, w in enumerate((ln_g, ln_b)):
                sp.dma_start(lnB[:, k, :], all_row(w, D)).then_inc(ld_l1, 16)
            for k, (w, b) in enumerate(((sw1, sb1), (sw3, sb3))):
                sp.dma_start(sw13[:, k, :], w).then_inc(ld_l1, 16)
                for c, (a, m) in enumerate(SC):
                    sp.dma_start(sb13[0:m, k, c:c + 1], b[a:a + m].rearrange("(p a) -> p a", a=1)).then_inc(ld_l1, 16)
            for c, (a, m) in enumerate(SC):
                sp.dma_start(sw2s[0:m, c, :], sw2[a:a + m, :]).then_inc(ld_l1, 16)
            sp.dma_start(sb2r[:, :], sb2.rearrange("(a n) -> a n", a=1)).then_inc(ld_l1, 16)
            sp.wait_ge(s_consts, 1)
            for l in range(2):
                sp.dma_start(xs[l][DUMMY:ROWS, :].rearrange("(k p) d -> p k d", p=P),
                             zeros[:, :].unsqueeze(1).to_broadcast([P, SPARE, D])).then_inc(z_sent, 16)

            for l in range(2):
                sp.wait_ge(t_ready, l + 1)
                with sp.Fori(0, E) as e:
                    n = sp.value_load(tbl[0:1, bass.ds(e + 2 * P, 1)], min_val=0, max_val=T)
                    sp.dma_start(xs[l][bass.ds(e * REGION + n, P), :], zeros[:, :]).then_inc(z_sent, 16)
                sp.wait_ge(z_sent, 32 + 16 * E * (l + 1))
                for b in range(2):
                    sp.wait_ge(routers[l]["sent"][b], 16 * NT)

                def load(t, b):
                    row = sp.value_load(tbl[0:1, bass.ds(t, 1)], min_val=0, max_val=ROWS - P)
                    after(sp, e_xT, l * SLOTS + t - (NB - 1))
                    sp.dma_start(xg[b], xs[l][bass.ds(row, P), :]).then_inc(e_x[b], 16)

                def store(t, b):
                    sp.wait_ge(e_yo, l * SLOTS + t + 1)
                    sp.dma_start(ys[l][bass.ds(t * P, P), :], yo[b]).then_inc(e_y[b], 16)

                run_tiles(sp, SLOTS, NB, [(0, load), (3, store)])
                if l == 0:
                    sp.wait_ge(e_o, SLOTS)
                    sp.wait_ge(e_yo, SLOTS)
                    sp.dma_start(w13s.rearrange("p (e k h) -> p e k h", e=E, k=2)[:, :, 0, :],
                                 w1.rearrange("e d h -> d e h")).then_inc(ld_w1, 16)
                    sp.dma_start(w13s.rearrange("p (e k h) -> p e k h", e=E, k=2)[:, :, 1, :],
                                 w3.rearrange("e d h -> d e h")).then_inc(ld_w1, 16)
                    sp.dma_start(w2s.rearrange("p (e c d) -> p e c d", e=E, c=2),
                                 w2.rearrange("e (c p) d -> p e c d", p=K1)).then_inc(ld_w1, 16)
                    bv = bias_big[:, 0:2 * E * H1].rearrange("p (e k h) -> p e k h", e=E, k=2)
                    for k, b in enumerate((b1e, b3e)):
                        sp.dma_start(bv[:, :, k, :], b.rearrange("(a e) h -> a e h", a=1)
                                     .to_broadcast([P, E, H1])).then_inc(ld_w1, 16)
                    sp.dma_start(b2B[:, :], all_row(b2e.rearrange("e d -> (e d)"), E * D)).then_inc(ld_w1, 16)

            def put(t, b):
                sp.wait_ge(g_x, 4 * t + 4)
                sp.dma_start(out[bass.ds(t * P, P), :], xt(t)).then_inc(g_st, 16)

            run_tiles(sp, NT, 2, [(0, put)])
            sp.wait_ge(g_st, 16 * NT)

        @block.gpsimd
        def _(pool):
            pool.memset(zeros[:, :], 0.0)
            pool.memset(onerow[:, :], 1.0)
            pool.memset(eps[:, :], EPS)
            pool.memset(ones[:, :], 1.0)
            pool.memset(macc[:, :, :], 0.0)
            pool.memset(hT[:, 0:BAND], 0.0)
            pool.memset(hT[:, BAND + T:PADT], 0.0)
            pool.memset(kT[:, 0:BAND], 0.0)
            pool.memset(kT[:, BAND + T:PADT], 0.0)
            pool.memset(ident[:, :], 0.0)
            pool.memset(band[:, :], 1.0)
            pool.memset(before[:, :], 1.0)
            pool.memset(upto[:, :], 1.0)
            pool.iota(expert_id[:, :], [[1, E]], base=0, channel_multiplier=0, allow_small_or_imprecise_dtypes=True)
            pool.iota(region_at[:, :], [[REGION, E]], base=0, channel_multiplier=0, allow_small_or_imprecise_dtypes=True)
            pool.iota(slot_id[:, :], [[0, 1]], base=0, channel_multiplier=1,
                      allow_small_or_imprecise_dtypes=True).then_inc(s_consts, 1)
            pool.wait_ge(s_consts, 1)
            pool.affine_select(out=ident[:, :], in_=ident[:, :], compare_op=ALU.not_equal, fill=1.0, base=0,
                               pattern=[[1, P]], channel_multiplier=-1)
            pool.affine_select(out=band[:, :], in_=band[:, :], compare_op=ALU.is_ge, fill=0.0, base=0,
                               pattern=[[1, WIN]], channel_multiplier=-1)
            pool.affine_select(out=before[:, :], in_=before[:, :], compare_op=ALU.is_ge, fill=0.0, base=-1,
                               pattern=[[1, P]], channel_multiplier=-1)
            pool.affine_select(out=upto[:, :], in_=upto[:, :], compare_op=ALU.is_ge, fill=0.0, base=0,
                               pattern=[[1, E]], channel_multiplier=-1).then_inc(s_consts, 1)
            pool.wait_ge(s_consts, 2)
            pool.affine_select(out=band[:, :], in_=band[:, :], compare_op=ALU.is_ge, fill=0.0, base=2 * BAND - 1,
                               pattern=[[-1, WIN]], channel_multiplier=1).then_inc(s_consts, 1)

            def window(t, b):
                pool.wait_ge(a_h, t + 1)
                after(pool, a_kv, t - 1)
                pool.tensor_copy(hwin[:, b, :], hT[:, bass.ds(t * P, P)]).then_inc(a_win, 1)

            run_tiles(pool, NT, 2, [(0, window)])
            pool.wait_ge(a_kv, NT - 1)
            pool.tensor_copy(hwin[:, 0, 0:2 * BAND], hT[:, T:T + 2 * BAND]).then_inc(a_win, 1)

            run_tiles(pool, NT, 2, [(0, lambda t, b: pool_send(pool, router0, t, b))])

            def gather_from(layer, index_copied, gathered, used):
                def gather(t, b):
                    if not (isinstance(t, int) and t < 2):
                        pool.wait_ge(used, 4 * (t - 2) + 2)
                    pool.tensor_copy(gidx[:, 2 * b:2 * b + 2],
                                     result_at[:, layer, bass.ds(t, 1), :].rearrange("p a k -> p (a k)")
                                     ).then_inc(index_copied, 1)
                    pool.wait_ge(index_copied, t + 1)
                    settle(pool, passed)
                    for k in range(TOPK):
                        pool.indirect_dma_start(yg[b][:, k * D:(k + 1) * D], None, ys[layer],
                                                bass.IndirectOffsetOnAxis(gidx[:, 2 * b + k:2 * b + k + 1], 0)
                                                ).then_inc(gathered[b], 16)
                return gather

            for b in range(NB):
                pool.wait_ge(e_y[b], 16 * SLOTS // NB)

            pool.wait_ge(t_rows, 7)

            def product(t, b):
                pool.wait_ge(d_f, 2 * t + 2)
                after(pool, d_sum, DS * (t - 1) + 2)
                pool.tensor_tensor(rf[:, 0:HD], ef[:, 0:HD], ef[:, HD:2 * HD], ALU.mult).then_inc(d_qk, 1)

            run_tiles(pool, NT, 2, [(0, gather_from(0, d_gi, d_g, d_x)), (1, product),
                                    (2, lambda t, b: pool_send(pool, router1, t, b))])
            for b in range(NB):
                pool.wait_ge(e_y[b], 2 * 16 * SLOTS // NB)
            pool.wait_ge(t_rows, 14)
            run_tiles(pool, NT, 2, [(0, gather_from(1, g_i, g_g, g_x))])

        @block.scalar
        def _(act):
            act.preload_act_table_set("natural_log_exp_and_others")
            act.wait_ge(ld_c, 48)
            act.activation(sc[:, 0, :], cT[:, :], ACT.Exp, scale=-1.0).then_inc(s_silu_act, 1)
            act.wait_ge(s_consts, 3)
            act.wait_ge(s_mod_ready, 1)

            def hidden(t, b):
                act.wait_ge(a_xT, t + 1)
                act.activation(hT[:, bass.ds(t * P + BAND, P)], bank[:, b, 0:P], ACT.Identity,
                               bias=mcol[:, 0, 0:1], scale=mcol[:, 0, 1:2],
                               accum_out=hsum[:, bass.ds(t, 1)]).then_inc(a_h, 1)

            def keys(t, b):
                act.wait_ge(a_kv, t + 1)
                act.copy(kT[:, bass.ds(t * P + BAND, P)], bank[:, 2 + b, 0:P]).then_inc(a_k, 1)

            run_tiles(act, NT, 2, [(2, keys), (0, lambda t, b: ln_deviation(act, ln1, t, b)), (1, hidden)])

            def queries(t, b):
                act.wait_ge(b_q, t + 1)
                after(act, b_s, t - 1)
                act.copy(qT[:, b, :], bank[:, ends[b], 0:P]).then_inc(b_qT, 1)

            def exps(t, b):
                act.wait_ge(b_nm, t + 1)
                after(act, b_pp, 4 * (t - 1))
                act.activation(pr[:, b, :], sm[:, b, :], ACT.Exp, bias=st6[:, 1, b:b + 1],
                               accum_out=st6[:, 2, b:b + 1]).then_inc(b_p, 1)
                act.activation(st6[:, 3, b:b + 1], st6[:, 1, b:b + 1], ACT.Exp).then_inc(b_p, 1)

            def probs(t, b):
                act.wait_ge(b_pT, t + 1)
                after(act, b_o, t - 1)
                act.copy(pT[:, b, 0:P], bank[:, 3, 0:P]).then_inc(b_pTc, 1)
                act.copy(pT[0:2 * BAND, b, P:2 * P],
                         bank[0:2 * BAND, 3, P:2 * P]).then_inc(b_pTc, 1)

            run_tiles(act, NT, 2, [(1, probs), (0, queries), (1, lambda t, b: ln_deviation(act, ln2, t, b)),
                                   (0, exps),
                                   (1, lambda t, b: act_modulate(act, router0, t, b)),
                                   (1, lambda t, b: act_exps(act, router0, t, b))])

            def tokens(l, scale_shift):
                def stage(t, b):
                    act.wait_ge(e_xT, l * SLOTS + t + 1)
                    after(act, e_h, l * SLOTS + t - 1)
                    act.activation(xgT[b % 2], bank[:, ends[b % 2], 0:P], ACT.Identity,
                                   bias=scale_shift[0], scale=scale_shift[1]).then_inc(e_xTc, 1)
                return stage

            def relu(t, b):
                act.wait_ge(e_hT, t + 1)
                after(act, e_o, t - 1)
                act.activation(hbT[b % 2], bank[:, 3 + b % 2, :], ACT.Relu).then_inc(e_hTc, 1)

            run_tiles(act, SLOTS, NB, [(0, tokens(0, router0["ss"])), (1, relu)])

            def hidden1(t, b):
                act.wait_ge(d_xT, t + 1)
                after(act, d_o, t - 1)
                act.activation(h3T[b], turned1, ACT.Identity,
                               bias=mcol[:, 1, 0:1], scale=mcol[:, 1, 1:2]).then_inc(d_h, 1)

            def feature_parts(t, b):
                for k, (ready, bk) in enumerate(((d_q, 0), (d_k, 2))):
                    act.wait_ge(ready, t + 1)
                    after(act, d_sum, DS * (t - 1) + 2)
                    act.activation(rf[:, k * HD:(k + 1) * HD], bank[:, bk:bk + 2, :].rearrange("p a n -> p (a n)"),
                                   ACT.Relu, scale=-1.0).then_inc(d_e, 1)
                    act.wait_ge(d_e, 4 * t + 2 * k + 1)
                    act.activation(ef[:, k * HD:(k + 1) * HD], rf[:, k * HD:(k + 1) * HD], ACT.Exp,
                                   scale=-1.0).then_inc(d_e, 1)
                act.wait_ge(d_b, t + 1)
                act.activation(eb[:, 0, :], beta, ACT.Relu, scale=-1.0).then_inc(d_eb, 1)
                act.activation(eb[:, 1, :], beta, ACT.Abs).then_inc(d_eb, 1)
                act.wait_ge(d_eb, 3 * t + 2)
                after(act, d_sum, DS * (t - 1) + 7)
                act.activation(eb[:, 2:4, :], eb[:, 0:2, :], ACT.Exp, scale=-1.0).then_inc(d_eb, 1)

            def values_turned(t, b):
                after(act, d_o, t)
                for k in range(2):
                    act.wait_ge(d_vT, 2 * t + k + 1)
                    act.copy(vT[:, k * 512:(k + 1) * 512], bank[:, 4 + k, :]).then_inc(d_vTc, 1)

            def keep(t, b):
                act.wait_ge(router1["h"], t + 1)
                act.copy(hT[:, bass.ds(t * P, P)], router1["hb"][:, b, :]).then_inc(f_in, 1)

            run_tiles(act, NT, 2, [
                (0, lambda t, b: ln_deviation(act, ln3, t, b)), (0, hidden1), (0, feature_parts), (0, values_turned),
                (0, lambda t, b: ln_deviation(act, ln4, t, b)), (0, lambda t, b: ln_deviation(act, ln5, t, b)),
                (0, lambda t, b: act_modulate(act, router1, t, b)),
                (0, keep),
                (0, lambda t, b: act_exps(act, router1, t, b))])

            act.preload_act_table_set("silu_and_others")

            def shared_silu(t, b):
                for c, (a, m) in enumerate(SC):
                    act.wait_ge(f_h, 2 * (len(SC) * t + c) + 1)
                    after(act, f_g, len(SC) * t)
                    act.activation(shT[c][0:m, :], bank[0:m, c, :], ACT.Silu,
                                   bias=sb13[0:m, 0, c:c + 1]).then_inc(f_a, 1)

            run_tiles(act, T // 512, 1, [(0, shared_silu)])

            def silu(t, b):
                act.wait_ge(e_hb, SLOTS + t + 1)
                act.wait_ge(e_hT, SLOTS + t - 1)
                act.activation(act1[b % 2], hb[b % 2][:, 0:H1], ACT.Silu).then_inc(e_silu, 1)

            def act_turned(t, b):
                act.wait_ge(e_hT, SLOTS + t + 1)
                act.wait_ge(e_o, SLOTS + t - 1)
                act.copy(hbT[b % 2][0:K1, 0:2 * P], bank[0:K1, 3 + b % 2, 0:2 * P]).then_inc(e_hTc, 1)

            run_tiles(act, SLOTS, NB, [(0, tokens(1, router1["ss"])), (2, act_turned), (1, silu)])

        @block.vector
        def _(dve):
            steps = [0]

            def link(ins):
                steps[0] += 1
                ins.then_inc(s_silu, 1)
                dve.wait_ge(s_silu, steps[0])

            dve.wait_ge(s_silu_act, 1)
            link(dve.tensor_scalar(sc[:, 1, :], sc[:, 0, :], 1.0, None, ALU.add))
            link(dve.reciprocal(sc[:, 2, :], sc[:, 1, :]))
            link(dve.tensor_tensor(sc[:, 3, :], sc[:, 2, :], cT[:, :], ALU.mult))
            dve.tensor_copy(siluB[:, :, :], sc[:, 3, :].unsqueeze(2).to_broadcast([P, 2, P])).then_inc(s_mod_used, 1)
            dve.wait_ge(s_mod, 1)
            for l in range(2):
                for k in range(2):
                    link(dve.tensor_copy(mcol[:, l, 2 * k:2 * k + 1], bank[:, 4, 8 * l + 2 * k:8 * l + 2 * k + 1]))
                    link(dve.tensor_scalar(mcol[:, l, 2 * k + 1:2 * k + 2],
                                           bank[:, 4, 8 * l + 2 * k + 1:8 * l + 2 * k + 2], 1.0, None, ALU.add))
                    g = bank[:, 2 * l + k, 0:D]
                    link(dve.tensor_scalar(gtmp[:, 0, :], g, -1.0, None, ALU.mult))
                    link(dve.tensor_tensor(gtmp[:, 1, :], gtmp[:, 0, :], g, ALU.max))
                    link(dve.tensor_scalar(gtmp[:, 0, :], gtmp[:, 1, :], 0.25, None, ALU.max))
                    link(dve.tensor_scalar(gtmp[:, 2, :], g, 0.0, 2.0, ALU.is_ge, ALU.mult))
                    link(dve.scalar_tensor_tensor(gB[:, l, k, :], gtmp[:, 2, :], -1.0, gtmp[:, 0, :], ALU.add, ALU.mult))
            dve.wait_ge(ld_attn, 48)
            dve.tensor_tensor(Wa[:, 2, :], Wa[:, 2, :], gB[:, 0, 0, :], ALU.mult).then_inc(s_mod_ready, 1)

            dve.wait_ge(ld_x, 16)
            dve.wait_ge(s_consts, 3)

            def values(t, b):
                dve.wait_ge(a_kv, t + 1)
                dve.tensor_copy(V[:, bass.ds(t * D, D)], bank[:, 4 + b, 0:D]).then_inc(a_v, 1)

            run_tiles(dve, NT, 2, [(2, values), (0, lambda t, b: ln_measure(dve, ln1, xt(t), t, b)),
                                   (0, lambda t, b: ln_scale(dve, ln1, xt(t), t, b))])
            dve.wait_ge(a_kv, NT + 1)
            dve.tensor_copy(V[0:2 * BAND, NT * D:(NT + 1) * D], bank[0:2 * BAND, 4, 0:D]).then_inc(a_v, 1)
            dve.wait_ge(a_h, NT)
            dve.reduce_sum(st6[:, 0, 0:1], hsum[:, :], AX_X).then_inc(a_hs, 1)
            dve.wait_ge(a_hs, 1)
            dve.tensor_copy(hsumB[:, :], st6[:, 0, 0:1].to_broadcast([P, P])).then_inc(a_hs, 1)
            dve.wait_ge(a_vt, 1)
            dve.tensor_copy(vtot[:, :], bank[:, 6, 0:D]).then_inc(a_vtc, 1)
            dve.wait_ge(a_vtc, 1)

            def masked(t, b):
                dve.wait_ge(b_s, t + 1)
                after(dve, b_p, 2 * (t - 1) - 1)
                settle(dve, passed)
                dve.tensor_tensor_reduce(sm[:, b, :], bank[:, 1 + b, 0:WIN], band[:, :],
                                         float(D) ** -0.5, 0.0, ALU.mult, ALU.max, st6[:, 0, b:b + 1]).then_inc(b_sm, 1)
                dve.wait_ge(b_sm, t + 1)
                after(dve, b_p, 2 * (t - 1))
                dve.tensor_scalar(st6[:, 1, b:b + 1], st6[:, 0, b:b + 1], -1.0, None, ALU.mult).then_inc(b_nm, 1)

            def excess(t, b):
                dve.wait_ge(b_p, 2 * t + 2)
                dve.tensor_scalar(pr[:, b, :], pr[:, b, :], st6[:, 3, b:b + 1], None, ALU.subtract).then_inc(b_pp, 1)
                dve.scalar_tensor_tensor(st6[:, 4, b:b + 1], st6[:, 3, b:b + 1], float(T - WIN), st6[:, 2, b:b + 1],
                                         ALU.mult, ALU.add).then_inc(b_pp, 1)
                dve.wait_ge(b_pp, 4 * t + 2)
                dve.reciprocal(st6[:, 5, b:b + 1], st6[:, 4, b:b + 1]).then_inc(b_pp, 1)

            def attended(t, b):
                dve.wait_ge(b_o, t + 1)
                dve.scalar_tensor_tensor(ao[:, :], vtot[:, :], st6[:, 3, b:b + 1], bank[:, 4, 0:D],
                                         ALU.mult, ALU.add).then_inc(b_pp, 1)
                dve.wait_ge(b_pp, 4 * t + 4)
                dve.scalar_tensor_tensor(xt(t), ao[:, :], st6[:, 5, b:b + 1], xt(t), ALU.mult, ALU.add).then_inc(b_x, 1)
                dve.wait_ge(b_x, t + 1)

            def norm2(t, b):
                if not (isinstance(t, int) and t < 2):
                    dve.wait_ge(router0["sent"][b], 16 * (t - b))
                ln_scale(dve, ln2, xt(t), t, b)

            run_tiles(dve, NT, 2, [(1, attended), (1, lambda t, b: ln_measure(dve, ln2, xt(t), t, b)),
                                   (0, masked), (1, norm2), (0, excess),
                                   (1, lambda t, b: dve_pick(dve, router0, t, b)),
                                   (1, lambda t, b: dve_place(dve, router0, t, b))])

            def slot_table(l):
                r = routers[l]
                k0 = 11 * l

                def step(k, ins):
                    ins.then_inc(t_dve, 1)
                    dve.wait_ge(t_dve, k0 + k)

                dve.wait_ge(t_cnt, l + 1)
                step(1, dve.tensor_scalar(tiles_int[:, 0, :], bank[0:E, 0, 0:P], float(P - 1), None, ALU.add))
                step(2, dve.tensor_scalar(tiles_int[:, 1, :], tiles_int[:, 0, :], 7, None, ALU.logical_shift_right))
                step(3, dve.tensor_copy(tiles_per[:, :], tiles_int[:, 1, :]))
                dve.wait_ge(t_cum, l + 1)
                step(4, dve.tensor_copy(cumt[:, 0, :], bank[:, 1, 0:E]))
                step(5, dve.tensor_scalar(cumt[:, 1, :], cumt[:, 0, :], slot_id[:, :], None, ALU.is_le))
                step(6, dve.tensor_tensor(cumt[:, 2, :], cumt[:, 0, :], cumt[:, 1, :], ALU.mult))
                step(7, dve.reduce_sum(sl[:, 0:1], cumt[:, 1, :], AX_X))
                step(8, dve.reduce_max(sl[:, 1:2], cumt[:, 2, :], AX_X))
                step(9, dve.tensor_scalar(sl[:, 2:3], sl[:, 1:2], slot_id[:, :], -float(P), ALU.subtract, ALU.mult))
                step(10, dve.scalar_tensor_tensor(slot_vals[:, 0:1], sl[:, 0:1], float(REGION), sl[:, 2:3],
                                                  ALU.mult, ALU.add))
                step(11, dve.tensor_scalar(slot_vals[:, 1:2], sl[:, 0:1], float(E - 1), None, ALU.min))
                dve.wait_ge(t_val, l + 1)
                dve.tensor_copy(tbl[:, :], bank[0:1, 2, 0:2 * P + E]).then_inc(t_ready, 1)
                dve.wait_ge(t_ready, l + 1)

                k1 = 7 * l

                def place(k, ins):
                    ins.then_inc(t_rows, 1)
                    dve.wait_ge(t_rows, k1 + k)

                place(1, dve.memset(slot_shift[:, 0, 0:1], 0.0))
                place(2, dve.tensor_copy(slot_shift[:, 0, 1:E], cumt[:, 0, 0:E - 1]))
                place(3, dve.scalar_tensor_tensor(slot_shift[:, 1, :], slot_shift[:, 0, :], float(P), region_at[:, :],
                                                  ALU.mult, ALU.subtract))
                mine = chosen[:, l, :, :].rearrange("p t k -> p (t k)")
                place(4, dve.tensor_tensor(match[:, :, :], expert_id[:, :].unsqueeze(1).to_broadcast([P, 2 * NT, E]),
                                           mine.unsqueeze(2).to_broadcast([P, 2 * NT, E]), ALU.is_equal))
                place(5, dve.tensor_tensor(match[:, :, :], match[:, :, :],
                                           slot_shift[:, 1, :].unsqueeze(1).to_broadcast([P, 2 * NT, E]), ALU.mult))
                place(6, dve.reduce_sum(shifts[:, :], match[:, :, :], AX_X))
                place(7, dve.tensor_tensor(result_at[:, l, :, :].rearrange("p t k -> p (t k)"), shifts[:, :],
                                           where[:, l, :, :].rearrange("p t k -> p (t k)"), ALU.add))

            slot_table(0)

            def expert_of(eng, t):
                return eng.value_load(tbl[0:1, bass.ds(t + P, 1)], min_val=0, max_val=E - 1)

            def biased(l, width):
                def stage(t, b):
                    e = expert_of(dve, t)
                    dve.wait_ge(e_h, l * SLOTS + t + 1)
                    after(dve, e_hT, t - 1) if l == 0 else after(dve, e_silu, t - 1)
                    dve.tensor_tensor(hb[b % 2][:, 0:width], bank[:, 1 + b % 2, 0:width],
                                      bias_big[:, bass.ds(e * width, width)], ALU.add).then_inc(e_hb, 1)
                return stage

            def result(l):
                def stage(t, b):
                    e = expert_of(dve, t)
                    dve.wait_ge(e_o, l * SLOTS + t + 1)
                    if not (isinstance(t, int) and t < NB):
                        dve.wait_ge(e_y[b], 16 * l * (SLOTS // NB) + 4 * (t - b))
                    dve.tensor_tensor(yo[b], bank[:, 5 + b % 2, 0:D], b2B[:, bass.ds(e * D, D)],
                                      ALU.add).then_inc(e_yo, 1)
                return stage

            dve.wait_ge(ld_w0, 64)
            run_tiles(dve, SLOTS, NB, [(2, result(0)), (0, biased(0, H0))])

            dve.wait_ge(ld_l1, 16 * (4 + 2 * (1 + len(SC)) + len(SC) + 1))
            for k in range(2):
                link(dve.tensor_tensor(lnG[:, k, :], lnB[:, k, :], gB[:, 1, 0, :], ALU.mult))
            for c, (a, m) in enumerate(SC):
                link(dve.tensor_tensor(sw2s[0:m, c, :], sw2s[0:m, c, :], gB[0:m, 1, 1, :], ALU.mult))
            link(dve.tensor_tensor(sb2r[:, :], sb2r[:, :], gB[0:1, 1, 1, :], ALU.mult))

            def combine(layer, gathered, signal):
                def stage(t, b):
                    dve.wait_ge(gathered[b], 16 * (t - b) + 32)
                    g = gates[:, layer, bass.ds(t, 1), :].rearrange("p a k -> p (a k)")
                    k0 = 4 * t
                    dve.tensor_scalar(mix[:, 0, :], yg[b][:, 0:D], g[:, 0:1], None, ALU.mult).then_inc(signal, 1)
                    dve.wait_ge(signal, k0 + 1)
                    dve.scalar_tensor_tensor(mix[:, 1, :], yg[b][:, D:2 * D], g[:, 1:2], mix[:, 0, :],
                                             ALU.mult, ALU.add).then_inc(signal, 1)
                    dve.wait_ge(signal, k0 + 2)
                    dve.tensor_tensor(mix[:, 2, :], mix[:, 1, :], gB[:, layer, 1, :], ALU.mult).then_inc(signal, 1)
                    dve.wait_ge(signal, k0 + 3)
                    dve.tensor_tensor(xt(t), xt(t), mix[:, 2, :], ALU.add).then_inc(signal, 1)
                    dve.wait_ge(signal, k0 + 4)
                return stage

            def features(t, b):
                for k in range(2):
                    dve.wait_ge(d_e, 4 * t + 2 * k + 2)
                    dve.scalar_tensor_tensor(ef[:, k * HD:(k + 1) * HD],
                                             bank[:, 2 * k:2 * k + 2, :].rearrange("p a n -> p (a n)"), 0.0,
                                             ef[:, k * HD:(k + 1) * HD], ALU.max, ALU.add).then_inc(d_f, 1)
                dve.wait_ge(d_f, 2 * t + 2)
                k0 = DS * t
                dve.reduce_sum(qk_sums[:, :, :], ef.rearrange("p (k h d) -> p k h d", k=2, h=NH), AX_X).then_inc(d_sum, 1)
                dve.wait_ge(d_qk, t + 1)
                dve.reduce_sum(sums[:, 0, :], rf[:, 0:HD].rearrange("p (h d) -> p h d", h=NH), AX_X).then_inc(d_sum, 1)
                dve.wait_ge(d_sum, k0 + 1)
                dve.tensor_tensor(sums[:, 1, :], qk_sums[:, 0, :], qk_sums[:, 1, :], ALU.mult).then_inc(d_sum, 1)
                dve.wait_ge(d_eb, 3 * t + 3)
                dve.wait_ge(d_sum, k0 + 3)
                dve.scalar_tensor_tensor(sums[:, 2, :], eb[:, 3, :], 1.0, sums[:, 1, :], ALU.add, ALU.mult
                                         ).then_inc(d_sum, 1)
                dve.wait_ge(d_sum, k0 + 4)
                dve.reciprocal(sums[:, 3, :], sums[:, 2, :]).then_inc(d_sum, 1)
                dve.wait_ge(d_sum, k0 + 5)
                dve.scalar_tensor_tensor(sums[:, 4, :], sums[:, 0, :], float(DH) ** -0.5, sums[:, 3, :],
                                         ALU.mult, ALU.mult).then_inc(d_sum, 1)
                dve.wait_ge(d_sum, k0 + 6)
                dve.tensor_tensor(sums[:, 5, :], sums[:, 4, :], eb[:, 2, :], ALU.mult).then_inc(d_sum, 1)
                dve.wait_ge(d_sum, k0 + 7)
                dve.wait_ge(d_v, t + 1)
                after(dve, d_vT, 2 * t)
                for k in range(2):
                    n = NH // 2
                    dve.tensor_tensor(vc[:, k * 512:(k + 1) * 512].rearrange("p (h d) -> p h d", h=n),
                                      bank[:, 4 + k, :].rearrange("p (h d) -> p h d", h=n),
                                      sums[:, 5, k * n:(k + 1) * n].unsqueeze(2).to_broadcast([P, n, DH]),
                                      ALU.mult).then_inc(d_sum, 1)

            def inner_norm(t, b):
                dve.wait_ge(d_o, t + 1)
                ln_measure(dve, ln4, attn1, t, b)
                ln_scale(dve, ln4, attn1, t, b)
                dve.wait_ge(ln4["normed"], t + 1)
                dve.tensor_tensor(ya[b], ln4["xn"][:, b, :], lnG[:, 0, :], ALU.mult).then_inc(d_y, 1)
                dve.wait_ge(d_y, 3 * t + 1)
                dve.tensor_tensor(ya[b], ya[b], lnG[:, 1, :], ALU.add).then_inc(d_y, 1)
                dve.wait_ge(d_y, 3 * t + 2)
                dve.tensor_tensor(xt(t), xt(t), ya[b], ALU.add).then_inc(d_y, 1)
                dve.wait_ge(d_y, 3 * t + 3)

            def norm5(t, b):
                if not (isinstance(t, int) and t < 2):
                    dve.wait_ge(router1["sent"][b], 16 * (t - b))
                ln_scale(dve, ln5, xt(t), t, b)

            run_tiles(dve, NT, 2, [
                (0, combine(0, d_g, d_x)), (0, lambda t, b: ln_measure(dve, ln3, xt(t), t, b)),
                (0, lambda t, b: ln_scale(dve, ln3, xt(t), t, b)), (0, features), (0, inner_norm),
                (0, lambda t, b: ln_measure(dve, ln5, xt(t), t, b)), (0, norm5),
                (0, lambda t, b: dve_pick(dve, router1, t, b)),
                (0, lambda t, b: dve_place(dve, router1, t, b))])
            slot_table(1)

            def shared(t, b):
                for c, (a, m) in enumerate(SC):
                    dve.wait_ge(f_h, 2 * (len(SC) * t + c) + 2)
                    dve.wait_ge(f_a, len(SC) * t + c + 1)
                    after(dve, f_o, t)
                    dve.scalar_tensor_tensor(shT[len(SC) + c][0:m, :], bank[0:m, 3 + c, :], sb13[0:m, 1, c:c + 1],
                                             shT[c][0:m, :], ALU.add, ALU.mult).then_inc(f_g, 1)
                dve.wait_ge(f_o, t + 1)
                xi = xres[:, bass.ds(t * 512, 512)]
                dve.tensor_tensor(xi, xi, bank[:, 6, :], ALU.add).then_inc(f_x, 1)

            run_tiles(dve, T // 512, 1, [(0, shared)])

            def gated(t, b):
                dve.wait_ge(e_silu, t + 1)
                dve.tensor_tensor(act1[b % 2], act1[b % 2], hb[b % 2][:, H1:2 * H1], ALU.mult).then_inc(e_act, 1)

            dve.wait_ge(ld_w1, 96)
            run_tiles(dve, SLOTS, NB, [(2, result(1)), (0, biased(1, 2 * H1)), (1, gated)])

            run_tiles(dve, NT, 2, [(0, combine(1, g_g, g_x))])

        @block.tensor
        def _(pe):
            pe.wait_ge(s_mod_used, 1)
            pe.wait_ge(ld_c, 48)
            for l in range(2):
                for k in range(2):
                    pe.matmul(bank[:, 2 * l + k, 0:D], siluB[:, l, :], wmod[:, l, (3 * k + 2) * D:(3 * k + 3) * D],
                              start=True, stop=True)
                    for i in range(2):
                        c = 8 * l + 2 * k + i
                        last = pe.matmul(bank[:, 4, c:c + 1], wmod[:, l, (3 * k + i) * D:(3 * k + i + 1) * D],
                                         sc[:, 3, l:l + 1], start=True, stop=True)
            last.then_inc(s_mod, 1)
            pe.wait_ge(s_mod_ready, 1)
            pe.wait_ge(s_consts, 3)
            pe.wait_ge(ld_attn, 48)

            def turn(t, b):
                pe.wait_ge(ln1["normed"], t + 1)
                after(pe, a_h, t - 1)
                pe.transpose(bank[:, b, 0:P], ln1["xn"][:, b, :], ident[:, :]).then_inc(a_xT, 1)

            def keys_values(t, b):
                pe.wait_ge(a_h, t + 1)
                pe.wait_ge(a_win, t + 1)
                after(pe, a_k, t - 1)
                after(pe, a_v, t - 1)
                pe.matmul(bank[:, 2 + b, 0:P], Wa[:, 1, :], hT[:, bass.ds(t * P + BAND, P)], start=True, stop=True)
                pe.matmul(bank[:, 4 + b, 0:D], hwin[:, b, :], Wa[:, 2, :], start=True, stop=True).then_inc(a_kv, 1)

            run_tiles(pe, NT, 2, [(1, keys_values), (0, turn)])
            pe.wait_ge(a_win, NT + 1)
            pe.wait_ge(a_v, NT - 1)
            pe.matmul(bank[0:2 * BAND, 4, 0:D], hwin[:, 0, 0:2 * BAND], Wa[:, 2, :], start=True, stop=True).then_inc(a_kv, 1)
            pe.wait_ge(a_hs, 2)
            pe.matmul(bank[:, 6, 0:D], hsumB[:, :], Wa[:, 2, :], start=True, stop=True).then_inc(a_vt, 1)
            pe.wait_ge(a_vtc, 1)
            pe.wait_ge(a_k, NT)
            pe.wait_ge(a_v, NT + 1)
            pe.wait_ge(ld_router, 64)

            def query(t, b):
                after(pe, b_qT, t - 1)
                pe.matmul(bank[:, ends[b], 0:P], Wa[:, 0, :], hT[:, bass.ds(t * P + BAND, P)],
                          start=True, stop=True).then_inc(b_q, 1)

            def score(t, b):
                pe.wait_ge(b_qT, t + 1)
                after(pe, b_sm, t - 1)
                pe.matmul(bank[:, 1 + b, 0:WIN], qT[:, b, :], kT[:, bass.ds(t * P, WIN)],
                          start=True, stop=True).then_inc(b_s, 1)

            def turn_probs(t, b):
                pe.wait_ge(b_pp, 4 * t + 1)
                after(pe, b_pTc, 2 * t)
                pe.transpose(bank[:, 3, 0:P], pr[:, b, 0:P], ident[:, :])
                pe.transpose(bank[0:2 * BAND, 3, P:2 * P], pr[:, b, P:WIN],
                             ident[:, :]).then_inc(b_pT, 1)

            def attend(t, b):
                pe.wait_ge(b_pTc, 2 * t + 2)
                after(pe, b_pp, 4 * t)
                o = bank[:, 4, 0:D]
                pe.matmul(o, pT[:, b, 0:P], V[:, bass.ds(t * D, D)], start=True, stop=False)
                pe.matmul(o, pT[0:2 * BAND, b, P:2 * P], V[0:2 * BAND, bass.ds(t * D + D, D)],
                          start=False, stop=True).then_inc(b_o, 1)

            run_tiles(pe, NT, 2, [(0, query), (1, attend), (0, score),
                                  (1, lambda t, b: pe_transpose(pe, router0, t, b)),
                                  (0, turn_probs),
                                  (1, lambda t, b: pe_logits(pe, router0, t, b)),
                                  (1, lambda t, b: pe_rank(pe, router0, t, b))])

            def slot_counts(l):
                r = routers[l]
                pe.wait_ge(r["placed"], RANK * NT)
                pe.matmul(bank[0:E, 0, 0:P], macc[:, l, :], ones[:, :], start=True, stop=True).then_inc(t_cnt, 1)
                pe.wait_ge(t_dve, 11 * l + 3)
                pe.matmul(bank[:, 1, 0:E], tiles_per[:, :], upto[:, :], start=True, stop=True).then_inc(t_cum, 1)
                pe.wait_ge(t_dve, 11 * l + 11)
                for k in range(2):
                    pe.matmul(bank[0:1, 2, k * P:(k + 1) * P], slot_vals[:, k:k + 1], ident[:, :], start=True, stop=True)
                pe.matmul(bank[0:1, 2, 2 * P:2 * P + E], ones[:, 0:1], macc[:, l, :], start=True, stop=True
                          ).then_inc(t_val, 1)
                pe.wait_ge(t_ready, l + 1)

            slot_counts(0)

            def expert_of(t):
                return pe.value_load(tbl[0:1, bass.ds(t + P, 1)], min_val=0, max_val=E - 1)

            def slot_turn(l):
                def stage(t, b):
                    pe.wait_ge(e_x[b], 16 * l * (SLOTS // NB) + 4 * (t - b) + 16)
                    after(pe, e_xTc, l * SLOTS + t - 1)
                    pe.transpose(bank[:, ends[b % 2], 0:P], xg[b], ident[:, :]).then_inc(e_xT, 1)
                return stage

            def slot_hidden(l, w, width):
                def stage(t, b):
                    e = expert_of(t)
                    pe.wait_ge(e_xTc, l * SLOTS + t + 1)
                    after(pe, e_hb, l * SLOTS + t - 1)
                    pe.matmul(bank[:, 1 + b % 2, 0:width], xgT[b % 2], w[:, bass.ds(e * width, width)],
                              start=True, stop=True).then_inc(e_h, 1)
                return stage

            def slot_turn_hidden(t, b):
                pe.wait_ge(e_hb, t + 1)
                after(pe, e_hTc, t - 1)
                for c in range(C0):
                    last = pe.transpose(bank[:, 3 + b % 2, c * P:(c + 1) * P], hb[b % 2][:, c * P:(c + 1) * P], ident[:, :])
                last.then_inc(e_hT, 1)

            def slot_out(t, b):
                e = expert_of(t)
                pe.wait_ge(e_hTc, t + 1)
                after(pe, e_yo, t - 1)
                for c in range(C0):
                    last = pe.matmul(bank[:, 5 + b % 2, 0:D], hbT[b % 2][:, c * P:(c + 1) * P],
                                     W2s[:, bass.ds(e * H0 + c * D, D)], start=(c == 0), stop=(c == C0 - 1))
                last.then_inc(e_o, 1)

            pe.wait_ge(ld_w0, 64)
            run_tiles(pe, SLOTS, NB, [(0, slot_turn(0)), (2, slot_out), (0, slot_hidden(0, W1s, H0)),
                                      (1, slot_turn_hidden)])
            pe.wait_ge(e_yo, SLOTS)

            pe.wait_ge(ld_l1, 16 * (4 + 2 * (1 + len(SC)) + len(SC) + 1))

            def turn1(t, b):
                pe.wait_ge(ln3["normed"], t + 1)
                after(pe, d_h, t)
                after(pe, d_eb, 3 * t)
                pe.transpose(turned1, ln3["xn"][:, b, :], ident[:, :]).then_inc(d_xT, 1)

            def project(t, b):
                pe.wait_ge(d_h, t + 1)
                for k, s in enumerate((d_q, d_k, d_v)):
                    after(pe, d_f, 2 * (t - 1) + k + 1) if k < 2 else after(pe, d_vTc, 2 * t)
                    for i in range(2):
                        last = pe.matmul(bank[:, 2 * k + i, :], h3T[b], Wqkvb[:, k * HD + i * 512:k * HD + (i + 1) * 512],
                                         start=True, stop=True)
                    last.then_inc(s, 1)
                pe.matmul(beta, h3T[b], Wqkvb[:, 3 * HD:3 * HD + NH], start=True, stop=True).then_inc(d_b, 1)

            def turn_values(t, b):
                pe.wait_ge(d_sum, DS * (t + 1))
                for k in range(2):
                    for c in range(4):
                        last = pe.transpose(bank[:, 4 + k, c * P:(c + 1) * P], vc[:, (4 * k + c) * P:(4 * k + c + 1) * P],
                                            ident[:, :])
                    last.then_inc(d_vT, 1)

            def attn_out(t, b):
                pe.wait_ge(d_vTc, 2 * t + 2)
                after(pe, router1["placed"], RANK * t - 2)
                pe.matmul(attn1, h3T[b], ident[:, :], start=True, stop=False)
                for c in range(HD // P):
                    last = pe.matmul(attn1, vT[:, c * P:(c + 1) * P], Wo[:, c, :],
                                     start=False, stop=(c == HD // P - 1))
                last.then_inc(d_o, 1)

            run_tiles(pe, NT, 2, [(0, turn1), (0, project), (0, turn_values), (0, attn_out),
                                  (0, lambda t, b: pe_transpose(pe, router1, t, b)),
                                  (0, lambda t, b: pe_logits(pe, router1, t, b)),
                                  (0, lambda t, b: pe_rank(pe, router1, t, b))])
            slot_counts(1)

            pe.wait_ge(f_in, NT)

            def shared_hidden(t, b):
                for c, (a, m) in enumerate(SC):
                    after(pe, f_g, len(SC) * t)
                    for k in range(2):
                        pe.matmul(bank[0:m, 3 * k + c, :], sw13[:, k, a:a + m], hT[:, bass.ds(t * 512, 512)],
                                  start=True, stop=True).then_inc(f_h, 1)

            def shared_out(t, b):
                pe.wait_ge(f_g, len(SC) * (t + 1))
                after(pe, f_x, t)
                for i in range(4):
                    o = bank[:, 6, i * D:(i + 1) * D]
                    pe.matmul(o, onerow[:, :], sb2r[:, :], start=True, stop=False)
                    for c, (a, m) in enumerate(SC):
                        last = pe.matmul(o, shT[len(SC) + c][0:m, i * P:(i + 1) * P], sw2s[0:m, c, :],
                                         start=False, stop=(c == len(SC) - 1))
                last.then_inc(f_o, 1)

            run_tiles(pe, T // 512, 1, [(0, shared_hidden), (0, shared_out)])
            pe.wait_ge(f_x, T // 512)

            def slot_turn_act(t, b):
                pe.wait_ge(e_act, t + 1)
                after(pe, e_hTc, SLOTS + t - 1)
                for c in range(2):
                    last = pe.transpose(bank[0:K1, 3 + b % 2, c * P:(c + 1) * P], act1[b % 2][:, c * K1:(c + 1) * K1],
                                        ident[:, :])
                last.then_inc(e_hT, 1)

            def slot_out1(t, b):
                e = expert_of(t)
                pe.wait_ge(e_hTc, SLOTS + t + 1)
                after(pe, e_yo, SLOTS + t - 1)
                for c in range(2):
                    last = pe.matmul(bank[:, 5 + b % 2, 0:D], hbT[b % 2][0:K1, c * P:(c + 1) * P],
                                     w2s[:, bass.ds(e * 2 * D + c * D, D)], start=(c == 0), stop=(c == 1))
                last.then_inc(e_o, 1)

            pe.wait_ge(ld_w1, 96)
            run_tiles(pe, SLOTS, NB, [(0, slot_turn(1)), (2, slot_out1), (0, slot_hidden(1, w13s, 2 * H1)),
                                      (1, slot_turn_act)])


def kernel(**inputs):
    import numpy as np
    import concourse.bacc as bacc
    from concourse.bass_utils import run_bass_kernel_spmd

    a = {k: np.ascontiguousarray(v) for k, v in inputs.items()}
    T, D = a["L0_attn_inputs"].shape[1:]
    NH, DH = 16, 64
    qkvb = a["L1_attn_W_qkvb"].reshape(NH, 3 * DH + 1, D)
    blocks = [qkvb[:, k * DH:(k + 1) * DH].reshape(NH * DH, D) for k in range(3)] + [qkvb[:, 3 * DH]]
    f = "L1_ffn_"
    arrays = {
        "x": a["L0_attn_inputs"].reshape(T, D), "WQ": a["L0_attn_WQ"], "WK": a["L0_attn_WK"], "WV": a["L0_attn_WV"],
        "Wr0": a["L0_ffn_Wr"], "br0": a["L0_ffn_br"], "W1": a["L0_ffn_W1"], "b1": a["L0_ffn_b1"],
        "W2": a["L0_ffn_W2"], "b2": a["L0_ffn_b2"],
        "c01": np.stack([a["L0_c"].reshape(D), a["L1_c"].reshape(D)], axis=1),
        "wmod0": a["L0_wmod"], "wmod1": a["L1_wmod"],
        "WqkvbT": np.concatenate(blocks, axis=0).T, "WoT": a["L1_attn_W_o"].T,
        "ln_g": a["L1_attn_ln_g"], "ln_b": a["L1_attn_ln_b"],
        "Wr1": a[f + "gate_w"], "br1": a[f + "gate_b"], "w1": a[f + "w1"], "b1e": a[f + "b1"],
        "w3": a[f + "w3"], "b3e": a[f + "b3"], "w2": a[f + "w2"], "b2e": a[f + "b2"],
        "sw1": a[f + "sw1"], "sb1": a[f + "sb1"], "sw3": a[f + "sw3"], "sb3": a[f + "sb3"],
        "sw2": a[f + "sw2"], "sb2": a[f + "sb2"],
    }
    nc = bacc.Bacc("TRN2", target_bir_lowering=False, num_devices=1)
    feed, args = {}, {}
    for name, v in arrays.items():
        v = np.ascontiguousarray(v)
        feed[f"in_{name}"] = v
        args[name] = nc.dram_tensor(f"in_{name}", v.shape, mybir.dt.from_np(v.dtype), kind="ExternalInput").ap()
    args["out"] = nc.dram_tensor("out_x", (T, D), F32, kind="ExternalOutput").ap()
    build(nc, **args)
    r = run_bass_kernel_spmd(nc, [feed], core_ids=[0])
    return r.results[0]["out_x"].reshape(1, T, D)
```

```python
from contextlib import ExitStack

import concourse.bass as bass
from concourse import mybir

ALU = mybir.AluOpType
ACT = mybir.ActivationFunctionType
AX_X = mybir.AxisListType.X
F32 = mybir.dt.float32
BF16 = mybir.dt.bfloat16
I32 = mybir.dt.int32
U32 = mybir.dt.uint32

P = 128
EPS = 1e-5


def after(eng, sem, n):
    if isinstance(n, int) and n <= 0:
        return
    eng.wait_ge(sem, n)


def settle(eng, passed):
    eng.sem_inc(passed, 1)


def run_tiles(eng, n, unroll, work):
    deepest = max(lag for lag, _ in work)
    head = (-(-deepest // unroll) + 1) * unroll
    for s in range(head):
        for lag, stage in work:
            if 0 <= s - lag:
                stage(s - lag, (s - lag) % unroll, (s - lag) // unroll)
    with eng.Fori(head // unroll, n // unroll) as j:
        for u in range(unroll):
            for lag, stage in work:
                stage(unroll * j + (u - lag), (u - lag) % unroll, j + (u - lag) // unroll)
    for s in range(n, n + deepest):
        for lag, stage in work:
            if s - lag < n:
                stage(s - lag, (s - lag) % unroll, (s - lag) // unroll)


def build(nc, x, WQ, WK, WV, Wr0, br0, W1, b1, W2, b2, c01, wmod0, wmod1,
          WqkvbT, WoT, ln_g, ln_b, Wr1, br1, w1, b1e, w3, b3e, w2, b2e,
          sw1, sb1, sw3, sb3, sw2, sb2, out):
    T, D = x.shape
    NT = T // P
    E = Wr0.shape[1]
    H0 = W1.shape[2]
    C0 = H0 // P
    H1 = w1.shape[2]
    K1 = H1 // 2
    HS = sw1.shape[1]
    SC = [(a, min(P, HS - a)) for a in range(0, HS, P)]
    NH = 16
    DH = (WqkvbT.shape[1] - NH) // (3 * NH)
    HD = NH * DH
    BAND = 32
    WIN = P + 2 * BAND
    PADT = T + 2 * BAND
    TOPK = 2
    NB = 8
    SLOTS = -(-(TOPK * T // P + E - 1) // NB) * NB
    REGION = T + P
    SPARE = SLOTS - TOPK * T // P
    DUMMY = E * REGION
    ROWS = DUMMY + SPARE * P
    RW = D + 1
    NOWHERE = 1 << 20
    assert D == P and T % (2 * P) == 0 and SLOTS <= P

    xs = [nc.dram_tensor(f"sorted_tokens_{l}", [ROWS, RW], F32, kind="Internal").ap() for l in range(2)]
    ys = [nc.dram_tensor(f"results_{l}", [TOPK * T, D], F32, kind="Internal").ap() for l in range(2)]

    with ExitStack() as ctx:
        def sb(name, shape, dt=F32):
            return ctx.enter_context(nc.sbuf_tensor(name, shape, dt))

        def sem(name):
            return ctx.enter_context(nc.semaphore(name))

        bank = ctx.enter_context(nc.psum_tensor("bank", [P, 8, 512], F32))

        xres = sb("xres", [P, NT * D])
        hT = sb("hT", [P, PADT])
        big = sb("big", [P, 2 * E * H0])
        W1s = big[:, 0:E * H0]
        W2s = big[:, E * H0:2 * E * H0]
        o13, o2, ob = 0, 2 * E * H1, 2 * E * H1 + 2 * E * D
        w13s = big[:, o13:o13 + 2 * E * H1]
        w2s = big[0:K1, o2:o2 + 2 * E * D]
        bias_big = sb("bias_big", [P, E * H0])
        b2B = sb("b2B", [P, E * D])
        Wa = sb("Wa", [P, 3, D])
        Wqkvb = sb("Wqkvb", [P, 3 * HD + NH])
        Wo = sb("Wo", [P, HD // P, D])
        Wr = sb("Wr", [P, 2, E])
        brB = sb("brB", [P, 2, E])
        sw13 = sb("sw13", [P, 2, HS])
        sw2s = sb("sw2s", [P, len(SC), D])
        sb13 = sb("sb13", [P, 2, len(SC)])
        sb2r = sb("sb2r", [1, D])
        lnB = sb("lnB", [P, 2, D])
        cT = sb("cT", [P, 2])

        ident = sb("ident", [P, P])
        band = sb("band", [P, WIN])
        before = sb("before", [P, P], BF16)
        ones = sb("ones", [P, P], BF16)
        onerow = sb("onerow", [1, P])
        zeros = sb("zeros", [P, RW])
        result_row = sb("result_row", [P, NT, TOPK], I32)
        expert_id = sb("expert_id", [P, E])
        region_at = sb("region_at", [P, E])
        upto = sb("upto", [E, E])
        slot_id = sb("slot_id", [P, 1])
        eps = sb("eps", [P, 1])

        sc = sb("sc", [P, 6, 2])
        mcol = sb("mcol", [P, 2, 4])
        gB = sb("gB", [P, 2, 2, D])
        lnG = sb("lnG", [P, 2, D])

        hsum = sb("hsum", [P, NT])
        vtot = sb("vtot", [P, D])
        ao = sb("ao", [P, D])
        st6 = sb("st6", [P, 6, 4])
        gates = sb("gates", [P, 2, NT, 2])
        rows = sb("rows", [P, 4, TOPK, RW])
        macc = sb("macc", [P, 2, 2, E], BF16)
        slot_vals = sb("slot_vals", [P, 2])
        tbl = sb("tbl", [1, 2 * P + E], I32)
        tiles_per = sb("tiles_per", [E, P])
        tiles_int = sb("tiles_int", [E, 2, P], I32)
        cumt = sb("cumt", [P, 3, E])
        sl = sb("sl", [P, 3])
        sums = sb("sums", [P, 6, NH])
        qk_sums = sb("qk_sums", [P, 2, NH])
        eb = sb("eb", [P, 4, NH])

        work = sb("work", [P, 7168])
        wmod = work[:, 4352:4352 + 12 * D].rearrange("p (l n) -> p l n", l=2)
        kT = work[:, 0:PADT]
        V = work[:, PADT:PADT + (NT + 1) * D]
        siluB = work[:, 5888:5888 + 2 * P].rearrange("p (l n) -> p l n", l=2)
        gtmp = work[:, 6144:6144 + 3 * D].rearrange("p (k n) -> p k n", k=3)
        hwin = work[:, 4352:4352 + 2 * P].rearrange("p (b n) -> p b n", b=2)
        qT = work[:, 4608:4608 + 2 * P].rearrange("p (b n) -> p b n", b=2)
        sm = work[:, 4864:4864 + 2 * WIN].rearrange("p (b n) -> p b n", b=2)
        pr = work[:, 5248:5248 + 2 * WIN].rearrange("p (b n) -> p b n", b=2)
        pT = work[:, 5632:5632 + 4 * P].rearrange("p (b n) -> p b n", b=2)
        hsumB = work[:, 6528:6528 + P]
        ef = work[:, 0:2 * HD]
        rf = work[:, 2 * HD:4 * HD]
        vc = work[:, 4 * HD:5 * HD]
        vT = work[:, 5 * HD:6 * HD]
        h3T = [work[:, 6 * HD + P * b:6 * HD + P * b + P] for b in range(4)]
        yg = [big[:, ob + 2 * D * b:ob + 2 * D * (b + 1)] for b in range(4)]
        ya = [big[:, ob + 8 * D + D * b:ob + 8 * D + D * (b + 1)] for b in range(4)]
        xg = [work[:, RW * b:RW * b + RW] for b in range(NB)]
        yo = [work[:, 1040 + D * b:1040 + D * b + D] for b in range(NB)]
        xgT = [work[:, 2064 + P * b:2064 + P * b + P] for b in range(2)]
        hb = [work[:, 2320 + H0 * b:2320 + H0 * (b + 1)] for b in range(2)]
        hbT = [work[:, 3344 + H0 * b:3344 + H0 * (b + 1)] for b in range(2)]
        act1 = [work[:, 4368 + 176 * b:4368 + 176 * b + H1] for b in range(2)]
        shT = [(work[:, 5120 + 512 * c:5120 + 512 * (c + 1)] if c < 4 else
                big[:, ob + 512 * c:ob + 512 * (c + 1)]) for c in range(2 * len(SC))]

        s_consts = sem("constants_made")
        passed = sem("passed")
        ld_x, ld_c, ld_attn, ld_router = sem("ld_x"), sem("ld_c"), sem("ld_attn"), sem("ld_router")
        ld_w0, ld_w1, ld_l1 = sem("ld_experts0"), sem("ld_experts1"), sem("ld_layer1")
        s_silu_act, s_silu = sem("silu_exp"), sem("silu_steps")
        s_mod, s_mod_used, s_mod_ready = sem("mod_products"), sem("mod_used"), sem("mod_ready")

        def layer_norm(name, xn=None):
            if xn is None:
                own = sb(name + "_xn", [P, 2, D])
                xn = [own[:, b % 2, :] for b in range(4)]
            return {
                "stats": sb(name + "_stats", [P, 2, 6]),
                "mv": sb(name + "_mv", [P, 4, 2]),
                "r": sb(name + "_r", [P, 4, 2]),
                "xn": xn,
                "moments": sem(name + "_moments"),
                "rstd": sem(name + "_rstd"),
                "normed": sem(name + "_normed"),
            }

        def ln_measure(dve, n, src, t, b):
            settle(dve, passed)
            dve.bn_stats(n["stats"][:, b % 2, :], src).then_inc(n["moments"], 1)
            dve.wait_ge(n["moments"], 2 * t + 1)
            settle(dve, passed)
            dve.bn_aggr(n["mv"][:, b, :], n["stats"][:, b % 2, :]).then_inc(n["moments"], 1)

        def ln_deviation(act, n, t, b):
            act.wait_ge(n["moments"], 2 * t + 2)
            act.activation(n["r"][:, b, 0:1], n["mv"][:, b, 1:2], ACT.Ln, bias=eps[:, :]).then_inc(n["rstd"], 1)
            act.wait_ge(n["rstd"], 2 * t + 1)
            act.activation(n["r"][:, b, 1:2], n["r"][:, b, 0:1], ACT.Exp, scale=-0.5).then_inc(n["rstd"], 1)

        def ln_scale(dve, n, src, t, b):
            dve.wait_ge(n["rstd"], 2 * t + 2)
            dve.tensor_scalar(n["xn"][b], src, n["mv"][:, b, 0:1], n["r"][:, b, 1:2],
                              ALU.subtract, ALU.mult).then_inc(n["normed"], 1)

        PICK, RANK, GATE = 10, 4, 4

        def router(layer, ln, scale_shift, logits_ps, rank_ps, xT_ps):
            n = f"router{layer}_"
            return {
                "layer": layer, "ln": ln, "ss": scale_shift,
                "logits_ps": logits_ps, "rank_ps": rank_ps, "xT_ps": xT_ps,
                "hb": sb(n + "hT", [P, 2, P]),
                "lg": sb(n + "lg", [P, 2, 2, E]),
                "top": sb(n + "top", [P, 2, 2, 8]),
                "ti": sb(n + "ti", [P, 2, 2, 8], U32),
                "tf": sb(n + "tf", [P, 2, 2, 2]),
                "hot": sb(n + "hot", [P, 2, 2, 2, E]),
                "pick": sb(n + "pick", [P, 2, 2, E], BF16),
                "dx": sb(n + "dx", [P, 2, 2 * E + 4]),
                "ex": sb(n + "ex", [P, 2, 2 * E + 4]),
                "se": sb(n + "se", [P, 2, 2, 2]),
                "rk": sb(n + "rk", [P, 2, 2, E]),
                "sel": sb(n + "sel", [P, 2, 2, 2, E]),
                "pf": sb(n + "pf", [P, 2, 4]),
                "at": sb(n + "at", [P, 2, 4], I32),
                "xT": sem(n + "xT"),
                "h": sem(n + "h"),
                "logits": sem(n + "logits"),
                "picked": sem(n + "picked"),
                "exps": sem(n + "exps"),
                "rank": sem(n + "rank"),
                "placed": sem(n + "placed"),
                "gated": sem(n + "gated"),
                "doubled": sem(n + "doubled"),
                "sent": [sem(n + f"sent{h}") for h in range(2)],
            }

        def wait_rows_sent(dve, r, t, b):
            if not (isinstance(t, int) and t < 4):
                dve.wait_ge(r["sent"][b // 2], 16 * (t - b))

        def pe_transpose(pe, r, t, b):
            pe.wait_ge(r["ln"]["normed"], t + 1)
            after(pe, r["h"], t)
            pe.transpose(r["xT_ps"], r["ln"]["xn"][b], ident[:, :]).then_inc(r["xT"], 1)

        def act_modulate(act, r, t, b):
            act.wait_ge(r["xT"], t + 1)
            after(act, r["logits"], t - 1)
            act.activation(r["hb"][:, b % 2, :], r["xT_ps"], ACT.Identity,
                           bias=r["ss"][0], scale=r["ss"][1]).then_inc(r["h"], 1)

        def pe_logits(pe, r, t, b):
            pe.wait_ge(r["h"], t + 1)
            pe.matmul(r["logits_ps"][:, b % 2, :], r["hb"][:, b % 2, :], Wr[:, r["layer"], :],
                      start=True, stop=True).then_inc(r["logits"], 1)

        def dve_pick(dve, r, t, b, q):
            if b % 2 == 0:
                return
            h, g = b // 2, 2 * q + b // 2
            k = PICK * g
            lg, top, ti, dx = r["lg"][:, h, :, :], r["top"][:, h, :, :], r["ti"][:, h, :, :], r["dx"][:, h, :]
            dve.wait_ge(r["logits"], t + 1)
            dve.tensor_tensor(lg, r["logits_ps"], brB[:, r["layer"], :].unsqueeze(1).to_broadcast([P, 2, E]),
                              ALU.add).then_inc(r["picked"], 1)
            dve.wait_ge(r["picked"], k + 1)
            settle(dve, passed)
            for i in range(2):
                dve.max(top[:, i, :], lg[:, i, :]).then_inc(r["picked"], 1)
            dve.wait_ge(r["picked"], k + 3)
            settle(dve, passed)
            for i in range(2):
                dve.max_index(ti[:, i, :], top[:, i, :], lg[:, i, :]).then_inc(r["picked"], 1)
            after(dve, r["exps"], g - 1)
            dve.tensor_tensor(dx[:, 0:2 * E].rearrange("p (i e) -> p i e", i=2), lg,
                              top[:, :, 0:1].to_broadcast([P, 2, E]), ALU.subtract).then_inc(r["picked"], 1)
            dve.tensor_tensor(dx[:, 2 * E:2 * E + 4].rearrange("p (i k) -> p i k", i=2), top[:, :, 0:2],
                              top[:, :, 0:1].to_broadcast([P, 2, 2]), ALU.subtract).then_inc(r["picked"], 1)
            dve.wait_ge(r["picked"], k + 5)
            dve.tensor_scalar(r["tf"][:, h, :, :], ti[:, :, 0:2], 1.0, None, ALU.mult).then_inc(r["picked"], 1)
            dve.wait_ge(r["picked"], k + 8)
            for i in range(1):
                dve.tensor_tensor(r["hot"][:, h, :, :, :].rearrange("p i k e -> p (i k) e"),
                                  expert_id[:, :].unsqueeze(1).to_broadcast([P, 4, E]),
                                  r["tf"][:, h, :, :].rearrange("p i k -> p (i k)").unsqueeze(2)
                                  .to_broadcast([P, 4, E]), ALU.is_equal).then_inc(r["picked"], 1)
            dve.wait_ge(r["picked"], k + 9)
            after(dve, r["rank"], g - 1)
            dve.tensor_tensor(r["pick"][:, h, :, :], r["hot"][:, h, :, 0, :], r["hot"][:, h, :, 1, :],
                              ALU.add).then_inc(r["picked"], 1)

        def act_exps(act, r, t, b, q):
            if b % 2 == 0:
                return
            h, g = b // 2, 2 * q + b // 2
            act.wait_ge(r["picked"], PICK * g + 7)
            after(act, r["gated"], GATE * (g - 1))
            act.activation(r["ex"][:, h, :], r["dx"][:, h, :], ACT.Exp).then_inc(r["exps"], 1)

        def pe_rank(pe, r, t, b, q):
            if b % 2 == 0:
                return
            h, g = b // 2, 2 * q + b // 2
            pe.wait_ge(r["picked"], PICK * (g + 1))
            after(pe, r["placed"], RANK * (g - 1) + 2)
            for i in range(2):
                o = r["rank_ps"][:, i, :]
                pe.matmul(o, before[:, :], r["pick"][:, h, i, :], start=True, stop=False)
                if i:
                    pe.matmul(o, ones[:, :], r["pick"][:, h, 0, :], start=False, stop=False)
                pe.matmul(o, ones[:, :], macc[:, r["layer"], 0, :], start=False, stop=False)
                last = pe.matmul(o, ones[:, :], macc[:, r["layer"], 1, :], start=False, stop=True)
            last.then_inc(r["rank"], 1)

        def dve_place(dve, r, t, b, q):
            if b % 2 == 0:
                return
            h, g = b // 2, 2 * q + b // 2
            k = RANK * g
            dve.wait_ge(r["rank"], g + 1)
            dve.tensor_tensor(r["rk"][:, h, :, :], r["rank_ps"],
                              region_at[:, :].unsqueeze(1).to_broadcast([P, 2, E]), ALU.add).then_inc(r["placed"], 1)
            dve.tensor_tensor(macc[:, r["layer"], :, :], macc[:, r["layer"], :, :], r["pick"][:, h, :, :],
                              ALU.add).then_inc(r["placed"], 1)
            dve.wait_ge(r["placed"], k + 1)
            dve.tensor_tensor(r["sel"][:, h, :, :, :], r["hot"][:, h, :, :, :],
                              r["rk"][:, h, :, :].unsqueeze(2).to_broadcast([P, 2, 2, E]),
                              ALU.mult).then_inc(r["placed"], 1)
            dve.wait_ge(r["exps"], g + 1)
            dve.reduce_sum(r["se"][:, h, 0, :], r["ex"][:, h, 0:2 * E].rearrange("p (i e) -> p i e", i=2),
                           AX_X).then_inc(r["gated"], 1)
            dve.wait_ge(r["placed"], k + 3)
            dve.reduce_sum(r["pf"][:, h, :], r["sel"][:, h, :, :, :].rearrange("p i k e -> p (i k) e"),
                           AX_X).then_inc(r["placed"], 1)
            dve.wait_ge(r["gated"], GATE * g + 1)
            dve.reciprocal(r["se"][:, h, 1, :], r["se"][:, h, 0, :]).then_inc(r["gated"], 1)
            wait_rows_sent(dve, r, t, b)
            dve.wait_ge(r["placed"], k + 4)
            dve.tensor_scalar(r["at"][:, h, :], r["pf"][:, h, :], 1.0, None, ALU.mult).then_inc(r["gated"], 1)
            dve.wait_ge(r["gated"], GATE * g + 2)
            dve.tensor_tensor(gates[:, r["layer"], bass.ds(t - 1, 2), :],
                              r["ex"][:, h, 2 * E:2 * E + 4].rearrange("p (i k) -> p i k", i=2),
                              r["se"][:, h, 1, :].unsqueeze(2).to_broadcast([P, 2, 2]),
                              ALU.mult).then_inc(r["gated"], 1)

        def pool_double(pool, r, t, b):
            pool.wait_ge(r["ln"]["normed"], t + 1)
            settle(pool, passed)
            pool.tensor_copy(rows[:, b, 1, 0:D], rows[:, b, 0, 0:D]).then_inc(r["doubled"], 1)
            pool.tensor_copy(rows[:, b, :, D:RW].rearrange("p k a -> p (k a)").bitcast(I32),
                             result_row[:, bass.ds(t, 1), :].rearrange("p a k -> p (a k)")).then_inc(r["doubled"], 1)

        def pool_send(pool, r, t, b, q):
            if b % 2 == 0:
                return
            h, g = b // 2, 2 * q + b // 2
            pool.wait_ge(r["gated"], GATE * g + 3)
            pool.wait_ge(r["doubled"], 2 * t + 2)
            settle(pool, passed)
            for i in range(2):
                for k in range(TOPK):
                    c = 2 * i + k
                    pool.indirect_dma_start(xs[r["layer"]], bass.IndirectOffsetOnAxis(r["at"][:, h, c:c + 1], 0),
                                            rows[:, b - 1 + i, k, :], None).then_inc(r["sent"][h], 16)

        outgoing = [rows[:, b, 0, 0:D] for b in range(4)]
        ln1, ln2, ln3, ln4, ln5 = (layer_norm(f"ln{k}", outgoing if k in (2, 5) else None) for k in range(1, 6))
        small = [bank[:, 6, 2 * E * i:2 * E * (i + 1)].rearrange("p (i e) -> p i e", i=2) for i in range(2)]
        router0 = router(0, ln2, (mcol[:, 0, 2:3], mcol[:, 0, 3:4]), *small,
                         bank[:, 5, 0:P])
        router1 = router(1, ln5, (mcol[:, 1, 2:3], mcol[:, 1, 3:4]), *small,
                         bank[:, 6, P:2 * P])
        turned1, beta = bank[:, 7, 0:P], bank[:, 7, P:P + NH]
        attn1 = bank[:, 6, 2 * P:3 * P]
        ends = (0, 7)
        routers = [router0, router1]

        a_xT, a_h, a_win = sem("a_xT"), sem("a_h"), sem("a_window")
        a_kv, a_k, a_v = sem("a_kv"), sem("a_k_copied"), sem("a_v_copied")
        a_hs, a_vt, a_vtc = sem("a_hsum"), sem("a_vtot"), sem("a_vtot_copied")
        b_q, b_qT, b_s, b_sm = sem("b_q"), sem("b_qT"), sem("b_scores"), sem("b_masked")
        b_nm, b_p, b_pp, b_pT, b_pTc = sem("b_negmax"), sem("b_exp"), sem("b_probs"), sem("b_pT"), sem("b_pTc")
        b_o, b_ao, b_x = sem("b_out"), sem("b_attended"), sem("b_x")
        t_cnt, t_dve, t_cum, t_val, t_ready = (sem("t_counts"), sem("t_dve"), sem("t_cumulated"),
                                               sem("t_values"), sem("t_ready"))
        z_sent = sem("zero_rows_sent")
        e_x = [sem(f"e_x{b}") for b in range(NB)]
        e_y = [sem(f"e_y{b}") for b in range(NB)]
        e_xT, e_xTc, e_h, e_hb, e_hT, e_hTc, e_o, e_yo = (
            sem("e_xT"), sem("e_xTc"), sem("e_hidden"), sem("e_hb"), sem("e_hT"), sem("e_hTc"),
            sem("e_out"), sem("e_yo"))
        e_silu, e_act = sem("e_silu"), sem("e_act")
        d_x = sem("d_x")
        d_g = [sem(f"d_results{b}") for b in range(4)]
        w2_scaled, w2_steps = sem("w2_scaled"), sem("w2_steps")
        d_xT, d_h, d_q, d_k, d_v, d_b = sem("d_xT"), sem("d_h"), sem("d_q"), sem("d_k"), sem("d_v"), sem("d_beta")
        DS = 9
        d_eb = sem("d_exp_beta")
        d_e, d_f, d_qk, d_sum = sem("d_exp"), sem("d_feature"), sem("d_qk"), sem("d_sums")
        d_vT, d_vTc, d_o, d_y = sem("d_vT"), sem("d_vTc"), sem("d_out"), sem("d_y")
        f_in, f_h, f_a, f_g, f_o, f_x = (sem("f_in"), sem("f_hidden"), sem("f_act"), sem("f_gated"), sem("f_out"),
                                        sem("f_x"))
        g_x, g_st = sem("g_x"), sem("g_stored")
        g_g = [sem(f"g_results{b}") for b in range(4)]

        def zero_rows(eng, l, first, count):
            eng.wait_ge(t_ready, l + 1)
            with eng.Fori(0, count // 4) as j:
                n = [eng.value_load(tbl[0:1, bass.ds(4 * j + (first + i + 2 * P), 1)], min_val=0, max_val=T)
                     for i in range(4)]
                for i in range(4):
                    eng.dma_start(xs[l][bass.ds(4 * REGION * j + n[i] + (first + i) * REGION, P), :],
                                  zeros[:, :]).then_inc(z_sent, 16)

        def all_row(ap, n):
            return ap.rearrange("(a n) -> a n", a=1).to_broadcast([P, n])

        def xt(t):
            return xres[:, bass.ds(t * D, D)]

        block = ctx.enter_context(nc.Block())

        @block.sync
        def _(sp):
            sp.dma_start(cT[:, :], c01).then_inc(ld_c, 16)
            sp.dma_start(xres[:, :].rearrange("p (t d) -> p t d", d=D),
                         x.rearrange("(t p) d -> p t d", p=P)).then_inc(ld_x, 16)
            sp.dma_start(wmod[:, 0, :], wmod0).then_inc(ld_c, 16)
            sp.dma_start(wmod[:, 1, :], wmod1).then_inc(ld_c, 16)
            for k, w in enumerate((WQ, WK, WV)):
                sp.dma_start(Wa[:, k, :], w).then_inc(ld_attn, 16)
            for k, (w, b) in enumerate(((Wr0, br0), (Wr1, br1))):
                sp.dma_start(Wr[:, k, :], w).then_inc(ld_router, 16)
                sp.dma_start(brB[:, k, :], all_row(b, E)).then_inc(ld_router, 16)
            sp.dma_start(W1s.rearrange("p (e h) -> p e h", e=E), W1.rearrange("e d h -> d e h")).then_inc(ld_w0, 16)
            sp.dma_start(W2s.rearrange("p (e c d) -> p e c d", e=E, c=C0),
                         W2.rearrange("e (c p) d -> p e c d", p=P)).then_inc(ld_w0, 16)
            sp.dma_start(bias_big[:, :], all_row(b1.rearrange("e h -> (e h)"), E * H0)).then_inc(ld_w0, 16)
            sp.dma_start(b2B[:, :], all_row(b2.rearrange("e d -> (e d)"), E * D)).then_inc(ld_w0, 16)
            sp.dma_start(Wqkvb[:, :], WqkvbT).then_inc(ld_l1, 16)
            sp.dma_start(Wo[:, :, :], WoT.rearrange("(c p) d -> p c d", p=P)).then_inc(ld_l1, 16)
            for k, w in enumerate((ln_g, ln_b)):
                sp.dma_start(lnB[:, k, :], all_row(w, D)).then_inc(ld_l1, 16)
            for k, (w, b) in enumerate(((sw1, sb1), (sw3, sb3))):
                sp.dma_start(sw13[:, k, :], w).then_inc(ld_l1, 16)
                for c, (a, m) in enumerate(SC):
                    sp.dma_start(sb13[0:m, k, c:c + 1], b[a:a + m].rearrange("(p a) -> p a", a=1)).then_inc(ld_l1, 16)
            for c, (a, m) in enumerate(SC):
                sp.dma_start(sw2s[0:m, c, :], sw2[a:a + m, :]).then_inc(ld_l1, 16)
            sp.dma_start(sb2r[:, :], sb2.rearrange("(a n) -> a n", a=1)).then_inc(ld_l1, 16)
            sp.wait_ge(s_consts, 2)
            for l in range(2):
                sp.dma_start(xs[l][DUMMY:ROWS, :].rearrange("(k p) d -> p k d", p=P),
                             zeros[:, :].unsqueeze(1).to_broadcast([P, SPARE, RW])).then_inc(z_sent, 16)

            for l in range(2):
                zero_rows(sp, l, 0, E // 2)
                sp.wait_ge(z_sent, 32 + 16 * E * (l + 1))
                for h in range(2):
                    sp.wait_ge(routers[l]["sent"][h], 16 * NT)

                def load(t, b, q):
                    row = sp.value_load(tbl[0:1, bass.ds(t, 1)], min_val=0, max_val=ROWS - P)
                    if l or not (isinstance(t, int) and t < NB):
                        sp.wait_ge(e_xT, l * SLOTS + t - NB + 1)
                        settle(sp, passed)
                        sp.wait_ge(e_y[b], 16 * (l * (SLOTS // NB) + q))
                        settle(sp, passed)
                    sp.dma_start(xg[b], xs[l][bass.ds(row, P), :]).then_inc(e_x[b], 16)

                run_tiles(sp, SLOTS, NB, [(0, load)])
                for b in range(NB):
                    sp.wait_ge(e_y[b], 16 * (l + 1) * (SLOTS // NB))

                def results(t, b, q):
                    if not (isinstance(t, int) and t < 4):
                        sp.wait_ge((d_x, g_x)[l], 2 * (t - 3))
                        settle(sp, passed)
                    sp.dma_start(yg[b], ys[l].rearrange("(n k) d -> n (k d)", k=TOPK)[bass.ds(t * P, P), :]
                                 ).then_inc((d_g, g_g)[l][b], 16)
                    if l and (not isinstance(t, int) or t >= 3):
                        put(t - 3)

                def put(t):
                    sp.wait_ge(g_x, 2 * t + 2)
                    settle(sp, passed)
                    sp.dma_start(out[bass.ds(t * P, P), :], xt(t)).then_inc(g_st, 16)

                run_tiles(sp, NT, 4, [(0, results)])
                if l:
                    for t in range(NT - 3, NT):
                        put(t)

            sp.wait_ge(g_st, 16 * NT)


        @block.gpsimd
        def _(pool):
            pool.memset(zeros[:, :], 0.0)
            pool.memset(onerow[:, :], 1.0)
            pool.memset(eps[:, :], EPS)
            pool.memset(ones[:, :], 1.0)
            pool.memset(macc[:, :, :, :], 0.0)
            pool.memset(hT[:, 0:BAND], 0.0)
            pool.memset(hT[:, BAND + T:PADT], 0.0)
            pool.memset(kT[:, 0:BAND], 0.0)
            pool.memset(kT[:, BAND + T:PADT], 0.0)
            pool.iota(result_row[:, :, :], [[TOPK * P, NT], [1, TOPK]], base=0, channel_multiplier=TOPK)
            pool.memset(ident[:, :], 0.0)
            pool.memset(band[:, :], 1.0)
            pool.memset(before[:, :], 1.0)
            pool.memset(upto[:, :], 1.0)
            pool.iota(expert_id[:, :], [[1, E]], base=0, channel_multiplier=0, allow_small_or_imprecise_dtypes=True)
            pool.iota(region_at[:, :], [[REGION, E]], base=0, channel_multiplier=0, allow_small_or_imprecise_dtypes=True)
            pool.iota(slot_id[:, :], [[0, 1]], base=0, channel_multiplier=1,
                      allow_small_or_imprecise_dtypes=True).then_inc(s_consts, 1)
            pool.wait_ge(s_consts, 1)
            pool.affine_select(out=ident[:, :], in_=ident[:, :], compare_op=ALU.not_equal, fill=1.0, base=0,
                               pattern=[[1, P]], channel_multiplier=-1)
            pool.affine_select(out=band[:, :], in_=band[:, :], compare_op=ALU.is_ge, fill=0.0, base=0,
                               pattern=[[1, WIN]], channel_multiplier=-1)
            pool.memset(zeros[:, D:RW].bitcast(I32), NOWHERE)
            pool.affine_select(out=before[:, :], in_=before[:, :], compare_op=ALU.is_ge, fill=0.0, base=-1,
                               pattern=[[1, P]], channel_multiplier=-1)
            pool.affine_select(out=upto[:, :], in_=upto[:, :], compare_op=ALU.is_ge, fill=0.0, base=0,
                               pattern=[[1, E]], channel_multiplier=-1).then_inc(s_consts, 1)
            pool.wait_ge(s_consts, 2)
            pool.affine_select(out=band[:, :], in_=band[:, :], compare_op=ALU.is_ge, fill=0.0, base=2 * BAND - 1,
                               pattern=[[-1, WIN]], channel_multiplier=1).then_inc(s_consts, 1)

            def window(t, b, q):
                pool.wait_ge(a_h, t + 1)
                after(pool, a_kv, t - 1)
                settle(pool, passed)
                pool.tensor_copy(hwin[:, b, :], hT[:, bass.ds(t * P, P)]).then_inc(a_win, 1)

            run_tiles(pool, NT, 2, [(2, window)])
            pool.wait_ge(a_kv, NT - 1)
            pool.tensor_copy(hwin[:, 0, 0:2 * BAND], hT[:, T:T + 2 * BAND]).then_inc(a_win, 1)

            def scale_w2(t, b, q):
                w = W2s[:, bass.ds(t * H0, H0)].rearrange("p (c d) -> p c d", c=C0)
                pool.tensor_tensor(w, w, gB[:, 0, 1, :].unsqueeze(1).to_broadcast([P, C0, D]),
                                   ALU.mult).then_inc(w2_scaled, 1)

            assert E == NT
            pool.wait_ge(ld_w0, 64)
            run_tiles(pool, NT, 4, [(4, lambda t, b, q: pool_double(pool, router0, t, b)), (0, scale_w2),
                                    (4, lambda t, b, q: pool_send(pool, router0, t, b, q))])

            def scatter_results(l):
                def stage(t, b, q):
                    pool.wait_ge(e_yo, l * SLOTS + t + 1)
                    settle(pool, passed)
                    pool.indirect_dma_start(ys[l], bass.IndirectOffsetOnAxis(xg[b][:, D:RW].bitcast(I32), 0), yo[b], None,
                                            bounds_check=TOPK * T - 1, oob_is_err=False).then_inc(e_y[b], 16)
                return stage

            run_tiles(pool, SLOTS, NB, [(4, scatter_results(0))])

            def product(t, b, q):
                pool.wait_ge(d_f, 2 * t + 2)
                pool.tensor_tensor(rf[:, 0:HD], ef[:, 0:HD], ef[:, HD:2 * HD], ALU.mult).then_inc(d_qk, 1)

            def residual(t, b, q):
                pool.wait_ge(ln4["normed"], t + 1)
                pool.tensor_tensor(ya[b], ln4["xn"][b], lnG[:, 0, :], ALU.mult).then_inc(d_y, 1)
                pool.wait_ge(d_y, 3 * t + 1)
                pool.tensor_tensor(ya[b], ya[b], lnG[:, 1, :], ALU.add).then_inc(d_y, 1)
                pool.wait_ge(d_y, 3 * t + 2)
                pool.tensor_tensor(xt(t), xt(t), ya[b], ALU.add).then_inc(d_y, 1)

            run_tiles(pool, NT, 4, [(4, residual), (2, product),
                                    (5, lambda t, b, q: pool_double(pool, router1, t, b)),
                                    (5, lambda t, b, q: pool_send(pool, router1, t, b, q))])
            pool.wait_ge(ld_w1, 96)
            w = w2s.rearrange("p (e d) -> p e d", d=D)
            pool.tensor_tensor(w, w, gB[0:K1, 1, 1, :].unsqueeze(1).to_broadcast([K1, 2 * E, D]),
                               ALU.mult).then_inc(w2_scaled, 1)
            run_tiles(pool, SLOTS, NB, [(4, scatter_results(1))])

        @block.scalar
        def _(act):
            act.preload_act_table_set("natural_log_exp_and_others")
            act.wait_ge(ld_c, 48)
            act.activation(sc[:, 0, :], cT[:, :], ACT.Exp, scale=-1.0).then_inc(s_silu_act, 1)
            act.wait_ge(s_consts, 3)
            act.wait_ge(s_mod_ready, 1)

            def hidden(t, b, q):
                act.wait_ge(a_xT, t + 1)
                act.activation(hT[:, bass.ds(t * P + BAND, P)], bank[:, b, 0:P], ACT.Identity,
                               bias=mcol[:, 0, 0:1], scale=mcol[:, 0, 1:2],
                               accum_out=hsum[:, bass.ds(t, 1)]).then_inc(a_h, 1)

            def keys(t, b, q):
                act.wait_ge(a_kv, t + 1)
                act.copy(kT[:, bass.ds(t * P + BAND, P)], bank[:, 2 + b, 0:P]).then_inc(a_k, 1)

            run_tiles(act, NT, 2, [(2, hidden), (4, keys), (0, lambda t, b, q: ln_deviation(act, ln1, t, b))])

            def queries(t, b, q):
                act.wait_ge(b_q, t + 1)
                after(act, b_s, t - 1)
                act.copy(qT[:, b % 2, :], bank[:, ends[b % 2], 0:P]).then_inc(b_qT, 1)

            def exps(t, b, q):
                act.wait_ge(b_nm, t + 1)
                after(act, b_pT, t - 1)
                after(act, b_ao, t - 3)
                act.activation(pr[:, b % 2, :], sm[:, b % 2, :], ACT.Exp, bias=st6[:, 1, b:b + 1],
                               accum_out=st6[:, 2, b:b + 1]).then_inc(b_p, 1)
                act.activation(st6[:, 3, b:b + 1], st6[:, 1, b:b + 1], ACT.Exp).then_inc(b_p, 1)

            def probs(t, b, q):
                act.wait_ge(b_pT, t + 1)
                after(act, b_o, t - 1)
                act.copy(pT[:, b % 2, 0:P], bank[:, 3, 0:P]).then_inc(b_pTc, 1)
                act.copy(pT[0:2 * BAND, b % 2, P:2 * P], bank[0:2 * BAND, 3, P:2 * P]).then_inc(b_pTc, 1)

            run_tiles(act, NT, 4, [(0, queries), (4, lambda t, b, q: act_modulate(act, router0, t, b)), (1, exps),
                                   (2, probs), (3, lambda t, b, q: ln_deviation(act, ln2, t, b)),
                                   (4, lambda t, b, q: act_exps(act, router0, t, b, q))])

            def tokens(l, scale_shift):
                def stage(t, b, q):
                    act.wait_ge(e_xT, l * SLOTS + t + 1)
                    after(act, e_h, l * SLOTS + t - 1)
                    act.activation(xgT[b % 2], bank[:, ends[b % 2], 0:P], ACT.Identity,
                                   bias=scale_shift[0], scale=scale_shift[1]).then_inc(e_xTc, 1)
                return stage

            def relu(t, b, q):
                act.wait_ge(e_hT, t + 1)
                after(act, e_o, t - 1)
                act.activation(hbT[b % 2], bank[:, 3 + b % 2, :], ACT.Relu).then_inc(e_hTc, 1)

            zero_rows(act, 0, E // 2, E // 2)
            run_tiles(act, SLOTS, NB, [(2, relu), (0, tokens(0, router0["ss"]))])

            act.wait_ge(e_o, SLOTS)
            act.wait_ge(e_yo, SLOTS)
            w13v = w13s.rearrange("p (e k h) -> p e k h", e=E, k=2)
            bv = bias_big[:, 0:2 * E * H1].rearrange("p (e k h) -> p e k h", e=E, k=2)
            for k, (w, b) in enumerate(((w1, b1e), (w3, b3e))):
                act.dma_start(w13v[:, :, k, :], w.rearrange("e d h -> d e h")).then_inc(ld_w1, 16)
                act.dma_start(bv[:, :, k, :], b.rearrange("(a e) h -> a e h", a=1)
                              .to_broadcast([P, E, H1])).then_inc(ld_w1, 16)
            act.dma_start(w2s.rearrange("p (e c d) -> p e c d", e=E, c=2),
                          w2.rearrange("e (c p) d -> p e c d", p=K1)).then_inc(ld_w1, 16)
            act.dma_start(b2B[:, :], all_row(b2e.rearrange("e d -> (e d)"), E * D)).then_inc(ld_w1, 16)

            def hidden1(t, b, q):
                act.wait_ge(d_xT, t + 1)
                after(act, d_o, t - 3)
                act.activation(h3T[b], turned1, ACT.Identity,
                               bias=mcol[:, 1, 0:1], scale=mcol[:, 1, 1:2]).then_inc(d_h, 1)

            def feature_parts(t, b, q):
                for k, (ready, bk) in enumerate(((d_q, 0), (d_k, 2))):
                    act.wait_ge(ready, t + 1)
                    after(act, d_sum, DS * (t - 1) + 2)
                    act.activation(rf[:, k * HD:(k + 1) * HD], bank[:, bk:bk + 2, :].rearrange("p a n -> p (a n)"),
                                   ACT.Relu, scale=-1.0).then_inc(d_e, 1)
                    act.wait_ge(d_e, 4 * t + 2 * k + 1)
                    act.activation(ef[:, k * HD:(k + 1) * HD], rf[:, k * HD:(k + 1) * HD], ACT.Exp,
                                   scale=-1.0).then_inc(d_e, 1)
                act.wait_ge(d_b, t + 1)
                act.activation(eb[:, 0, :], beta, ACT.Relu, scale=-1.0).then_inc(d_eb, 1)
                act.activation(eb[:, 1, :], beta, ACT.Abs).then_inc(d_eb, 1)
                act.wait_ge(d_eb, 3 * t + 2)
                after(act, d_sum, DS * (t - 1) + 7)
                act.activation(eb[:, 2:4, :], eb[:, 0:2, :], ACT.Exp, scale=-1.0).then_inc(d_eb, 1)

            def values_turned(t, b, q):
                after(act, d_o, t)
                for k in range(2):
                    act.wait_ge(d_vT, 2 * t + k + 1)
                    act.copy(vT[:, k * 512:(k + 1) * 512], bank[:, 4 + k, :]).then_inc(d_vTc, 1)

            def keep(t, b, q):
                act.wait_ge(router1["h"], t + 1)
                act.copy(hT[:, bass.ds(t * P, P)], router1["hb"][:, b % 2, :]).then_inc(f_in, 1)

            run_tiles(act, NT, 4, [
                (3, values_turned), (1, lambda t, b, q: ln_deviation(act, ln3, t, b)),
                (4, lambda t, b, q: ln_deviation(act, ln5, t, b)), (2, feature_parts),
                (5, lambda t, b, q: act_modulate(act, router1, t, b)), (5, keep), (1, hidden1),
                (5, lambda t, b, q: act_exps(act, router1, t, b, q)),
                (3, lambda t, b, q: ln_deviation(act, ln4, t, b))])
            zero_rows(act, 1, E // 2, E // 2)

            act.preload_act_table_set("silu_and_others")

            def shared_silu(t, b, q):
                for c, (a, m) in enumerate(SC):
                    act.wait_ge(f_h, 2 * (len(SC) * t + c) + 1)
                    after(act, f_g, len(SC) * t)
                    act.activation(shT[c][0:m, :], bank[0:m, c, :], ACT.Silu,
                                   bias=sb13[0:m, 0, c:c + 1]).then_inc(f_a, 1)

            run_tiles(act, T // 512, 1, [(0, shared_silu)])

            def silu(t, b, q):
                act.wait_ge(e_hb, SLOTS + t + 1)
                act.wait_ge(e_hT, SLOTS + t - 1)
                act.activation(act1[b % 2], hb[b % 2][:, 0:H1], ACT.Silu).then_inc(e_silu, 1)

            def act_turned(t, b, q):
                act.wait_ge(e_hT, SLOTS + t + 1)
                act.wait_ge(e_o, SLOTS + t - 1)
                act.copy(hbT[b % 2][0:K1, 0:2 * P], bank[0:K1, 3 + b % 2, 0:2 * P]).then_inc(e_hTc, 1)

            run_tiles(act, SLOTS, NB, [(2, silu), (3, act_turned), (0, tokens(1, router1["ss"]))])

        @block.vector
        def _(dve):
            steps = [0]

            def link(ins):
                steps[0] += 1
                ins.then_inc(s_silu, 1)
                dve.wait_ge(s_silu, steps[0])

            dve.wait_ge(s_silu_act, 1)
            link(dve.tensor_scalar(sc[:, 1, :], sc[:, 0, :], 1.0, None, ALU.add))
            link(dve.reciprocal(sc[:, 2, :], sc[:, 1, :]))
            link(dve.tensor_tensor(sc[:, 3, :], sc[:, 2, :], cT[:, :], ALU.mult))
            dve.tensor_copy(siluB[:, :, :], sc[:, 3, :].unsqueeze(2).to_broadcast([P, 2, P])).then_inc(s_mod_used, 1)
            dve.wait_ge(s_mod, 1)
            for l in range(2):
                for k in range(2):
                    link(dve.tensor_copy(mcol[:, l, 2 * k:2 * k + 1], bank[:, 4, 8 * l + 2 * k:8 * l + 2 * k + 1]))
                    link(dve.tensor_scalar(mcol[:, l, 2 * k + 1:2 * k + 2],
                                           bank[:, 4, 8 * l + 2 * k + 1:8 * l + 2 * k + 2], 1.0, None, ALU.add))
                    g = bank[:, 2 * l + k, 0:D]
                    link(dve.tensor_scalar(gtmp[:, 0, :], g, -1.0, None, ALU.mult))
                    link(dve.tensor_tensor(gtmp[:, 1, :], gtmp[:, 0, :], g, ALU.max))
                    link(dve.tensor_scalar(gtmp[:, 0, :], gtmp[:, 1, :], 0.25, None, ALU.max))
                    link(dve.tensor_scalar(gtmp[:, 2, :], g, 0.0, 2.0, ALU.is_ge, ALU.mult))
                    link(dve.scalar_tensor_tensor(gB[:, l, k, :], gtmp[:, 2, :], -1.0, gtmp[:, 0, :], ALU.add, ALU.mult))
            dve.wait_ge(ld_attn, 48)
            dve.tensor_tensor(Wa[:, 2, :], Wa[:, 2, :], gB[:, 0, 0, :], ALU.mult).then_inc(s_mod_ready, 1)

            dve.wait_ge(ld_x, 16)
            dve.wait_ge(s_consts, 3)

            def values(t, b, q):
                dve.wait_ge(a_kv, t + 1)
                dve.tensor_copy(V[:, bass.ds(t * D, D)], bank[:, 4 + b, 0:D]).then_inc(a_v, 1)

            run_tiles(dve, NT, 2, [(1, lambda t, b, q: ln_scale(dve, ln1, xt(t), t, b)), (4, values),
                                   (0, lambda t, b, q: ln_measure(dve, ln1, xt(t), t, b))])
            dve.wait_ge(a_kv, NT + 1)
            dve.tensor_copy(V[0:2 * BAND, NT * D:(NT + 1) * D], bank[0:2 * BAND, 4, 0:D]).then_inc(a_v, 1)
            dve.wait_ge(a_h, NT)
            dve.reduce_sum(st6[:, 0, 0:1], hsum[:, :], AX_X).then_inc(a_hs, 1)
            dve.wait_ge(a_hs, 1)
            dve.tensor_copy(hsumB[:, :], st6[:, 0, 0:1].to_broadcast([P, P])).then_inc(a_hs, 1)
            dve.wait_ge(a_vt, 1)
            dve.tensor_copy(vtot[:, :], bank[:, 6, 0:D]).then_inc(a_vtc, 1)
            dve.wait_ge(a_vtc, 1)

            def masked(t, b, q):
                dve.wait_ge(b_s, t + 1)
                after(dve, b_p, 2 * (t - 1) - 1)
                settle(dve, passed)
                dve.tensor_tensor_reduce(sm[:, b % 2, :], bank[:, 1 + b % 2, 0:WIN], band[:, :],
                                         float(D) ** -0.5, 0.0, ALU.mult, ALU.max, st6[:, 0, b:b + 1]).then_inc(b_sm, 1)
                dve.wait_ge(b_sm, t + 1)
                dve.tensor_scalar(st6[:, 1, b:b + 1], st6[:, 0, b:b + 1], -1.0, None, ALU.mult).then_inc(b_nm, 1)

            def excess(t, b, q):
                dve.wait_ge(b_p, 2 * t + 2)
                dve.tensor_scalar(pr[:, b % 2, :], pr[:, b % 2, :], st6[:, 3, b:b + 1], None,
                                  ALU.subtract).then_inc(b_pp, 1)
                dve.scalar_tensor_tensor(st6[:, 4, b:b + 1], st6[:, 3, b:b + 1], float(T - WIN), st6[:, 2, b:b + 1],
                                         ALU.mult, ALU.add).then_inc(b_pp, 1)
                dve.wait_ge(b_pp, 3 * t + 2)
                dve.reciprocal(st6[:, 5, b:b + 1], st6[:, 4, b:b + 1]).then_inc(b_pp, 1)

            def attended(t, b, q):
                dve.wait_ge(b_o, t + 1)
                dve.wait_ge(b_pp, 3 * t + 3)
                dve.scalar_tensor_tensor(ao[:, :], vtot[:, :], st6[:, 3, b:b + 1], bank[:, 4, 0:D],
                                         ALU.mult, ALU.add).then_inc(b_ao, 1)
                dve.wait_ge(b_ao, t + 1)
                dve.scalar_tensor_tensor(xt(t), ao[:, :], st6[:, 5, b:b + 1], xt(t), ALU.mult, ALU.add).then_inc(b_x, 1)

            def measure2(t, b, q):
                dve.wait_ge(b_x, t + 1)
                ln_measure(dve, ln2, xt(t), t, b)

            def norm2(t, b, q):
                wait_rows_sent(dve, router0, t, b)
                ln_scale(dve, ln2, xt(t), t, b)

            run_tiles(dve, NT, 4, [(4, norm2), (2, excess), (1, masked), (3, attended),
                                   (4, lambda t, b, q: dve_pick(dve, router0, t, b, q)), (3, measure2),
                                   (4, lambda t, b, q: dve_place(dve, router0, t, b, q))])
            link(dve.tensor_tensor(b2B[:, :].rearrange("p (e d) -> p e d", e=E), b2B[:, :].rearrange("p (e d) -> p e d", e=E),
                                   gB[:, 0, 1, :].unsqueeze(1).to_broadcast([P, E, D]), ALU.mult))

            def slot_table(l):
                r = routers[l]
                k0 = 11 * l

                def step(k, ins):
                    ins.then_inc(t_dve, 1)
                    dve.wait_ge(t_dve, k0 + k)

                dve.wait_ge(t_cnt, l + 1)
                step(1, dve.tensor_scalar(tiles_int[:, 0, :], bank[0:E, 0, 0:P], float(P - 1), None, ALU.add))
                step(2, dve.tensor_scalar(tiles_int[:, 1, :], tiles_int[:, 0, :], 7, None, ALU.logical_shift_right))
                step(3, dve.tensor_copy(tiles_per[:, :], tiles_int[:, 1, :]))
                dve.wait_ge(t_cum, l + 1)
                step(4, dve.tensor_copy(cumt[:, 0, :], bank[:, 1, 0:E]))
                step(5, dve.tensor_scalar(cumt[:, 1, :], cumt[:, 0, :], slot_id[:, :], None, ALU.is_le))
                step(6, dve.tensor_tensor(cumt[:, 2, :], cumt[:, 0, :], cumt[:, 1, :], ALU.mult))
                step(7, dve.reduce_sum(sl[:, 0:1], cumt[:, 1, :], AX_X))
                step(8, dve.reduce_max(sl[:, 1:2], cumt[:, 2, :], AX_X))
                step(9, dve.tensor_scalar(sl[:, 2:3], sl[:, 1:2], slot_id[:, :], -float(P), ALU.subtract, ALU.mult))
                step(10, dve.scalar_tensor_tensor(slot_vals[:, 0:1], sl[:, 0:1], float(REGION), sl[:, 2:3],
                                                  ALU.mult, ALU.add))
                step(11, dve.tensor_scalar(slot_vals[:, 1:2], sl[:, 0:1], float(E - 1), None, ALU.min))
                dve.wait_ge(t_val, l + 1)
                dve.tensor_copy(tbl[:, :], bank[0:1, 2, 0:2 * P + E]).then_inc(t_ready, 1)
                dve.wait_ge(t_ready, l + 1)

            slot_table(0)

            def expert_of(eng, t):
                return eng.value_load(tbl[0:1, bass.ds(t + P, 1)], min_val=0, max_val=E - 1)

            def biased(l, width):
                def stage(t, b, q):
                    e = expert_of(dve, t)
                    dve.wait_ge(e_h, l * SLOTS + t + 1)
                    after(dve, e_hT, t - 1) if l == 0 else after(dve, e_act, t - 1)
                    dve.tensor_tensor(hb[b % 2][:, 0:width], bank[:, 1 + b % 2, 0:width],
                                      bias_big[:, bass.ds(e * width, width)], ALU.add).then_inc(e_hb, 1)
                return stage

            def result(l):
                def stage(t, b, q):
                    e = expert_of(dve, t)
                    dve.wait_ge(e_o, l * SLOTS + t + 1)
                    if l or not (isinstance(t, int) and t < NB):
                        dve.wait_ge(e_y[b], 16 * (l * (SLOTS // NB) + q))
                    dve.tensor_tensor(yo[b], bank[:, 5 + b % 2, 0:D], b2B[:, bass.ds(e * D, D)],
                                      ALU.add).then_inc(e_yo, 1)
                return stage

            dve.wait_ge(ld_w0, 64)
            run_tiles(dve, SLOTS, NB, [(1, biased(0, H0)), (3, result(0))])

            dve.wait_ge(ld_l1, 16 * (4 + 2 * (1 + len(SC)) + len(SC) + 1))
            for k in range(2):
                link(dve.tensor_tensor(lnG[:, k, :], lnB[:, k, :], gB[:, 1, 0, :], ALU.mult))
            for c, (a, m) in enumerate(SC):
                link(dve.tensor_tensor(sw2s[0:m, c, :], sw2s[0:m, c, :], gB[0:m, 1, 1, :], ALU.mult))
            link(dve.tensor_tensor(sb2r[:, :], sb2r[:, :], gB[0:1, 1, 1, :], ALU.mult))

            def combine(layer, gathered, signal):
                def stage(t, b, q):
                    dve.wait_ge(gathered[b], 16 * (q + 1))
                    g = gates[:, layer, bass.ds(t, 1), :].rearrange("p a k -> p (a k)")
                    for k in range(TOPK):
                        dve.scalar_tensor_tensor(xt(t), yg[b][:, k * D:(k + 1) * D], g[:, k:k + 1], xt(t),
                                                 ALU.mult, ALU.add).then_inc(signal, 1)
                        dve.wait_ge(signal, 2 * t + k + 1)
                return stage

            def feature(k):
                def stage(t, b, q):
                    dve.wait_ge(d_e, 4 * t + 2 * k + 2)
                    dve.scalar_tensor_tensor(ef[:, k * HD:(k + 1) * HD],
                                             bank[:, 2 * k:2 * k + 2, :].rearrange("p a n -> p (a n)"), 0.0,
                                             ef[:, k * HD:(k + 1) * HD], ALU.max, ALU.add).then_inc(d_f, 1)
                return stage

            def feature_sums(t, b, q):
                dve.wait_ge(d_f, 2 * t + 2)
                dve.reduce_sum(qk_sums[:, :, :], ef.rearrange("p (k h d) -> p k h d", k=2, h=NH), AX_X).then_inc(d_sum, 1)

            def coefficients(t, b, q):
                k0 = DS * t
                dve.wait_ge(d_qk, t + 1)
                dve.reduce_sum(sums[:, 0, :], rf[:, 0:HD].rearrange("p (h d) -> p h d", h=NH), AX_X).then_inc(d_sum, 1)
                dve.wait_ge(d_sum, k0 + 1)
                dve.tensor_tensor(sums[:, 1, :], qk_sums[:, 0, :], qk_sums[:, 1, :], ALU.mult).then_inc(d_sum, 1)
                dve.wait_ge(d_eb, 3 * t + 3)
                dve.wait_ge(d_sum, k0 + 3)
                dve.scalar_tensor_tensor(sums[:, 2, :], eb[:, 3, :], 1.0, sums[:, 1, :], ALU.add, ALU.mult
                                         ).then_inc(d_sum, 1)
                dve.wait_ge(d_sum, k0 + 4)
                dve.reciprocal(sums[:, 3, :], sums[:, 2, :]).then_inc(d_sum, 1)
                dve.wait_ge(d_sum, k0 + 5)
                dve.scalar_tensor_tensor(sums[:, 4, :], sums[:, 0, :], float(DH) ** -0.5, sums[:, 3, :],
                                         ALU.mult, ALU.mult).then_inc(d_sum, 1)
                dve.wait_ge(d_sum, k0 + 6)
                dve.tensor_tensor(sums[:, 5, :], sums[:, 4, :], eb[:, 2, :], ALU.mult).then_inc(d_sum, 1)

            def weighted(t, b, q):
                k0 = DS * t
                dve.wait_ge(d_sum, k0 + 7)
                dve.wait_ge(d_v, t + 1)
                after(dve, d_vT, 2 * t)
                for k in range(2):
                    n = NH // 2
                    dve.tensor_tensor(vc[:, k * 512:(k + 1) * 512].rearrange("p (h d) -> p h d", h=n),
                                      bank[:, 4 + k, :].rearrange("p (h d) -> p h d", h=n),
                                      sums[:, 5, k * n:(k + 1) * n].unsqueeze(2).to_broadcast([P, n, DH]),
                                      ALU.mult).then_inc(d_sum, 1)

            def measure4(t, b, q):
                dve.wait_ge(d_o, t + 1)
                ln_measure(dve, ln4, attn1, t, b)

            def scale4(t, b, q):
                after(dve, d_y, 3 * (t - 2) + 1)
                ln_scale(dve, ln4, attn1, t, b)

            def measure5(t, b, q):
                dve.wait_ge(d_y, 3 * t + 3)
                ln_measure(dve, ln5, xt(t), t, b)

            def norm5(t, b, q):
                wait_rows_sent(dve, router1, t, b)
                ln_scale(dve, ln5, xt(t), t, b)

            run_tiles(dve, NT, 4, [
                (5, norm5), (1, combine(0, d_g, d_x)), (1, lambda t, b, q: ln_measure(dve, ln3, xt(t), t, b)),
                (4, measure5), (2, feature(0)), (1, lambda t, b, q: ln_scale(dve, ln3, xt(t), t, b)),
                (2, feature(1)), (2, feature_sums),
                (5, lambda t, b, q: dve_pick(dve, router1, t, b, q)), (2, coefficients),
                (5, lambda t, b, q: dve_place(dve, router1, t, b, q)), (2, weighted), (3, measure4), (3, scale4)])
            slot_table(1)

            def shared(t, b, q):
                for c, (a, m) in enumerate(SC):
                    dve.wait_ge(f_h, 2 * (len(SC) * t + c) + 2)
                    dve.wait_ge(f_a, len(SC) * t + c + 1)
                    after(dve, f_o, t)
                    dve.scalar_tensor_tensor(shT[len(SC) + c][0:m, :], bank[0:m, 3 + c, :], sb13[0:m, 1, c:c + 1],
                                             shT[c][0:m, :], ALU.add, ALU.mult).then_inc(f_g, 1)
                dve.wait_ge(f_o, t + 1)
                xi = xres[:, bass.ds(t * 512, 512)]
                dve.tensor_tensor(xi, xi, bank[:, 6, :], ALU.add).then_inc(f_x, 1)

            run_tiles(dve, T // 512, 1, [(0, shared)])

            def gated(t, b, q):
                dve.wait_ge(e_silu, t + 1)
                dve.tensor_tensor(act1[b % 2], act1[b % 2], hb[b % 2][:, H1:2 * H1], ALU.mult).then_inc(e_act, 1)

            dve.wait_ge(ld_w1, 96)
            link(dve.tensor_tensor(b2B[:, :].rearrange("p (e d) -> p e d", e=E), b2B[:, :].rearrange("p (e d) -> p e d", e=E),
                                   gB[:, 1, 1, :].unsqueeze(1).to_broadcast([P, E, D]), ALU.mult))
            run_tiles(dve, SLOTS, NB, [(1, biased(1, 2 * H1)), (2, gated), (4, result(1))])

            run_tiles(dve, NT, 4, [(0, combine(1, g_g, g_x))])

        @block.tensor
        def _(pe):
            pe.wait_ge(s_mod_used, 1)
            pe.wait_ge(ld_c, 48)
            for l in range(2):
                for k in range(2):
                    pe.matmul(bank[:, 2 * l + k, 0:D], siluB[:, l, :], wmod[:, l, (3 * k + 2) * D:(3 * k + 3) * D],
                              start=True, stop=True)
                    for i in range(2):
                        c = 8 * l + 2 * k + i
                        last = pe.matmul(bank[:, 4, c:c + 1], wmod[:, l, (3 * k + i) * D:(3 * k + i + 1) * D],
                                         sc[:, 3, l:l + 1], start=True, stop=True)
            last.then_inc(s_mod, 1)
            pe.wait_ge(s_mod_ready, 1)
            pe.wait_ge(s_consts, 3)
            pe.wait_ge(ld_attn, 48)

            def turn(t, b, q):
                pe.wait_ge(ln1["normed"], t + 1)
                after(pe, a_h, t - 1)
                pe.transpose(bank[:, b, 0:P], ln1["xn"][b], ident[:, :]).then_inc(a_xT, 1)

            def keys_values(t, b, q):
                pe.wait_ge(a_h, t + 1)
                pe.wait_ge(a_win, t + 1)
                after(pe, a_k, t - 1)
                after(pe, a_v, t - 1)
                pe.matmul(bank[:, 2 + b, 0:P], Wa[:, 1, :], hT[:, bass.ds(t * P + BAND, P)], start=True, stop=True)
                pe.matmul(bank[:, 4 + b, 0:D], hwin[:, b, :], Wa[:, 2, :], start=True, stop=True).then_inc(a_kv, 1)

            run_tiles(pe, NT, 2, [(3, keys_values), (1, turn)])
            pe.wait_ge(a_win, NT + 1)
            pe.wait_ge(a_v, NT - 1)
            pe.matmul(bank[0:2 * BAND, 4, 0:D], hwin[:, 0, 0:2 * BAND], Wa[:, 2, :], start=True, stop=True).then_inc(a_kv, 1)
            pe.wait_ge(a_hs, 2)
            pe.matmul(bank[:, 6, 0:D], hsumB[:, :], Wa[:, 2, :], start=True, stop=True).then_inc(a_vt, 1)
            pe.wait_ge(a_vtc, 1)
            pe.wait_ge(a_k, NT)
            pe.wait_ge(a_v, NT + 1)
            pe.wait_ge(ld_router, 64)

            def query(t, b, q):
                after(pe, b_qT, t - 1)
                pe.matmul(bank[:, ends[b % 2], 0:P], Wa[:, 0, :], hT[:, bass.ds(t * P + BAND, P)],
                          start=True, stop=True).then_inc(b_q, 1)

            def score(t, b, q):
                pe.wait_ge(b_qT, t + 1)
                after(pe, b_sm, t - 1)
                pe.matmul(bank[:, 1 + b % 2, 0:WIN], qT[:, b % 2, :], kT[:, bass.ds(t * P, WIN)],
                          start=True, stop=True).then_inc(b_s, 1)

            def turn_probs(t, b, q):
                pe.wait_ge(b_pp, 3 * t + 1)
                after(pe, b_pTc, 2 * t)
                pe.transpose(bank[:, 3, 0:P], pr[:, b % 2, 0:P], ident[:, :])
                pe.transpose(bank[0:2 * BAND, 3, P:2 * P], pr[:, b % 2, P:WIN],
                             ident[:, :]).then_inc(b_pT, 1)

            def attend(t, b, q):
                pe.wait_ge(b_pTc, 2 * t + 2)
                after(pe, b_ao, t)
                o = bank[:, 4, 0:D]
                pe.matmul(o, pT[:, b % 2, 0:P], V[:, bass.ds(t * D, D)], start=True, stop=False)
                pe.matmul(o, pT[0:2 * BAND, b % 2, P:2 * P], V[0:2 * BAND, bass.ds(t * D + D, D)],
                          start=False, stop=True).then_inc(b_o, 1)

            run_tiles(pe, NT, 4, [(1, score), (0, query), (3, attend),
                                  (4, lambda t, b, q: pe_transpose(pe, router0, t, b)), (2, turn_probs),
                                  (4, lambda t, b, q: pe_logits(pe, router0, t, b)),
                                  (4, lambda t, b, q: pe_rank(pe, router0, t, b, q))])

            def slot_counts(l):
                r = routers[l]
                pe.wait_ge(r["placed"], RANK * (NT // 2))
                pe.matmul(bank[0:E, 0, 0:P], macc[:, l, 0, :], ones[:, :], start=True, stop=False)
                pe.matmul(bank[0:E, 0, 0:P], macc[:, l, 1, :], ones[:, :], start=False, stop=True).then_inc(t_cnt, 1)
                pe.wait_ge(t_dve, 11 * l + 3)
                pe.matmul(bank[:, 1, 0:E], tiles_per[:, :], upto[:, :], start=True, stop=True).then_inc(t_cum, 1)
                pe.wait_ge(t_dve, 11 * l + 11)
                for k in range(2):
                    pe.matmul(bank[0:1, 2, k * P:(k + 1) * P], slot_vals[:, k:k + 1], ident[:, :], start=True, stop=True)
                pe.matmul(bank[0:1, 2, 2 * P:2 * P + E], ones[:, 0:1], macc[:, l, 0, :], start=True, stop=False)
                pe.matmul(bank[0:1, 2, 2 * P:2 * P + E], ones[:, 0:1], macc[:, l, 1, :], start=False, stop=True
                          ).then_inc(t_val, 1)
                pe.wait_ge(t_ready, l + 1)

            slot_counts(0)

            def expert_of(t):
                return pe.value_load(tbl[0:1, bass.ds(t + P, 1)], min_val=0, max_val=E - 1)

            def slot_turn(l):
                def stage(t, b, q):
                    pe.wait_ge(e_x[b], 16 * (l * (SLOTS // NB) + q + 1))
                    after(pe, e_xTc, l * SLOTS + t - 1)
                    pe.transpose(bank[:, ends[b % 2], 0:P], xg[b][:, 0:D], ident[:, :]).then_inc(e_xT, 1)
                return stage

            def slot_hidden(l, w, width):
                def stage(t, b, q):
                    e = expert_of(t)
                    pe.wait_ge(e_xTc, l * SLOTS + t + 1)
                    after(pe, e_hb, l * SLOTS + t - 1)
                    pe.matmul(bank[:, 1 + b % 2, 0:width], xgT[b % 2], w[:, bass.ds(e * width, width)],
                              start=True, stop=True).then_inc(e_h, 1)
                return stage

            def slot_turn_hidden(t, b, q):
                pe.wait_ge(e_hb, t + 1)
                after(pe, e_hTc, t - 1)
                for c in range(C0):
                    last = pe.transpose(bank[:, 3 + b % 2, c * P:(c + 1) * P], hb[b % 2][:, c * P:(c + 1) * P], ident[:, :])
                last.then_inc(e_hT, 1)

            def slot_out(t, b, q):
                e = expert_of(t)
                pe.wait_ge(e_hTc, t + 1)
                after(pe, e_yo, t - 1)
                for c in range(C0):
                    last = pe.matmul(bank[:, 5 + b % 2, 0:D], hbT[b % 2][:, c * P:(c + 1) * P],
                                     W2s[:, bass.ds(e * H0 + c * D, D)], start=(c == 0), stop=(c == C0 - 1))
                last.then_inc(e_o, 1)

            pe.wait_ge(ld_w0, 64)
            pe.wait_ge(w2_scaled, E)
            run_tiles(pe, SLOTS, NB, [(1, slot_hidden(0, W1s, H0)), (2, slot_turn_hidden), (3, slot_out),
                                      (0, slot_turn(0))])
            pe.wait_ge(e_yo, SLOTS)

            pe.wait_ge(ld_l1, 16 * (4 + 2 * (1 + len(SC)) + len(SC) + 1))

            def turn1(t, b, q):
                pe.wait_ge(ln3["normed"], t + 1)
                after(pe, d_h, t)
                after(pe, d_eb, 3 * t)
                pe.transpose(turned1, ln3["xn"][b], ident[:, :]).then_inc(d_xT, 1)

            def project(k, s):
                def stage(t, b, q):
                    pe.wait_ge(d_h, t + 1)
                    after(pe, d_f, 2 * (t - 1) + k + 1) if k < 2 else after(pe, d_vTc, 2 * t)
                    for i in range(2):
                        last = pe.matmul(bank[:, 2 * k + i, :], h3T[b], Wqkvb[:, k * HD + i * 512:k * HD + (i + 1) * 512],
                                         start=True, stop=True)
                    last.then_inc(s, 1)
                return stage

            def project_beta(t, b, q):
                pe.matmul(beta, h3T[b], Wqkvb[:, 3 * HD:3 * HD + NH], start=True, stop=True).then_inc(d_b, 1)

            def turn_values(t, b, q):
                pe.wait_ge(d_sum, DS * (t + 1))
                for k in range(2):
                    for c in range(4):
                        last = pe.transpose(bank[:, 4 + k, c * P:(c + 1) * P], vc[:, (4 * k + c) * P:(4 * k + c + 1) * P],
                                            ident[:, :])
                    last.then_inc(d_vT, 1)

            def attn_out(t, b, q):
                pe.wait_ge(d_vTc, 2 * t + 2)
                if b % 2 == 1 and not (isinstance(t, int) and t < 3):
                    pe.wait_ge(router1["placed"], RANK * (2 * q + (b - 3) // 2) + 1)
                pe.matmul(attn1, h3T[b], ident[:, :], start=True, stop=False)
                for c in range(HD // P):
                    last = pe.matmul(attn1, vT[:, c * P:(c + 1) * P], Wo[:, c, :],
                                     start=False, stop=(c == HD // P - 1))
                last.then_inc(d_o, 1)

            run_tiles(pe, NT, 4, [(3, turn_values), (2, project(0, d_q)),
                                  (5, lambda t, b, q: pe_transpose(pe, router1, t, b)), (2, project(1, d_k)),
                                  (2, project_beta), (5, lambda t, b, q: pe_logits(pe, router1, t, b)), (1, turn1),
                                  (2, project(2, d_v)), (5, lambda t, b, q: pe_rank(pe, router1, t, b, q)),
                                  (3, attn_out)])
            slot_counts(1)

            pe.wait_ge(f_in, NT)

            def shared_hidden(t, b, q):
                for c, (a, m) in enumerate(SC):
                    after(pe, f_g, len(SC) * t)
                    for k in range(2):
                        pe.matmul(bank[0:m, 3 * k + c, :], sw13[:, k, a:a + m], hT[:, bass.ds(t * 512, 512)],
                                  start=True, stop=True).then_inc(f_h, 1)

            def shared_out(t, b, q):
                pe.wait_ge(f_g, len(SC) * (t + 1))
                after(pe, f_x, t)
                for i in range(4):
                    o = bank[:, 6, i * D:(i + 1) * D]
                    pe.matmul(o, onerow[:, :], sb2r[:, :], start=True, stop=False)
                    for c, (a, m) in enumerate(SC):
                        last = pe.matmul(o, shT[len(SC) + c][0:m, i * P:(i + 1) * P], sw2s[0:m, c, :],
                                         start=False, stop=(c == len(SC) - 1))
                last.then_inc(f_o, 1)

            run_tiles(pe, T // 512, 1, [(0, shared_hidden), (0, shared_out)])
            pe.wait_ge(f_x, T // 512)

            def slot_turn_act(t, b, q):
                pe.wait_ge(e_act, t + 1)
                after(pe, e_hTc, SLOTS + t - 1)
                for c in range(2):
                    last = pe.transpose(bank[0:K1, 3 + b % 2, c * P:(c + 1) * P], act1[b % 2][:, c * K1:(c + 1) * K1],
                                        ident[:, :])
                last.then_inc(e_hT, 1)

            def slot_out1(t, b, q):
                e = expert_of(t)
                pe.wait_ge(e_hTc, SLOTS + t + 1)
                after(pe, e_yo, SLOTS + t - 1)
                for c in range(2):
                    last = pe.matmul(bank[:, 5 + b % 2, 0:D], hbT[b % 2][0:K1, c * P:(c + 1) * P],
                                     w2s[:, bass.ds(e * 2 * D + c * D, D)], start=(c == 0), stop=(c == 1))
                last.then_inc(e_o, 1)

            pe.wait_ge(ld_w1, 96)
            pe.wait_ge(w2_scaled, E + 1)
            run_tiles(pe, SLOTS, NB, [(1, slot_hidden(1, w13s, 2 * H1)), (3, slot_turn_act), (4, slot_out1),
                                      (0, slot_turn(1))])


def kernel(**inputs):
    import numpy as np
    import concourse.bacc as bacc
    from concourse.bass_utils import run_bass_kernel_spmd

    a = {k: np.ascontiguousarray(v) for k, v in inputs.items()}
    T, D = a["L0_attn_inputs"].shape[1:]
    NH, DH = 16, 64
    qkvb = a["L1_attn_W_qkvb"].reshape(NH, 3 * DH + 1, D)
    blocks = [qkvb[:, k * DH:(k + 1) * DH].reshape(NH * DH, D) for k in range(3)] + [qkvb[:, 3 * DH]]
    f = "L1_ffn_"
    arrays = {
        "x": a["L0_attn_inputs"].reshape(T, D), "WQ": a["L0_attn_WQ"], "WK": a["L0_attn_WK"], "WV": a["L0_attn_WV"],
        "Wr0": a["L0_ffn_Wr"], "br0": a["L0_ffn_br"], "W1": a["L0_ffn_W1"], "b1": a["L0_ffn_b1"],
        "W2": a["L0_ffn_W2"], "b2": a["L0_ffn_b2"],
        "c01": np.stack([a["L0_c"].reshape(D), a["L1_c"].reshape(D)], axis=1),
        "wmod0": a["L0_wmod"], "wmod1": a["L1_wmod"],
        "WqkvbT": np.concatenate(blocks, axis=0).T, "WoT": a["L1_attn_W_o"].T,
        "ln_g": a["L1_attn_ln_g"], "ln_b": a["L1_attn_ln_b"],
        "Wr1": a[f + "gate_w"], "br1": a[f + "gate_b"], "w1": a[f + "w1"], "b1e": a[f + "b1"],
        "w3": a[f + "w3"], "b3e": a[f + "b3"], "w2": a[f + "w2"], "b2e": a[f + "b2"],
        "sw1": a[f + "sw1"], "sb1": a[f + "sb1"], "sw3": a[f + "sw3"], "sb3": a[f + "sb3"],
        "sw2": a[f + "sw2"], "sb2": a[f + "sb2"],
    }
    nc = bacc.Bacc("TRN2", target_bir_lowering=False, num_devices=1)
    feed, args = {}, {}
    for name, v in arrays.items():
        v = np.ascontiguousarray(v)
        feed[f"in_{name}"] = v
        args[name] = nc.dram_tensor(f"in_{name}", v.shape, mybir.dt.from_np(v.dtype), kind="ExternalInput").ap()
    args["out"] = nc.dram_tensor("out_x", (T, D), F32, kind="ExternalOutput").ap()
    build(nc, **args)
    r = run_bass_kernel_spmd(nc, [feed], core_ids=[0])
    return r.results[0]["out_x"].reshape(1, T, D)
```

```python
from contextlib import ExitStack

import concourse.bass as bass
from concourse import mybir

ALU = mybir.AluOpType
ACT = mybir.ActivationFunctionType
AX_X = mybir.AxisListType.X
F32 = mybir.dt.float32
BF16 = mybir.dt.bfloat16
I32 = mybir.dt.int32
U32 = mybir.dt.uint32

P = 128
EPS = 1e-5


def after(eng, sem, n):
    if isinstance(n, int) and n <= 0:
        return
    eng.wait_ge(sem, n)


def settle(eng, passed):
    eng.sem_inc(passed, 1)


def run_tiles(eng, n, unroll, work):
    deepest = max(lag for lag, _ in work)
    head = (-(-deepest // unroll) + 1) * unroll
    for s in range(head):
        for lag, stage in work:
            if 0 <= s - lag:
                stage(s - lag, (s - lag) % unroll, (s - lag) // unroll)
    with eng.Fori(head // unroll, n // unroll) as j:
        for u in range(unroll):
            for lag, stage in work:
                stage(unroll * j + (u - lag), (u - lag) % unroll, j + (u - lag) // unroll)
    for s in range(n, n + deepest):
        for lag, stage in work:
            if s - lag < n:
                stage(s - lag, (s - lag) % unroll, (s - lag) // unroll)


def run_slots(eng, n, unroll, work, look_up, begin=None):
    deepest = max(lag for lag, _ in work)
    head = (-(-deepest // unroll) + 1) * unroll
    entries = {}
    for s in range(head):
        if s % unroll == 0:
            first = max(s - deepest, 0)
            entries = dict(enumerate(look_up(first, s + unroll - first), start=first))
            if begin and s == 0:
                begin()
        for lag, stage in work:
            if 0 <= s - lag:
                stage(s - lag, (s - lag) % unroll, (s - lag) // unroll, entries[s - lag])
    with eng.Fori(head // unroll, n // unroll) as j:
        entries = look_up(unroll * j - deepest, unroll + deepest)
        for u in range(unroll):
            for lag, stage in work:
                stage(unroll * j + (u - lag), (u - lag) % unroll, j + (u - lag) // unroll, entries[u - lag + deepest])
    if deepest:
        entries = dict(enumerate(look_up(n - deepest, deepest), start=n - deepest))
    for s in range(n, n + deepest):
        for lag, stage in work:
            if s - lag < n:
                stage(s - lag, (s - lag) % unroll, (s - lag) // unroll, entries[s - lag])


def build(nc, x, WQ, WK, WV, Wr0, br0, W1, b1, W2, b2, c01, wmod0, wmod1,
          WqkvbT, WoT, ln_g, ln_b, Wr1, br1, w1, b1e, w3, b3e, w2, b2e,
          sw1, sb1, sw3, sb3, sw2, sb2, out):
    T, D = x.shape
    NT = T // P
    E = Wr0.shape[1]
    H0 = W1.shape[2]
    C0 = H0 // P
    H1 = w1.shape[2]
    K1 = H1 // 2
    HS = sw1.shape[1]
    SC = [(a, min(P, HS - a)) for a in range(0, HS, P)]
    NH = 16
    DH = (WqkvbT.shape[1] - NH) // (3 * NH)
    HD = NH * DH
    BAND = 32
    WIN = P + 2 * BAND
    PADT = T + 2 * BAND
    TOPK = 2
    NB = 8
    SLOTS = -(-(TOPK * T // P + E - 1) // NB) * NB
    REGION = T + P
    SPARE = SLOTS - TOPK * T // P
    DUMMY = E * REGION
    ROWS = DUMMY + SPARE * P
    RW = D + 1
    NOWHERE = 1 << 20
    assert D == P and T % (2 * P) == 0 and SLOTS <= P

    xs = [nc.dram_tensor(f"sorted_tokens_{l}", [ROWS, RW], F32, kind="Internal").ap() for l in range(2)]
    ys = [nc.dram_tensor(f"results_{l}", [TOPK * T, D], F32, kind="Internal").ap() for l in range(2)]

    with ExitStack() as ctx:
        def sb(name, shape, dt=F32):
            return ctx.enter_context(nc.sbuf_tensor(name, shape, dt))

        def sem(name):
            return ctx.enter_context(nc.semaphore(name))

        bank = ctx.enter_context(nc.psum_tensor("bank", [P, 8, 512], F32))

        xres = sb("xres", [P, NT * D])
        hT = sb("hT", [P, PADT])
        big = sb("big", [P, 2 * E * H0])
        W1s = big[:, 0:E * H0]
        W2s = big[:, E * H0:2 * E * H0]
        o13, o2, ob = 0, 2 * E * H1, 2 * E * H1 + 2 * E * D
        w13s = big[:, o13:o13 + 2 * E * H1]
        w2s = big[0:K1, o2:o2 + 2 * E * D]
        bias_big = sb("bias_big", [P, E * H0])
        b2B = sb("b2B", [P, E * D])
        Wa = sb("Wa", [P, 3, D])
        Wqkvb = sb("Wqkvb", [P, 3 * HD + NH])
        Wo = sb("Wo", [P, HD // P, D])
        Wr = sb("Wr", [P, 2, E])
        brB = sb("brB", [P, 2, E])
        sw13 = sb("sw13", [P, 2, HS])
        sw2s = sb("sw2s", [P, len(SC), D])
        sb13 = sb("sb13", [P, 2, len(SC)])
        sb2r = sb("sb2r", [1, D])
        lnB = sb("lnB", [P, 2, D])
        cT = sb("cT", [P, 2])

        ident = sb("ident", [P, P])
        band = sb("band", [P, WIN])
        before = sb("before", [P, P], BF16)
        ones = sb("ones", [P, P], BF16)
        onerow = sb("onerow", [1, P])
        zeros = sb("zeros", [P, RW])
        result_row = sb("result_row", [P, NT, TOPK], I32)
        expert_id = sb("expert_id", [P, E])
        region_at = sb("region_at", [P, E])
        upto = sb("upto", [E, E])
        slot_id = sb("slot_id", [P, 1])
        eps = sb("eps", [P, 1])

        sc = sb("sc", [P, 6, 2])
        mcol = sb("mcol", [P, 2, 4])
        gB = sb("gB", [P, 2, 2, D])
        lnG = sb("lnG", [P, 2, D])

        hsum = sb("hsum", [P, NT])
        vtot = sb("vtot", [P, D])
        ao = sb("ao", [P, D])
        st6 = sb("st6", [P, 6, 4])
        gates = sb("gates", [P, 2, NT, 2])
        rows = sb("rows", [P, 4, TOPK, RW])
        macc = sb("macc", [P, 2, 2, E], BF16)
        slot_vals = sb("slot_vals", [P, 2])
        tbl = sb("tbl", [1, 2 * P], I32)
        counts = sb("counts", [1, E], I32)
        tiles_per = sb("tiles_per", [E, P])
        tiles_int = sb("tiles_int", [E, 2, P], I32)
        cumt = sb("cumt", [P, 3, E])
        sl = sb("sl", [P, 3])
        sums = sb("sums", [P, 6, NH])
        qk_sums = sb("qk_sums", [P, 2, NH])
        eb = sb("eb", [P, 4, NH])

        work = sb("work", [P, 7168])
        wmod = work[:, 4352:4352 + 12 * D].rearrange("p (l n) -> p l n", l=2)
        kT = work[:, 0:PADT]
        V = work[:, PADT:PADT + (NT + 1) * D]
        siluB = work[:, 5888:5888 + 2 * P].rearrange("p (l n) -> p l n", l=2)
        gtmp = work[:, 4352:4352 + 12 * D].rearrange("p (k c n) -> p k c n", k=3, c=4)
        hwin = work[:, 4352:4352 + 2 * P].rearrange("p (b n) -> p b n", b=2)
        qT = work[:, 4608:4608 + 2 * P].rearrange("p (b n) -> p b n", b=2)
        sm = work[:, 4864:4864 + 2 * WIN].rearrange("p (b n) -> p b n", b=2)
        pr = work[:, 5248:5248 + 2 * WIN].rearrange("p (b n) -> p b n", b=2)
        pT = work[:, 5632:5632 + 4 * P].rearrange("p (b n) -> p b n", b=2)
        hsumB = work[:, 6528:6528 + P]
        free = ob + 12 * D
        ef = (work[:, 0:2 * HD], big[:, free:free + 2 * HD])
        rf = (work[:, 2 * HD:4 * HD], big[:, free + 2 * HD:free + 4 * HD])
        vc = work[:, 4 * HD:5 * HD]
        vT = work[:, 5 * HD:6 * HD]
        h3T = [work[:, 6 * HD + P * b:6 * HD + P * b + P] for b in range(4)]
        yg = [big[:, ob + 2 * D * b:ob + 2 * D * (b + 1)] for b in range(4)]
        y_all = big[:, 0:2 * NT * D]
        ya = [big[:, ob + 8 * D + D * b:ob + 8 * D + D * (b + 1)] for b in range(4)]
        xg = [work[:, RW * b:RW * b + RW] for b in range(NB)]
        yo = [work[:, 1040 + D * b:1040 + D * b + D] for b in range(NB)]
        xgT = [work[:, 2064 + P * b:2064 + P * b + P] for b in range(2)]
        hb = [work[:, 2320 + H0 * b:2320 + H0 * (b + 1)] for b in range(2)]
        hbT = [work[:, 3344 + H0 * b:3344 + H0 * (b + 1)] for b in range(2)]
        act1 = [work[:, 4368 + 176 * b:4368 + 176 * b + H1] for b in range(2)]
        shT = [(work[:, 5120 + 512 * c:5120 + 512 * (c + 1)] if c < 4 else
                big[:, ob + 512 * c:ob + 512 * (c + 1)]) for c in range(2 * len(SC))]

        s_consts = sem("constants_made")
        passed = sem("passed")
        ld_silu = sem("ld_silu")
        ld_x, ld_c, ld_attn, ld_router = sem("ld_x"), sem("ld_c"), sem("ld_attn"), sem("ld_router")
        ld_w0, ld_w1, ld_l1 = sem("ld_experts0"), sem("ld_experts1"), sem("ld_layer1")
        s_silu_act, s_silu = sem("silu_exp"), sem("silu_steps")
        s_mod, s_mod_used, s_mod_ready = sem("mod_products"), sem("mod_used"), sem("mod_ready")

        def layer_norm(name, xn=None):
            if xn is None:
                own = sb(name + "_xn", [P, 2, D])
                xn = [own[:, b % 2, :] for b in range(4)]
            return {
                "stats": sb(name + "_stats", [P, 2, 6]),
                "mv": sb(name + "_mv", [P, 4, 2]),
                "r": sb(name + "_r", [P, 4, 2]),
                "xn": xn,
                "moments": sem(name + "_moments"),
                "rstd": sem(name + "_rstd"),
                "normed": sem(name + "_normed"),
            }

        def ln_stats(dve, n, src, t, b):
            settle(dve, passed)
            dve.bn_stats(n["stats"][:, b % 2, :], src).then_inc(n["moments"], 1)

        def ln_moments(dve, n, t, b):
            dve.wait_ge(n["moments"], 2 * t + 1)
            settle(dve, passed)
            dve.bn_aggr(n["mv"][:, b, :], n["stats"][:, b % 2, :]).then_inc(n["moments"], 1)

        def ln_deviation(act, n, t, b):
            act.wait_ge(n["moments"], 2 * t + 2)
            act.activation(n["r"][:, b, 0:1], n["mv"][:, b, 1:2], ACT.Ln, bias=eps[:, :]).then_inc(n["rstd"], 1)
            act.wait_ge(n["rstd"], 2 * t + 1)
            act.activation(n["r"][:, b, 1:2], n["r"][:, b, 0:1], ACT.Exp, scale=-0.5).then_inc(n["rstd"], 1)

        def ln_scale(dve, n, src, t, b):
            dve.wait_ge(n["rstd"], 2 * t + 2)
            dve.tensor_scalar(n["xn"][b], src, n["mv"][:, b, 0:1], n["r"][:, b, 1:2],
                              ALU.subtract, ALU.mult).then_inc(n["normed"], 1)

        PICK, RANK, GATE = 10, 4, 4

        def router(layer, ln, scale_shift, logits_ps, rank_ps, xT_ps):
            n = f"router{layer}_"
            return {
                "layer": layer, "ln": ln, "ss": scale_shift,
                "logits_ps": logits_ps, "rank_ps": rank_ps, "xT_ps": xT_ps,
                "hb": sb(n + "hT", [P, 2, P]),
                "lg": sb(n + "lg", [P, 2, 2, E]),
                "top": sb(n + "top", [P, 2, 2, 8]),
                "ti": sb(n + "ti", [P, 2, 2, 8], U32),
                "tf": sb(n + "tf", [P, 2, 2, 2]),
                "hot": sb(n + "hot", [P, 2, 2, 2, E]),
                "pick": sb(n + "pick", [P, 2, 2, E], BF16),
                "dx": sb(n + "dx", [P, 2, 2 * E + 4]),
                "ex": sb(n + "ex", [P, 2, 2 * E + 4]),
                "se": sb(n + "se", [P, 2, 2, 2]),
                "rk": sb(n + "rk", [P, 2, 2, E]),
                "sel": sb(n + "sel", [P, 2, 2, 2, E]),
                "pf": sb(n + "pf", [P, 2, 4]),
                "at": sb(n + "at", [P, 2, 4], I32),
                "xT": sem(n + "xT"),
                "h": sem(n + "h"),
                "logits": sem(n + "logits"),
                "picked": sem(n + "picked"),
                "exps": sem(n + "exps"),
                "rank": sem(n + "rank"),
                "placed": sem(n + "placed"),
                "gated": sem(n + "gated"),
                "doubled": sem(n + "doubled"),
                "sent": [sem(n + f"sent{h}") for h in range(2)],
            }

        def wait_rows_sent(eng, r, t, b):
            if not (isinstance(t, int) and t < 4):
                eng.wait_ge(r["sent"][b // 2], 16 * (t - b))

        def pe_transpose(pe, r, t, b):
            pe.wait_ge(r["ln"]["normed"], t + 1)
            after(pe, r["h"], t)
            pe.transpose(r["xT_ps"], r["ln"]["xn"][b], ident[:, :]).then_inc(r["xT"], 1)

        def act_modulate(act, r, t, b):
            act.wait_ge(r["xT"], t + 1)
            after(act, r["logits"], t - 1)
            act.activation(r["hb"][:, b % 2, :], r["xT_ps"], ACT.Identity,
                           bias=r["ss"][0], scale=r["ss"][1]).then_inc(r["h"], 1)

        def pe_logits(pe, r, t, b):
            pe.wait_ge(r["h"], t + 1)
            pe.matmul(r["logits_ps"][:, b % 2, :], r["hb"][:, b % 2, :], Wr[:, r["layer"], :],
                      start=True, stop=True).then_inc(r["logits"], 1)

        def pick_parts(dve, r):
            def add_bias(t, h, g, k):
                dve.wait_ge(r["logits"], t + 1)
                dve.tensor_tensor(r["lg"][:, h, :, :], r["logits_ps"],
                                  brB[:, r["layer"], :].unsqueeze(1).to_broadcast([P, 2, E]),
                                  ALU.add).then_inc(r["picked"], 1)

            def largest(t, h, g, k):
                dve.wait_ge(r["picked"], k + 1)
                settle(dve, passed)
                for i in range(2):
                    dve.max(r["top"][:, h, i, :], r["lg"][:, h, i, :]).then_inc(r["picked"], 1)

            def indices(t, h, g, k):
                lg, top, dx = r["lg"][:, h, :, :], r["top"][:, h, :, :], r["dx"][:, h, :]
                dve.wait_ge(r["picked"], k + 3)
                settle(dve, passed)
                for i in range(2):
                    dve.max_index(r["ti"][:, h, i, :], top[:, i, :], lg[:, i, :]).then_inc(r["picked"], 1)
                after(dve, r["exps"], g - 1)
                dve.tensor_tensor(dx[:, 0:2 * E].rearrange("p (i e) -> p i e", i=2), lg,
                                  top[:, :, 0:1].to_broadcast([P, 2, E]), ALU.subtract).then_inc(r["picked"], 1)
                dve.tensor_tensor(dx[:, 2 * E:2 * E + 4].rearrange("p (i k) -> p i k", i=2), top[:, :, 0:2],
                                  top[:, :, 0:1].to_broadcast([P, 2, 2]), ALU.subtract).then_inc(r["picked"], 1)

            def as_float(t, h, g, k):
                dve.wait_ge(r["picked"], k + 5)
                dve.tensor_scalar(r["tf"][:, h, :, :], r["ti"][:, h, :, 0:2], 1.0, None, ALU.mult
                                  ).then_inc(r["picked"], 1)

            def one_hot(t, h, g, k):
                dve.wait_ge(r["picked"], k + 8)
                dve.tensor_tensor(r["hot"][:, h, :, :, :].rearrange("p i k e -> p (i k) e"),
                                  expert_id[:, :].unsqueeze(1).to_broadcast([P, 4, E]),
                                  r["tf"][:, h, :, :].rearrange("p i k -> p (i k)").unsqueeze(2)
                                  .to_broadcast([P, 4, E]), ALU.is_equal).then_inc(r["picked"], 1)

            def both(t, h, g, k):
                dve.wait_ge(r["picked"], k + 9)
                after(dve, r["rank"], g - 1)
                dve.tensor_tensor(r["pick"][:, h, :, :], r["hot"][:, h, :, 0, :], r["hot"][:, h, :, 1, :],
                                  ALU.add).then_inc(r["picked"], 1)

            return [of_group(part, PICK) for part in (add_bias, largest, indices, as_float, one_hot, both)]

        def of_group(part, steps):
            def stage(t, b, q):
                if b % 2:
                    part(t, b // 2, 2 * q + b // 2, steps * (2 * q + b // 2))
            return stage

        def act_exps(act, r, t, b, q):
            if b % 2 == 0:
                return
            h, g = b // 2, 2 * q + b // 2
            act.wait_ge(r["picked"], PICK * g + 7)
            after(act, r["gated"], GATE * (g - 1))
            act.activation(r["ex"][:, h, :], r["dx"][:, h, :], ACT.Exp).then_inc(r["exps"], 1)

        def pe_rank(pe, r, t, b, q):
            if b % 2 == 0:
                return
            h, g = b // 2, 2 * q + b // 2
            pe.wait_ge(r["picked"], PICK * (g + 1))
            after(pe, r["placed"], RANK * (g - 1) + 2)
            for i in range(2):
                o = r["rank_ps"][:, i, :]
                pe.matmul(o, before[:, :], r["pick"][:, h, i, :], start=True, stop=False)
                if i:
                    pe.matmul(o, ones[:, :], r["pick"][:, h, 0, :], start=False, stop=False)
                pe.matmul(o, ones[:, :], macc[:, r["layer"], 0, :], start=False, stop=False)
                last = pe.matmul(o, ones[:, :], macc[:, r["layer"], 1, :], start=False, stop=True)
            last.then_inc(r["rank"], 1)

        def place_parts(dve, r):
            def by_expert(t, h, g, k):
                dve.wait_ge(r["rank"], g + 1)
                dve.tensor_tensor(r["rk"][:, h, :, :], r["rank_ps"],
                                  region_at[:, :].unsqueeze(1).to_broadcast([P, 2, E]),
                                  ALU.add).then_inc(r["placed"], 1)
                dve.tensor_tensor(macc[:, r["layer"], :, :], macc[:, r["layer"], :, :], r["pick"][:, h, :, :],
                                  ALU.add).then_inc(r["placed"], 1)

            def chosen(t, h, g, k):
                dve.wait_ge(r["placed"], k + 1)
                dve.tensor_tensor(r["sel"][:, h, :, :, :], r["hot"][:, h, :, :, :],
                                  r["rk"][:, h, :, :].unsqueeze(2).to_broadcast([P, 2, 2, E]),
                                  ALU.mult).then_inc(r["placed"], 1)
                dve.wait_ge(r["exps"], g + 1)
                dve.reduce_sum(r["se"][:, h, 0, :], r["ex"][:, h, 0:2 * E].rearrange("p (i e) -> p i e", i=2),
                               AX_X).then_inc(r["gated"], 1)

            def summed(t, h, g, k):
                dve.wait_ge(r["placed"], k + 3)
                dve.reduce_sum(r["pf"][:, h, :], r["sel"][:, h, :, :, :].rearrange("p i k e -> p (i k) e"),
                               AX_X).then_inc(r["placed"], 1)
                dve.wait_ge(r["gated"], GATE * g + 1)
                dve.reciprocal(r["se"][:, h, 1, :], r["se"][:, h, 0, :]).then_inc(r["gated"], 1)

            def stored(t, h, g, k):
                if not (isinstance(t, int) and t < 4):
                    dve.wait_ge(r["sent"][h], 16 * (t - 1 - 2 * h))
                dve.wait_ge(r["placed"], k + 4)
                dve.tensor_scalar(r["at"][:, h, :], r["pf"][:, h, :], 1.0, None, ALU.mult).then_inc(r["gated"], 1)
                dve.wait_ge(r["gated"], GATE * g + 2)
                dve.tensor_tensor(gates[:, r["layer"], bass.ds(t - 1, 2), :],
                                  r["ex"][:, h, 2 * E:2 * E + 4].rearrange("p (i k) -> p i k", i=2),
                                  r["se"][:, h, 1, :].unsqueeze(2).to_broadcast([P, 2, 2]),
                                  ALU.mult).then_inc(r["gated"], 1)

            return [of_group(part, RANK) for part in (by_expert, chosen, summed, stored)]

        def pool_double(pool, r, t, b):
            if r["layer"] == 0:
                wait_rows_sent(pool, r, t, b)
            pool.wait_ge(r["ln"]["normed"], t + 1)
            settle(pool, passed)
            if r["layer"] == 0:
                pool.tensor_copy(rows[:, b, :, 0:D], r["ln"]["xn"][b].unsqueeze(1).to_broadcast([P, TOPK, D])
                                 ).then_inc(r["doubled"], 1)
            else:
                pool.tensor_copy(rows[:, b, 1, 0:D], rows[:, b, 0, 0:D]).then_inc(r["doubled"], 1)
            pool.tensor_copy(rows[:, b, :, D:RW].rearrange("p k a -> p (k a)").bitcast(I32),
                             result_row[:, bass.ds(t, 1), :].rearrange("p a k -> p (a k)")).then_inc(r["doubled"], 1)

        def pool_send(pool, r, t, b, q):
            if b % 2 == 0:
                return
            h, g = b // 2, 2 * q + b // 2
            pool.wait_ge(r["gated"], GATE * g + 3)
            pool.wait_ge(r["doubled"], 2 * t + 2)
            settle(pool, passed)
            for i in range(2):
                for k in range(TOPK):
                    c = 2 * i + k
                    pool.indirect_dma_start(xs[r["layer"]], bass.IndirectOffsetOnAxis(r["at"][:, h, c:c + 1], 0),
                                            rows[:, b - 1 + i, k, :], None).then_inc(r["sent"][h], 16)

        normed = sb("normed_tokens", [P, 4, D])
        own = {2: [normed[:, b, :] for b in range(4)], 5: [rows[:, b, 0, 0:D] for b in range(4)]}
        ln1, ln2, ln3, ln4, ln5 = (layer_norm(f"ln{k}", own.get(k)) for k in range(1, 6))
        stats1 = sb("ln1_all_stats", [P, NT, 6])
        mv1, r1 = sb("ln1_all_mv", [P, NT, 2]), sb("ln1_all_r", [P, 2, NT])
        small = [bank[:, 6, 2 * E * i:2 * E * (i + 1)].rearrange("p (i e) -> p i e", i=2) for i in range(2)]
        router0 = router(0, ln2, (mcol[:, 0, 2:3], mcol[:, 0, 3:4]), *small,
                         bank[:, 5, 0:P])
        router1 = router(1, ln5, (mcol[:, 1, 2:3], mcol[:, 1, 3:4]), *small,
                         bank[:, 6, P:2 * P])
        turned1, beta = bank[:, 7, 0:P], bank[:, 7, P:P + NH]
        attn1 = bank[:, 6, 2 * P:3 * P]
        ends = (0, 7)
        routers = [router0, router1]
        by_row, cumulated = bank[0:E, 7, 0:P], bank[:, 7, P:P + E]
        count_row, value_row = bank[0:1, 7, P + E:P + 2 * E], bank[0:1, 7, 2 * P:4 * P]

        a_mv, a_xT, a_h, a_win = sem("a_moments"), sem("a_xT"), sem("a_h"), sem("a_window")
        a_kv, a_k, a_v = sem("a_kv"), sem("a_k_copied"), sem("a_v_copied")
        a_hs, a_vt, a_vtc = sem("a_hsum"), sem("a_vtot"), sem("a_vtot_copied")
        b_q, b_qT, b_s, b_sm = sem("b_q"), sem("b_qT"), sem("b_scores"), sem("b_masked")
        b_nm, b_p, b_pp, b_pT, b_pTc = sem("b_negmax"), sem("b_exp"), sem("b_probs"), sem("b_pT"), sem("b_pTc")
        b_o, b_ao, b_x = sem("b_out"), sem("b_attended"), sem("b_x")
        t_cnt, t_dve, t_cum, t_val, t_ready = (sem("t_counts"), sem("t_dve"), sem("t_cumulated"),
                                               sem("t_values"), sem("t_ready"))
        t_counted = sem("t_counted")
        z_sent = sem("zero_rows_sent")
        e_x = [sem(f"e_x{b}") for b in range(NB)]
        e_y = [sem(f"e_y{b}") for b in range(NB)]
        e_xT, e_xTc, e_h, e_hb, e_hT, e_hTc, e_o, e_yo = (
            sem("e_xT"), sem("e_xTc"), sem("e_hidden"), sem("e_hb"), sem("e_hT"), sem("e_hTc"),
            sem("e_out"), sem("e_yo"))
        e_silu, e_act = sem("e_silu"), sem("e_act")
        d_x, d_gy = sem("d_x"), sem("d_gated_results")
        d_g = [sem(f"d_results{h}") for h in range(2)]
        w2_scaled, w2_low = sem("w2_scaled"), sem("w2_low_scaled")
        d_xT, d_h, d_q, d_k, d_v, d_b = sem("d_xT"), sem("d_h"), sem("d_q"), sem("d_k"), sem("d_v"), sem("d_beta")
        DS = 9
        d_eb = sem("d_exp_beta")
        d_e, d_f, d_qk, d_sum = sem("d_exp"), sem("d_feature"), sem("d_qk"), sem("d_sums")
        d_vT, d_vTc, d_o, d_y = sem("d_vT"), sem("d_vTc"), sem("d_out"), sem("d_y")
        f_in, f_h, f_a, f_g, f_o, f_x = (sem("f_in"), sem("f_hidden"), sem("f_act"), sem("f_gated"), sem("f_out"),
                                        sem("f_x"))
        g_first = sem("g_first_added")
        g_x, g_st = sem("g_x"), sem("g_stored")
        g_g = [sem(f"g_results{h}") for h in range(NT // 2)]

        def zero_rows(eng, engine, l, first, count):
            eng.wait_ge(t_counted, l + 1)
            for a in range(first, first + count, 8):
                n = table(engine, counts, 0, T)(a, 8)
                for i in range(8):
                    eng.dma_start(xs[l][bass.ds(n[i] + (a + i) * REGION, P), :], zeros[:, :]).then_inc(z_sent, 16)

        def table(engine, entries, at, top):
            def look_up(t, count):
                _, values = nc.values_load_multi_w_load_instructions(
                    entries[0:1, bass.ds(t + at, count)], engines=[engine], min_val=0, max_val=top,
                    skip_runtime_bounds_check_because="experts are made with a minimum against E - 1, rows and "
                                                      "counts come from the counts of at most T tokens")
                return values
            return look_up

        def scale_w2(eng, e):
            w = W2s[:, e * H0:(e + 1) * H0].rearrange("p (c d) -> p c d", c=C0)
            return eng.tensor_tensor(w, w, gB[:, 0, 1, :].unsqueeze(1).to_broadcast([P, C0, D]), ALU.mult)

        def all_row(ap, n):
            return ap.rearrange("(a n) -> a n", a=1).to_broadcast([P, n])

        def xt(t):
            return xres[:, bass.ds(t * D, D)]

        block = ctx.enter_context(nc.Block())

        @block.sync
        def _(sp):
            sp.dma_start(cT[:, :], c01).then_inc(ld_silu, 16)
            sp.dma_start(xres[:, :].rearrange("p (t d) -> p t d", d=D),
                         x.rearrange("(t p) d -> p t d", p=P)).then_inc(ld_x, 16)
            sp.dma_start(wmod[:, 0, :], wmod0).then_inc(ld_c, 16)
            sp.dma_start(wmod[:, 1, :], wmod1).then_inc(ld_c, 16)
            for k, w in enumerate((WQ, WK, WV)):
                sp.dma_start(Wa[:, k, :], w).then_inc(ld_attn, 16)
            for k, (w, b) in enumerate(((Wr0, br0), (Wr1, br1))):
                sp.dma_start(Wr[:, k, :], w).then_inc(ld_router, 16)
                sp.dma_start(brB[:, k, :], all_row(b, E)).then_inc(ld_router, 16)
            sp.dma_start(W1s.rearrange("p (e h) -> p e h", e=E), W1.rearrange("e d h -> d e h")).then_inc(ld_w0, 16)
            sp.dma_start(W2s.rearrange("p (e c d) -> p e c d", e=E, c=C0),
                         W2.rearrange("e (c p) d -> p e c d", p=P)).then_inc(ld_w0, 16)
            sp.dma_start(bias_big[:, :], all_row(b1.rearrange("e h -> (e h)"), E * H0)).then_inc(ld_w0, 16)
            sp.dma_start(b2B[:, :], all_row(b2.rearrange("e d -> (e d)"), E * D)).then_inc(ld_w0, 16)
            sp.dma_start(Wqkvb[:, :], WqkvbT).then_inc(ld_l1, 16)
            sp.dma_start(Wo[:, :, :], WoT.rearrange("(c p) d -> p c d", p=P)).then_inc(ld_l1, 16)
            for k, w in enumerate((ln_g, ln_b)):
                sp.dma_start(lnB[:, k, :], all_row(w, D)).then_inc(ld_l1, 16)
            for k, (w, b) in enumerate(((sw1, sb1), (sw3, sb3))):
                sp.dma_start(sw13[:, k, :], w).then_inc(ld_l1, 16)
                for c, (a, m) in enumerate(SC):
                    sp.dma_start(sb13[0:m, k, c:c + 1], b[a:a + m].rearrange("(p a) -> p a", a=1)).then_inc(ld_l1, 16)
            for c, (a, m) in enumerate(SC):
                sp.dma_start(sw2s[0:m, c, :], sw2[a:a + m, :]).then_inc(ld_l1, 16)
            sp.dma_start(sb2r[:, :], sb2.rearrange("(a n) -> a n", a=1)).then_inc(ld_l1, 16)
            sp.wait_ge(s_consts, 2)
            for l in range(2):
                sp.dma_start(xs[l][DUMMY:ROWS, :].rearrange("(k p) d -> p k d", p=P),
                             zeros[:, :].unsqueeze(1).to_broadcast([P, SPARE, RW])).then_inc(z_sent, 16)

            for l in range(2):
                zero_rows(sp, mybir.EngineType.SP, l, 0, (E // 2, E)[l])
                sp.wait_ge(t_ready, l + 1)
                def rows_written():
                    sp.wait_ge(z_sent, 32 + 16 * E * (l + 1))
                    for h in range(2):
                        sp.wait_ge(routers[l]["sent"][h], 16 * NT)

                def load(t, b, q, row):
                    if l or not (isinstance(t, int) and t < NB):
                        sp.wait_ge(e_xT, l * SLOTS + t - NB + 1)
                        settle(sp, passed)
                        sp.wait_ge(e_y[b], 16 * (l * (SLOTS // NB) + q))
                        settle(sp, passed)
                    sp.dma_start(xg[b], xs[l][bass.ds(row, P), :]).then_inc(e_x[b], 16)

                run_slots(sp, SLOTS, NB, [(0, load)], table(mybir.EngineType.SP, tbl, 0, ROWS - P), rows_written)
                for b in range(NB):
                    sp.wait_ge(e_y[b], 16 * (l + 1) * (SLOTS // NB))

                def weights1(t, b, q):
                    e = bass.ds(t, 1)
                    w13v = w13s.rearrange("p (e k h) -> p e k h", e=E, k=2)
                    bv = bias_big[:, 0:2 * E * H1].rearrange("p (e k h) -> p e k h", e=E, k=2)
                    for k, (w, bias) in enumerate(((w1, b1e), (w3, b3e))):
                        sp.dma_start(w13v[:, e, k, :], w[e, :, :].rearrange("e d h -> d e h")).then_inc(ld_w1, 16)
                        sp.dma_start(bv[:, e, k, :], bias[e, :].rearrange("(a e) h -> a e h", a=1)
                                     .to_broadcast([P, 1, H1])).then_inc(ld_w1, 16)
                    sp.dma_start(w2s.rearrange("p (e c d) -> p e c d", e=E, c=2)[:, e, :, :],
                                 w2[e, :, :].rearrange("e (c p) d -> p e c d", p=K1)).then_inc(ld_w1, 16)
                    sp.dma_start(b2B[:, :].rearrange("p (e d) -> p e d", e=E)[:, e, :],
                                 b2e[e, :].rearrange("(a e) d -> a e d", a=1).to_broadcast([P, 1, D])).then_inc(ld_w1, 16)

                def results(t, b, q):
                    if b % 2:
                        return
                    if not (isinstance(t, int) and t < 4):
                        sp.wait_ge(d_x, 2 * (t - 2))
                        settle(sp, passed)
                    sp.dma_start(big[:, ob + 2 * D * b:ob + 2 * D * (b + 2)].rearrange("p (a e) -> p a e", a=2),
                                 pair_rows(0, t)).then_inc(d_g[b // 2], 16)

                def pair_rows(l, t):
                    return (ys[l].rearrange("(n k) d -> n (k d)", k=TOPK)[bass.ds(t * P, 2 * P), :]
                            .rearrange("(a p) e -> p a e", a=2))

                if l == 0:
                    sp.wait_ge(e_o, SLOTS)
                    sp.wait_ge(e_yo, SLOTS)
                    run_tiles(sp, NT, 4, [(0, results), (2, weights1)])
                else:
                    for h in range(NT // 2):
                        sp.dma_start(y_all[:, 4 * D * h:4 * D * (h + 1)].rearrange("p (a e) -> p a e", a=2),
                                     pair_rows(1, 2 * h)).then_inc(g_g[h], 16)
                    for h in range(NT // 2):
                        sp.wait_ge(g_x, 2 * h + 2)
                        sp.dma_start(out[2 * h * P:2 * (h + 1) * P, :].rearrange("(a p) d -> p a d", a=2),
                                     xres[:, 2 * h * D:2 * (h + 1) * D].rearrange("p (a d) -> p a d", a=2)
                                     ).then_inc(g_st, 16)

            sp.wait_ge(g_st, 16 * (NT // 2))


        @block.gpsimd
        def _(pool):
            pool.memset(zeros[:, :], 0.0)
            pool.memset(onerow[:, :], 1.0)
            pool.memset(eps[:, :], EPS)
            pool.memset(ones[:, :], 1.0)
            pool.memset(macc[:, :, :, :], 0.0)
            pool.memset(hT[:, 0:BAND], 0.0)
            pool.memset(hT[:, BAND + T:PADT], 0.0)
            pool.memset(kT[:, 0:BAND], 0.0)
            pool.memset(kT[:, BAND + T:PADT], 0.0)
            pool.iota(result_row[:, :, :], [[TOPK * P, NT], [1, TOPK]], base=0, channel_multiplier=TOPK)
            pool.memset(ident[:, :], 0.0)
            pool.memset(band[:, :], 1.0)
            pool.memset(before[:, :], 1.0)
            pool.memset(upto[:, :], 1.0)
            pool.iota(expert_id[:, :], [[1, E]], base=0, channel_multiplier=0, allow_small_or_imprecise_dtypes=True)
            pool.iota(region_at[:, :], [[REGION, E]], base=0, channel_multiplier=0, allow_small_or_imprecise_dtypes=True)
            pool.iota(slot_id[:, :], [[0, 1]], base=0, channel_multiplier=1,
                      allow_small_or_imprecise_dtypes=True).then_inc(s_consts, 1)
            pool.wait_ge(s_consts, 1)
            pool.affine_select(out=ident[:, :], in_=ident[:, :], compare_op=ALU.not_equal, fill=1.0, base=0,
                               pattern=[[1, P]], channel_multiplier=-1)
            pool.affine_select(out=band[:, :], in_=band[:, :], compare_op=ALU.is_ge, fill=0.0, base=0,
                               pattern=[[1, WIN]], channel_multiplier=-1)
            pool.memset(zeros[:, D:RW].bitcast(I32), NOWHERE)
            pool.affine_select(out=before[:, :], in_=before[:, :], compare_op=ALU.is_ge, fill=0.0, base=-1,
                               pattern=[[1, P]], channel_multiplier=-1)
            pool.affine_select(out=upto[:, :], in_=upto[:, :], compare_op=ALU.is_ge, fill=0.0, base=0,
                               pattern=[[1, E]], channel_multiplier=-1).then_inc(s_consts, 1)
            pool.wait_ge(s_consts, 2)
            pool.affine_select(out=band[:, :], in_=band[:, :], compare_op=ALU.is_ge, fill=0.0, base=2 * BAND - 1,
                               pattern=[[-1, WIN]], channel_multiplier=1).then_inc(s_consts, 1)

            def window(t, b, q):
                pool.wait_ge(a_h, t + 1)
                after(pool, a_kv, t - 1)
                settle(pool, passed)
                pool.tensor_copy(hwin[:, b, :], hT[:, bass.ds(t * P, P)]).then_inc(a_win, 1)

            run_tiles(pool, NT, 2, [(1, window)])
            pool.wait_ge(a_kv, NT - 1)
            pool.tensor_copy(hwin[:, 0, 0:2 * BAND], hT[:, T:T + 2 * BAND]).then_inc(a_win, 1)

            run_tiles(pool, NT, 4, [(4, lambda t, b, q: pool_double(pool, router0, t, b)),
                                    (6, lambda t, b, q: pool_send(pool, router0, t, b, q))])
            pool.wait_ge(ld_w0, 64)
            biases = b2B[:, :].rearrange("p (e d) -> p e d", e=E)
            pool.tensor_tensor(biases, biases, gB[:, 0, 1, :].unsqueeze(1).to_broadcast([P, E, D]),
                               ALU.mult).then_inc(w2_scaled, E // 2)
            for e in range(E // 2, E):
                scale_w2(pool, e).then_inc(w2_scaled, 1)

            def scatter_results(l):
                def stage(t, b, q):
                    pool.wait_ge(e_yo, l * SLOTS + t + 1)
                    settle(pool, passed)
                    pool.indirect_dma_start(ys[l], bass.IndirectOffsetOnAxis(xg[b][:, D:RW].bitcast(I32), 0), yo[b], None,
                                            bounds_check=TOPK * T - 1, oob_is_err=False).then_inc(e_y[b], 16)
                return stage

            run_tiles(pool, SLOTS, NB, [(4, scatter_results(0))])

            def add_results(t, b, q):
                for k in range(TOPK):
                    pool.wait_ge(d_gy, 2 * t + k + 1)
                    after(pool, d_x, 2 * t + k)
                    pool.tensor_tensor(xt(t), xt(t), yg[b][:, k * D:(k + 1) * D], ALU.add).then_inc(d_x, 1)

            def product(t, b, q):
                pool.wait_ge(d_f, 2 * t + 2)
                f = ef[b % 2]
                pool.tensor_tensor(rf[b % 2][:, 0:HD], f[:, 0:HD], f[:, HD:2 * HD], ALU.mult).then_inc(d_qk, 1)

            def residual(t, b, q):
                pool.wait_ge(ln4["normed"], t + 1)
                pool.tensor_tensor(ya[b], ln4["xn"][b], lnG[:, 0, :], ALU.mult).then_inc(d_y, 1)
                pool.wait_ge(d_y, 3 * t + 1)
                pool.tensor_tensor(ya[b], ya[b], lnG[:, 1, :], ALU.add).then_inc(d_y, 1)
                pool.wait_ge(d_y, 3 * t + 2)
                pool.tensor_tensor(xt(t), xt(t), ya[b], ALU.add).then_inc(d_y, 1)

            run_tiles(pool, NT, 4, [(8, lambda t, b, q: pool_send(pool, router1, t, b, q)),
                                    (6, lambda t, b, q: pool_double(pool, router1, t, b)), (3, product), (4, residual),
                                    (0, add_results)])
            pool.wait_ge(ld_w1, 96 * E)
            w = w2s.rearrange("p (e d) -> p e d", d=D)
            pool.tensor_tensor(w, w, gB[0:K1, 1, 1, :].unsqueeze(1).to_broadcast([K1, 2 * E, D]),
                               ALU.mult).then_inc(w2_scaled, 1)
            run_tiles(pool, SLOTS, NB, [(4, scatter_results(1))])

        @block.scalar
        def _(act):
            act.preload_act_table_set("natural_log_exp_and_others")
            act.wait_ge(ld_silu, 16)
            act.activation(sc[:, 0, :], cT[:, :], ACT.Exp, scale=-1.0).then_inc(s_silu_act, 1)
            act.wait_ge(s_consts, 3)
            act.wait_ge(a_mv, NT)
            act.activation(r1[:, 0, :], mv1[:, :, 1], ACT.Ln, bias=eps[:, :]).then_inc(ln1["rstd"], 1)
            act.wait_ge(ln1["rstd"], 1)
            act.activation(r1[:, 1, :], r1[:, 0, :], ACT.Exp, scale=-0.5).then_inc(ln1["rstd"], 1)
            act.wait_ge(s_mod_ready, 1)

            def hidden(t, b, q):
                act.wait_ge(a_xT, t + 1)
                act.activation(hT[:, bass.ds(t * P + BAND, P)], bank[:, b, 0:P], ACT.Identity,
                               bias=mcol[:, 0, 0:1], scale=mcol[:, 0, 1:2],
                               accum_out=hsum[:, bass.ds(t, 1)]).then_inc(a_h, 1)

            def keys(t, b, q):
                act.wait_ge(a_kv, t + 1)
                act.copy(kT[:, bass.ds(t * P + BAND, P)], bank[:, 2 + b, 0:P]).then_inc(a_k, 1)

            run_tiles(act, NT, 2, [(1, hidden), (3, keys)])

            def queries(t, b, q):
                act.wait_ge(b_q, t + 1)
                after(act, b_s, t - 1)
                act.copy(qT[:, b % 2, :], bank[:, ends[b % 2], 0:P]).then_inc(b_qT, 1)

            def exps(t, b, q):
                act.wait_ge(b_nm, t + 1)
                after(act, b_pT, t - 1)
                after(act, b_ao, t - 3)
                act.activation(pr[:, b % 2, :], sm[:, b % 2, :], ACT.Exp, bias=st6[:, 1, b:b + 1],
                               accum_out=st6[:, 2, b:b + 1]).then_inc(b_p, 1)
                act.activation(st6[:, 3, b:b + 1], st6[:, 1, b:b + 1], ACT.Exp).then_inc(b_p, 1)

            def probs(t, b, q):
                act.wait_ge(b_pT, t + 1)
                after(act, b_o, t - 1)
                act.copy(pT[:, b % 2, 0:P], bank[:, 3, 0:P]).then_inc(b_pTc, 1)
                act.copy(pT[0:2 * BAND, b % 2, P:2 * P], bank[0:2 * BAND, 3, P:2 * P]).then_inc(b_pTc, 1)

            run_tiles(act, NT, 4, [
                (0, queries), (2, probs), (1, exps), (4, lambda t, b, q: act_modulate(act, router0, t, b)),
                (3, lambda t, b, q: ln_deviation(act, ln2, t, b)),
                (5, lambda t, b, q: act_exps(act, router0, t, b, q))])

            def tokens(l, scale_shift):
                def stage(t, b, q):
                    act.wait_ge(e_xT, l * SLOTS + t + 1)
                    after(act, e_h, l * SLOTS + t - 1)
                    act.activation(xgT[b % 2], bank[:, ends[b % 2], 0:P], ACT.Identity,
                                   bias=scale_shift[0], scale=scale_shift[1]).then_inc(e_xTc, 1)
                return stage

            def relu(t, b, q):
                act.wait_ge(e_hT, t + 1)
                after(act, e_o, t - 1)
                act.activation(hbT[b % 2], bank[:, 3 + b % 2, :], ACT.Relu).then_inc(e_hTc, 1)

            zero_rows(act, mybir.EngineType.Activation, 0, E // 2, E // 2)
            run_tiles(act, SLOTS, NB, [(0, tokens(0, router0["ss"])), (2, relu)])

            def gate_results(t, b, q):
                act.wait_ge(d_g[b // 2], 16 * (q + 1))
                for k in range(TOPK):
                    y = yg[b][:, k * D:(k + 1) * D]
                    g = gates[:, 0, bass.ds(t, 1), :].rearrange("p a k -> p (a k)")[:, k:k + 1]
                    act.activation(y, y, ACT.Copy, scale=g).then_inc(d_gy, 1)

            def hidden1(t, b, q):
                act.wait_ge(d_xT, t + 1)
                after(act, d_o, t - 3)
                act.activation(h3T[b], turned1, ACT.Identity,
                               bias=mcol[:, 1, 0:1], scale=mcol[:, 1, 1:2]).then_inc(d_h, 1)

            def feature_parts(k, ready, bk):
                def stage(t, b, q):
                    act.wait_ge(ready, t + 1)
                    after(act, d_sum, DS * (t - 2) + 6)
                    act.activation(rf[b % 2][:, k * HD:(k + 1) * HD], bank[:, bk:bk + 2, :].rearrange("p a n -> p (a n)"),
                                   ACT.Relu, scale=-1.0).then_inc(d_e, 1)
                    act.wait_ge(d_e, 4 * t + 2 * k + 1)
                    act.activation(ef[b % 2][:, k * HD:(k + 1) * HD], rf[b % 2][:, k * HD:(k + 1) * HD], ACT.Exp,
                                   scale=-1.0).then_inc(d_e, 1)
                return stage

            def beta_parts(t, b, q):
                act.wait_ge(d_b, t + 1)
                act.activation(eb[:, 0, :], beta, ACT.Relu, scale=-1.0).then_inc(d_eb, 1)
                act.activation(eb[:, 1, :], beta, ACT.Abs).then_inc(d_eb, 1)
                act.wait_ge(d_eb, 3 * t + 2)
                after(act, d_sum, DS * (t - 1) + 5)
                act.activation(eb[:, 2:4, :], eb[:, 0:2, :], ACT.Exp, scale=-1.0).then_inc(d_eb, 1)

            def values_turned(t, b, q):
                after(act, d_o, t)
                for k in range(2):
                    act.wait_ge(d_vT, 2 * t + k + 1)
                    act.copy(vT[:, k * 512:(k + 1) * 512], bank[:, 4 + k, :]).then_inc(d_vTc, 1)

            def keep(t, b, q):
                act.wait_ge(router1["h"], t + 1)
                act.copy(hT[:, bass.ds(t * P, P)], router1["hb"][:, b % 2, :]).then_inc(f_in, 1)

            run_tiles(act, NT, 4, [
                (3, feature_parts(0, d_q, 0)), (3, beta_parts), (3, feature_parts(1, d_k, 2)),
                (7, lambda t, b, q: act_modulate(act, router1, t, b)), (2, hidden1), (4, values_turned),
                (1, lambda t, b, q: ln_deviation(act, ln3, t, b)), (5, lambda t, b, q: ln_deviation(act, ln5, t, b)),
                (4, lambda t, b, q: ln_deviation(act, ln4, t, b)),
                (7, lambda t, b, q: act_exps(act, router1, t, b, q)), (7, keep), (0, gate_results)])

            act.preload_act_table_set("silu_and_others")

            def shared_silu(t, b, q):
                for c, (a, m) in enumerate(SC):
                    act.wait_ge(f_h, 2 * (len(SC) * t + c) + 1)
                    after(act, f_g, len(SC) * t)
                    act.activation(shT[c][0:m, :], bank[0:m, c, :], ACT.Silu,
                                   bias=sb13[0:m, 0, c:c + 1]).then_inc(f_a, 1)

            run_tiles(act, T // 512, 1, [(0, shared_silu)])

            def silu(t, b, q):
                act.wait_ge(e_hb, SLOTS + t + 1)
                act.wait_ge(e_hT, SLOTS + t - 1)
                act.activation(act1[b % 2], hb[b % 2][:, 0:H1], ACT.Silu).then_inc(e_silu, 1)

            def act_turned(t, b, q):
                act.wait_ge(e_hT, SLOTS + t + 1)
                act.wait_ge(e_o, SLOTS + t - 1)
                act.copy(hbT[b % 2][0:K1, 0:2 * P], bank[0:K1, 3 + b % 2, 0:2 * P]).then_inc(e_hTc, 1)

            run_tiles(act, SLOTS, NB, [(2, silu), (0, tokens(1, router1["ss"])), (3, act_turned)])

        @block.vector
        def _(dve):
            steps = [0]

            def link(ins):
                steps[0] += 1
                ins.then_inc(s_silu, 1)
                dve.wait_ge(s_silu, steps[0])

            dve.wait_ge(s_silu_act, 1)
            link(dve.tensor_scalar(sc[:, 1, :], sc[:, 0, :], 1.0, None, ALU.add))
            link(dve.reciprocal(sc[:, 2, :], sc[:, 1, :]))
            link(dve.tensor_tensor(sc[:, 3, :], sc[:, 2, :], cT[:, :], ALU.mult))
            dve.tensor_copy(siluB[:, :, :], sc[:, 3, :].unsqueeze(2).to_broadcast([P, 2, P])).then_inc(s_mod_used, 1)

            dve.wait_ge(ld_x, 16)
            settle(dve, passed)
            for t in range(NT):
                dve.bn_stats(stats1[:, t, :], xt(t)).then_inc(ln1["moments"], 1)
            dve.wait_ge(ln1["moments"], NT)
            settle(dve, passed)
            for t in range(NT):
                dve.bn_aggr(mv1[:, t, :], stats1[:, t, :]).then_inc(a_mv, 1)
            dve.wait_ge(s_mod, 1)
            cols = bank[:, 4, 0:8].rearrange("p (l k i) -> p l k i", l=2, k=2)
            mcols = mcol[:, :, :].rearrange("p l (k i) -> p l k i", k=2)
            dve.tensor_scalar(mcols[:, :, :, 0], cols[:, :, :, 0], 1.0, None, ALU.mult).then_inc(s_silu, 1)
            dve.tensor_scalar(mcols[:, :, :, 1], cols[:, :, :, 1], 1.0, None, ALU.add).then_inc(s_silu, 1)
            steps[0] += 2
            g = bank[:, 0:4, 0:D]
            link(dve.tensor_scalar(gtmp[:, 0, :, :], g, -1.0, None, ALU.mult))
            link(dve.tensor_tensor(gtmp[:, 1, :, :], gtmp[:, 0, :, :], g, ALU.max))
            link(dve.tensor_scalar(gtmp[:, 0, :, :], gtmp[:, 1, :, :], 0.25, None, ALU.max))
            link(dve.tensor_scalar(gtmp[:, 2, :, :], g, 0.0, 2.0, ALU.is_ge, ALU.mult))
            link(dve.scalar_tensor_tensor(gB[:, :, :, :].rearrange("p l k n -> p (l k) n"), gtmp[:, 2, :, :], -1.0,
                                          gtmp[:, 0, :, :], ALU.add, ALU.mult))
            dve.wait_ge(ld_attn, 48)
            dve.tensor_tensor(Wa[:, 2, :], Wa[:, 2, :], gB[:, 0, 0, :], ALU.mult).then_inc(s_mod_ready, 1)

            dve.wait_ge(s_consts, 3)

            def values(t, b, q):
                dve.wait_ge(a_kv, t + 1)
                dve.tensor_copy(V[:, bass.ds(t * D, D)], bank[:, 4 + b, 0:D]).then_inc(a_v, 1)

            def scale_all(t, b, q):
                dve.wait_ge(ln1["rstd"], 2)
                after(dve, a_xT, t - 1)
                dve.tensor_scalar(ln1["xn"][b], xt(t), mv1[:, bass.ds(t, 1), :].rearrange("p a k -> p (a k)")[:, 0:1],
                                  r1[:, 1, bass.ds(t, 1)], ALU.subtract, ALU.mult).then_inc(ln1["normed"], 1)

            run_tiles(dve, NT, 2, [(0, scale_all), (3, values)])
            dve.wait_ge(a_kv, NT + 1)
            dve.tensor_copy(V[0:2 * BAND, NT * D:(NT + 1) * D], bank[0:2 * BAND, 4, 0:D]).then_inc(a_v, 1)
            dve.wait_ge(a_h, NT)
            dve.reduce_sum(st6[:, 0, 0:1], hsum[:, :], AX_X).then_inc(a_hs, 1)
            dve.wait_ge(a_hs, 1)
            dve.tensor_copy(hsumB[:, :], st6[:, 0, 0:1].to_broadcast([P, P])).then_inc(a_hs, 1)
            dve.wait_ge(a_vt, 1)
            dve.tensor_copy(vtot[:, :], bank[:, 6, 0:D]).then_inc(a_vtc, 1)
            dve.wait_ge(a_vtc, 1)

            def masked(t, b, q):
                dve.wait_ge(b_s, t + 1)
                after(dve, b_p, 2 * (t - 1) - 1)
                settle(dve, passed)
                dve.tensor_tensor_reduce(sm[:, b % 2, :], bank[:, 1 + b % 2, 0:WIN], band[:, :],
                                         float(D) ** -0.5, 0.0, ALU.mult, ALU.max, st6[:, 0, b:b + 1]).then_inc(b_sm, 1)

            def negated(t, b, q):
                dve.wait_ge(b_sm, t + 1)
                dve.tensor_scalar(st6[:, 1, b:b + 1], st6[:, 0, b:b + 1], -1.0, None, ALU.mult).then_inc(b_nm, 1)

            def excess(t, b, q):
                dve.wait_ge(b_p, 2 * t + 2)
                dve.tensor_scalar(pr[:, b % 2, :], pr[:, b % 2, :], st6[:, 3, b:b + 1], None,
                                  ALU.subtract).then_inc(b_pp, 1)
                dve.scalar_tensor_tensor(st6[:, 4, b:b + 1], st6[:, 3, b:b + 1], float(T - WIN), st6[:, 2, b:b + 1],
                                         ALU.mult, ALU.add).then_inc(b_pp, 1)

            def inverse(t, b, q):
                dve.wait_ge(b_pp, 3 * t + 2)
                dve.reciprocal(st6[:, 5, b:b + 1], st6[:, 4, b:b + 1]).then_inc(b_pp, 1)

            def attended(t, b, q):
                dve.wait_ge(b_o, t + 1)
                dve.wait_ge(b_pp, 3 * t + 3)
                dve.scalar_tensor_tensor(ao[:, :], vtot[:, :], st6[:, 3, b:b + 1], bank[:, 4, 0:D],
                                         ALU.mult, ALU.add).then_inc(b_ao, 1)

            def add_attended(t, b, q):
                dve.wait_ge(b_ao, t + 1)
                dve.scalar_tensor_tensor(xt(t), ao[:, :], st6[:, 5, b:b + 1], xt(t), ALU.mult, ALU.add).then_inc(b_x, 1)

            def measure2(t, b, q):
                dve.wait_ge(b_x, t + 1)
                ln_stats(dve, ln2, xt(t), t, b)

            def norm2(t, b, q):
                after(dve, router0["doubled"], 2 * (t - 4) + 1)
                ln_scale(dve, ln2, xt(t), t, b)

            picks, places = pick_parts(dve, router0), place_parts(dve, router0)
            run_tiles(dve, NT, 4, [
                (2, excess), (1, masked), (3, attended), (6, places[0]), (2, inverse), (6, places[1]), (1, negated),
                (3, add_attended), (4, norm2), (6, places[2]), (3, measure2), (6, places[3]),
                (3, lambda t, b, q: ln_moments(dve, ln2, t, b)), (5, picks[0]), (5, picks[1]), (5, picks[2]),
                (5, picks[3]), (5, picks[4]), (5, picks[5])])

            def slot_table(l):
                r = routers[l]
                k0 = 11 * l

                def step(k, ins):
                    ins.then_inc(t_dve, 1)
                    dve.wait_ge(t_dve, k0 + k)

                dve.wait_ge(t_cnt, l + 1)
                dve.tensor_copy(counts[:, :], count_row).then_inc(t_counted, 1)
                step(1, dve.tensor_scalar(tiles_int[:, 0, :], by_row, float(P - 1), None, ALU.add))
                step(2, dve.tensor_scalar(tiles_int[:, 1, :], tiles_int[:, 0, :], 7, None, ALU.logical_shift_right))
                step(3, dve.tensor_copy(tiles_per[:, :], tiles_int[:, 1, :]))
                dve.wait_ge(t_cum, l + 1)
                step(4, dve.tensor_copy(cumt[:, 0, :], cumulated))
                step(5, dve.tensor_scalar(cumt[:, 1, :], cumt[:, 0, :], slot_id[:, :], None, ALU.is_le))
                step(6, dve.tensor_tensor(cumt[:, 2, :], cumt[:, 0, :], cumt[:, 1, :], ALU.mult))
                step(7, dve.reduce_sum(sl[:, 0:1], cumt[:, 1, :], AX_X))
                step(8, dve.reduce_max(sl[:, 1:2], cumt[:, 2, :], AX_X))
                step(9, dve.tensor_scalar(sl[:, 2:3], sl[:, 1:2], slot_id[:, :], -float(P), ALU.subtract, ALU.mult))
                step(10, dve.scalar_tensor_tensor(slot_vals[:, 0:1], sl[:, 0:1], float(REGION), sl[:, 2:3],
                                                  ALU.mult, ALU.add))
                step(11, dve.tensor_scalar(slot_vals[:, 1:2], sl[:, 0:1], float(E - 1), None, ALU.min))
                dve.wait_ge(t_val, l + 1)
                dve.tensor_copy(tbl[:, :], value_row).then_inc(t_ready, 1)
                dve.wait_ge(t_ready, l + 1)

            slot_table(0)

            def biased(l, width):
                def stage(t, b, q, e):
                    dve.wait_ge(e_h, l * SLOTS + t + 1)
                    after(dve, e_hT, t - 1) if l == 0 else after(dve, e_act, t - 1)
                    dve.tensor_tensor(hb[b % 2][:, 0:width], bank[:, 1 + b % 2, 0:width],
                                      bias_big[:, bass.ds(e * width, width)], ALU.add).then_inc(e_hb, 1)
                return stage

            def result(l):
                def stage(t, b, q, e):
                    dve.wait_ge(e_o, l * SLOTS + t + 1)
                    if l or not (isinstance(t, int) and t < NB):
                        dve.wait_ge(e_y[b], 16 * (l * (SLOTS // NB) + q))
                    dve.tensor_tensor(yo[b], bank[:, 5 + b % 2, 0:D], b2B[:, bass.ds(e * D, D)],
                                      ALU.add).then_inc(e_yo, 1)
                return stage

            dve.wait_ge(ld_w0, 64)
            for e in range(E // 2):
                scale_w2(dve, e).then_inc(w2_low, 1)
            dve.wait_ge(w2_scaled, E // 2)
            experts = table(mybir.EngineType.DVE, tbl, P, E - 1)
            run_slots(dve, SLOTS, NB, [(1, biased(0, H0)), (3, result(0))], experts)

            dve.wait_ge(ld_l1, 16 * (4 + 2 * (1 + len(SC)) + len(SC) + 1))
            for k in range(2):
                link(dve.tensor_tensor(lnG[:, k, :], lnB[:, k, :], gB[:, 1, 0, :], ALU.mult))
            for c, (a, m) in enumerate(SC):
                link(dve.tensor_tensor(sw2s[0:m, c, :], sw2s[0:m, c, :], gB[0:m, 1, 1, :], ALU.mult))
            link(dve.tensor_tensor(sb2r[:, :], sb2r[:, :], gB[0:1, 1, 1, :], ALU.mult))

            def measure3(t, b, q):
                dve.wait_ge(d_x, 2 * t + 2)
                ln_stats(dve, ln3, xt(t), t, b)

            def feature(k):
                def stage(t, b, q):
                    dve.wait_ge(d_e, 4 * t + 2 * k + 2)
                    dve.scalar_tensor_tensor(ef[b % 2][:, k * HD:(k + 1) * HD],
                                             bank[:, 2 * k:2 * k + 2, :].rearrange("p a n -> p (a n)"), 0.0,
                                             ef[b % 2][:, k * HD:(k + 1) * HD], ALU.max, ALU.add).then_inc(d_f, 1)
                return stage

            def feature_sums(t, b, q):
                dve.wait_ge(d_f, 2 * t + 2)
                dve.reduce_sum(qk_sums[:, :, :], ef[b % 2].rearrange("p (k h d) -> p k h d", k=2, h=NH), AX_X).then_inc(d_sum, 1)

            def sums_product(t, b, q):
                dve.wait_ge(d_sum, DS * t + 1)
                dve.tensor_tensor(sums[:, 1, :], qk_sums[:, 0, :], qk_sums[:, 1, :], ALU.mult).then_inc(d_sum, 1)

            def sigmoid_product(t, b, q):
                dve.wait_ge(d_eb, 3 * t + 3)
                dve.wait_ge(d_sum, DS * t + 2)
                dve.scalar_tensor_tensor(sums[:, 2, :], eb[:, 3, :], 1.0, sums[:, 1, :], ALU.add, ALU.mult
                                         ).then_inc(d_sum, 1)

            def sigmoid_inverse(t, b, q):
                dve.wait_ge(d_sum, DS * t + 3)
                dve.reciprocal(sums[:, 3, :], sums[:, 2, :]).then_inc(d_sum, 1)

            def sigmoid(t, b, q):
                dve.wait_ge(d_sum, DS * t + 4)
                dve.tensor_tensor(sums[:, 4, :], sums[:, 3, :], eb[:, 2, :], ALU.mult).then_inc(d_sum, 1)

            def qk_reduced(t, b, q):
                dve.wait_ge(d_qk, t + 1)
                dve.reduce_sum(sums[:, 0, :], rf[b % 2][:, 0:HD].rearrange("p (h d) -> p h d", h=NH), AX_X).then_inc(d_sum, 1)

            def coefficient(t, b, q):
                dve.wait_ge(d_sum, DS * t + 6)
                dve.scalar_tensor_tensor(sums[:, 5, :], sums[:, 0, :], float(DH) ** -0.5, sums[:, 4, :],
                                         ALU.mult, ALU.mult).then_inc(d_sum, 1)

            def weighted(t, b, q):
                k0 = DS * t
                dve.wait_ge(d_sum, k0 + 7)
                dve.wait_ge(d_v, t + 1)
                after(dve, d_vT, 2 * t)
                for k in range(2):
                    n = NH // 2
                    dve.tensor_tensor(vc[:, k * 512:(k + 1) * 512].rearrange("p (h d) -> p h d", h=n),
                                      bank[:, 4 + k, :].rearrange("p (h d) -> p h d", h=n),
                                      sums[:, 5, k * n:(k + 1) * n].unsqueeze(2).to_broadcast([P, n, DH]),
                                      ALU.mult).then_inc(d_sum, 1)

            def measure4(t, b, q):
                dve.wait_ge(d_o, t + 1)
                ln_stats(dve, ln4, attn1, t, b)

            def scale4(t, b, q):
                after(dve, d_y, 3 * (t - 2) + 1)
                ln_scale(dve, ln4, attn1, t, b)

            def measure5(t, b, q):
                dve.wait_ge(d_y, 3 * t + 3)
                ln_stats(dve, ln5, xt(t), t, b)

            def norm5(t, b, q):
                wait_rows_sent(dve, router1, t, b)
                ln_scale(dve, ln5, xt(t), t, b)

            picks, places = pick_parts(dve, router1), place_parts(dve, router1)
            run_tiles(dve, NT, 4, [
                (8, places[0]), (6, norm5), (8, places[1]), (1, measure3), (8, places[2]), (5, measure5),
                (8, places[3]), (1, lambda t, b, q: ln_moments(dve, ln3, t, b)),
                (5, lambda t, b, q: ln_moments(dve, ln5, t, b)), (3, feature(0)), (7, picks[0]), (3, feature(1)),
                (7, picks[1]), (3, feature_sums), (7, picks[2]), (3, sums_product), (4, measure4),
                (3, sigmoid_product), (7, picks[3]), (4, lambda t, b, q: ln_moments(dve, ln4, t, b)),
                (3, sigmoid_inverse), (1, lambda t, b, q: ln_scale(dve, ln3, xt(t), t, b)), (3, sigmoid),
                (7, picks[4]), (3, qk_reduced), (7, picks[5]), (3, coefficient), (4, scale4), (3, weighted)])
            slot_table(1)

            def shared(t, b, q):
                for c, (a, m) in enumerate(SC):
                    dve.wait_ge(f_h, 2 * (len(SC) * t + c) + 2)
                    dve.wait_ge(f_a, len(SC) * t + c + 1)
                    after(dve, f_o, t)
                    dve.scalar_tensor_tensor(shT[len(SC) + c][0:m, :], bank[0:m, 3 + c, :], sb13[0:m, 1, c:c + 1],
                                             shT[c][0:m, :], ALU.add, ALU.mult).then_inc(f_g, 1)
                dve.wait_ge(f_o, t + 1)
                xi = xres[:, bass.ds(t * 512, 512)]
                dve.tensor_tensor(xi, xi, bank[:, 6, :], ALU.add).then_inc(f_x, 1)

            run_tiles(dve, T // 512, 1, [(0, shared)])

            def gated(t, b, q, e):
                dve.wait_ge(e_silu, t + 1)
                dve.tensor_tensor(act1[b % 2], act1[b % 2], hb[b % 2][:, H1:2 * H1], ALU.mult).then_inc(e_act, 1)

            dve.wait_ge(ld_w1, 96 * E)
            link(dve.tensor_tensor(b2B[:, :].rearrange("p (e d) -> p e d", e=E), b2B[:, :].rearrange("p (e d) -> p e d", e=E),
                                   gB[:, 1, 1, :].unsqueeze(1).to_broadcast([P, E, D]), ALU.mult))
            run_slots(dve, SLOTS, NB, [(1, biased(1, 2 * H1)), (4, result(1)), (2, gated)], experts)

            def add_result(t, k):
                y = y_all[:, (2 * t + k) * D:(2 * t + k + 1) * D]
                dve.scalar_tensor_tensor(xt(t), y, gates[:, 1, t, k:k + 1], xt(t),
                                         ALU.mult, ALU.add).then_inc((g_first, g_x)[k], 1)

            for h in range(NT // 2):
                dve.wait_ge(g_g[h], 16)
                for t in (2 * h, 2 * h + 1):
                    add_result(t, 0)
                for t in (2 * h, 2 * h + 1):
                    dve.wait_ge(g_first, t + 1)
                    add_result(t, 1)

        @block.tensor
        def _(pe):
            pe.wait_ge(s_mod_used, 1)
            pe.wait_ge(ld_c, 32)
            for l in range(2):
                for k in range(2):
                    pe.matmul(bank[:, 2 * l + k, 0:D], siluB[:, l, :], wmod[:, l, (3 * k + 2) * D:(3 * k + 3) * D],
                              start=True, stop=True)
                    for i in range(2):
                        c = 4 * l + 2 * k + i
                        last = pe.matmul(bank[:, 4, c:c + 1], wmod[:, l, (3 * k + i) * D:(3 * k + i + 1) * D],
                                         sc[:, 3, l:l + 1], start=True, stop=True)
            last.then_inc(s_mod, 1)
            pe.wait_ge(s_mod_ready, 1)
            pe.wait_ge(s_consts, 3)
            pe.wait_ge(ld_attn, 48)

            def turn(t, b, q):
                pe.wait_ge(ln1["normed"], t + 1)
                after(pe, a_h, t - 1)
                pe.transpose(bank[:, b, 0:P], ln1["xn"][b], ident[:, :]).then_inc(a_xT, 1)

            def keys_values(t, b, q):
                pe.wait_ge(a_h, t + 1)
                pe.wait_ge(a_win, t + 1)
                after(pe, a_k, t - 1)
                after(pe, a_v, t - 1)
                pe.matmul(bank[:, 2 + b, 0:P], Wa[:, 1, :], hT[:, bass.ds(t * P + BAND, P)], start=True, stop=True)
                pe.matmul(bank[:, 4 + b, 0:D], hwin[:, b, :], Wa[:, 2, :], start=True, stop=True).then_inc(a_kv, 1)

            run_tiles(pe, NT, 2, [(0, turn), (2, keys_values)])
            pe.wait_ge(a_win, NT + 1)
            pe.wait_ge(a_v, NT - 1)
            pe.matmul(bank[0:2 * BAND, 4, 0:D], hwin[:, 0, 0:2 * BAND], Wa[:, 2, :], start=True, stop=True).then_inc(a_kv, 1)
            pe.wait_ge(a_hs, 2)
            pe.matmul(bank[:, 6, 0:D], hsumB[:, :], Wa[:, 2, :], start=True, stop=True).then_inc(a_vt, 1)
            pe.wait_ge(a_vtc, 1)
            pe.wait_ge(a_k, NT)
            pe.wait_ge(a_v, NT + 1)
            pe.wait_ge(ld_router, 64)

            def query(t, b, q):
                after(pe, b_qT, t - 1)
                pe.matmul(bank[:, ends[b % 2], 0:P], Wa[:, 0, :], hT[:, bass.ds(t * P + BAND, P)],
                          start=True, stop=True).then_inc(b_q, 1)

            def score(t, b, q):
                pe.wait_ge(b_qT, t + 1)
                after(pe, b_sm, t - 1)
                pe.matmul(bank[:, 1 + b % 2, 0:WIN], qT[:, b % 2, :], kT[:, bass.ds(t * P, WIN)],
                          start=True, stop=True).then_inc(b_s, 1)

            def turn_probs(t, b, q):
                pe.wait_ge(b_pp, 3 * t + 1)
                after(pe, b_pTc, 2 * t)
                pe.transpose(bank[:, 3, 0:P], pr[:, b % 2, 0:P], ident[:, :])
                pe.transpose(bank[0:2 * BAND, 3, P:2 * P], pr[:, b % 2, P:WIN],
                             ident[:, :]).then_inc(b_pT, 1)

            def attend(t, b, q):
                pe.wait_ge(b_pTc, 2 * t + 2)
                after(pe, b_ao, t)
                o = bank[:, 4, 0:D]
                pe.matmul(o, pT[:, b % 2, 0:P], V[:, bass.ds(t * D, D)], start=True, stop=False)
                pe.matmul(o, pT[0:2 * BAND, b % 2, P:2 * P], V[0:2 * BAND, bass.ds(t * D + D, D)],
                          start=False, stop=True).then_inc(b_o, 1)

            def router_logits0(t, b, q):
                if b % 2 == 0 and not (isinstance(t, int) and t < 2):
                    pe.wait_ge(router0["placed"], RANK * (2 * q + b // 2 - 1) + 1)
                pe_logits(pe, router0, t, b)

            run_tiles(pe, NT, 4, [
                (1, score), (3, attend), (0, query), (6, lambda t, b, q: pe_rank(pe, router0, t, b, q)),
                (2, turn_probs), (5, router_logits0), (4, lambda t, b, q: pe_transpose(pe, router0, t, b))])

            def slot_counts(l):
                r = routers[l]
                pe.wait_ge(r["placed"], RANK * (NT // 2))
                pe.matmul(count_row, ones[:, 0:1], macc[:, l, 0, :], start=True, stop=False)
                pe.matmul(count_row, ones[:, 0:1], macc[:, l, 1, :], start=False, stop=True)
                pe.matmul(by_row, macc[:, l, 0, :], ones[:, :], start=True, stop=False)
                pe.matmul(by_row, macc[:, l, 1, :], ones[:, :], start=False, stop=True).then_inc(t_cnt, 1)
                pe.wait_ge(t_dve, 11 * l + 3)
                pe.matmul(cumulated, tiles_per[:, :], upto[:, :], start=True, stop=True).then_inc(t_cum, 1)
                pe.wait_ge(t_dve, 11 * l + 11)
                for k in range(2):
                    last = pe.matmul(value_row[:, k * P:(k + 1) * P], slot_vals[:, k:k + 1], ident[:, :],
                                     start=True, stop=True)
                last.then_inc(t_val, 1)
                pe.wait_ge(t_ready, l + 1)

            slot_counts(0)

            experts = table(mybir.EngineType.PE, tbl, P, E - 1)

            def slot_turn(l):
                def stage(t, b, q, e):
                    pe.wait_ge(e_x[b], 16 * (l * (SLOTS // NB) + q + 1))
                    after(pe, e_xTc, l * SLOTS + t - 1)
                    pe.transpose(bank[:, ends[b % 2], 0:P], xg[b][:, 0:D], ident[:, :]).then_inc(e_xT, 1)
                return stage

            def slot_hidden(l, w, width):
                def stage(t, b, q, e):
                    pe.wait_ge(e_xTc, l * SLOTS + t + 1)
                    after(pe, e_hb, l * SLOTS + t - 1)
                    pe.matmul(bank[:, 1 + b % 2, 0:width], xgT[b % 2], w[:, bass.ds(e * width, width)],
                              start=True, stop=True).then_inc(e_h, 1)
                return stage

            def slot_turn_hidden(t, b, q, e):
                pe.wait_ge(e_hb, t + 1)
                after(pe, e_hTc, t - 1)
                for c in range(C0):
                    last = pe.transpose(bank[:, 3 + b % 2, c * P:(c + 1) * P], hb[b % 2][:, c * P:(c + 1) * P], ident[:, :])
                last.then_inc(e_hT, 1)

            def slot_out(t, b, q, e):
                if isinstance(t, int) and t == 0:
                    pe.wait_ge(w2_scaled, E)
                pe.wait_ge(e_hTc, t + 1)
                after(pe, e_yo, t - 1)
                for c in range(C0):
                    last = pe.matmul(bank[:, 5 + b % 2, 0:D], hbT[b % 2][:, c * P:(c + 1) * P],
                                     W2s[:, bass.ds(e * H0 + c * D, D)], start=(c == 0), stop=(c == C0 - 1))
                last.then_inc(e_o, 1)

            def weights_ready():
                pe.wait_ge(ld_w0, 64)
                pe.wait_ge(w2_low, E // 2)

            run_slots(pe, SLOTS, NB, [(1, slot_hidden(0, W1s, H0)), (0, slot_turn(0)), (2, slot_turn_hidden),
                                      (3, slot_out)], experts, weights_ready)
            pe.wait_ge(e_yo, SLOTS)

            pe.wait_ge(ld_l1, 16 * (4 + 2 * (1 + len(SC)) + len(SC) + 1))

            def turn1(t, b, q):
                pe.wait_ge(ln3["normed"], t + 1)
                after(pe, d_h, t)
                after(pe, d_eb, 3 * t)
                pe.transpose(turned1, ln3["xn"][b], ident[:, :]).then_inc(d_xT, 1)

            def project(k, s):
                def stage(t, b, q):
                    pe.wait_ge(d_h, t + 1)
                    after(pe, d_f, 2 * (t - 1) + k + 1) if k < 2 else after(pe, d_vTc, 2 * t)
                    for i in range(2):
                        last = pe.matmul(bank[:, 2 * k + i, :], h3T[b], Wqkvb[:, k * HD + i * 512:k * HD + (i + 1) * 512],
                                         start=True, stop=True)
                    last.then_inc(s, 1)
                return stage

            def project_beta(t, b, q):
                pe.matmul(beta, h3T[b], Wqkvb[:, 3 * HD:3 * HD + NH], start=True, stop=True).then_inc(d_b, 1)

            def turn_values(t, b, q):
                pe.wait_ge(d_sum, DS * (t + 1))
                for k in range(2):
                    for c in range(4):
                        last = pe.transpose(bank[:, 4 + k, c * P:(c + 1) * P], vc[:, (4 * k + c) * P:(4 * k + c + 1) * P],
                                            ident[:, :])
                    last.then_inc(d_vT, 1)

            def attn_out(t, b, q):
                pe.wait_ge(d_vTc, 2 * t + 2)
                if b % 2 == 0 and not (isinstance(t, int) and t < 4):
                    pe.wait_ge(router1["picked"], PICK * (2 * q + b // 2 - 2) + 1)
                pe.matmul(attn1, h3T[b], ident[:, :], start=True, stop=False)
                for c in range(HD // P):
                    last = pe.matmul(attn1, vT[:, c * P:(c + 1) * P], Wo[:, c, :],
                                     start=False, stop=(c == HD // P - 1))
                last.then_inc(d_o, 1)

            def rank1(t, b, q):
                pe.wait_ge(ln4["normed"], min(t + 4, NT) if isinstance(t, int) else t + 4)
                pe_rank(pe, router1, t, b, q)

            def router_turn1(t, b, q):
                pe.wait_ge(ln4["normed"], min(t + 3, NT) if isinstance(t, int) else t + 3)
                if b % 2 == 0 and not (isinstance(t, int) and t < 2):
                    pe.wait_ge(router1["placed"], RANK * (2 * q + b // 2 - 1) + 1)
                pe_transpose(pe, router1, t, b)

            def shared_chunk(t, c):
                a, m = SC[c]
                after(pe, f_g, len(SC) * t)
                for k in range(2):
                    pe.matmul(bank[0:m, 3 * k + c, :], sw13[:, k, a:a + m], hT[:, bass.ds(t * 512, 512)],
                              start=True, stop=True).then_inc(f_h, 1)

            def first_chunk(c):
                def stage(t, b, q):
                    if isinstance(t, int) and t == NT - 1:
                        pe.wait_ge(f_in, 4)
                        shared_chunk(0, c)
                return stage

            run_tiles(pe, NT, 4, [
                (3, project(0, d_q)), (3, project(1, d_k)), (3, project_beta), (8, rank1), (7, router_turn1),
                (4, turn_values), (2, turn1), (7, lambda t, b, q: pe_logits(pe, router1, t, b)), (4, attn_out),
                (3, project(2, d_v))] + [(5 + c, first_chunk(c)) for c in range(len(SC))])

            def shared_hidden(t, b, q):
                pe.wait_ge(f_in, 4 * t + 4)
                for c in range(len(SC)):
                    shared_chunk(t, c)

            def shared_out(t, b, q):
                pe.wait_ge(f_g, len(SC) * (t + 1))
                after(pe, f_x, t)
                for i in range(4):
                    o = bank[:, 6, i * D:(i + 1) * D]
                    pe.matmul(o, onerow[:, :], sb2r[:, :], start=True, stop=False)
                    for c, (a, m) in enumerate(SC):
                        last = pe.matmul(o, shT[len(SC) + c][0:m, i * P:(i + 1) * P], sw2s[0:m, c, :],
                                         start=False, stop=(c == len(SC) - 1))
                last.then_inc(f_o, 1)

            pe.wait_ge(d_eb, 3 * NT)
            slot_counts(1)
            run_tiles(pe, T // 512, 1, [
                (0, lambda t, b, q: None if isinstance(t, int) and t == 0 else shared_hidden(t, b, q)), (0, shared_out)])
            pe.wait_ge(f_x, T // 512)

            def slot_turn_act(t, b, q, e):
                pe.wait_ge(e_act, t + 1)
                after(pe, e_hTc, SLOTS + t - 1)
                for c in range(2):
                    last = pe.transpose(bank[0:K1, 3 + b % 2, c * P:(c + 1) * P], act1[b % 2][:, c * K1:(c + 1) * K1],
                                        ident[:, :])
                last.then_inc(e_hT, 1)

            def slot_out1(t, b, q, e):
                pe.wait_ge(e_hTc, SLOTS + t + 1)
                after(pe, e_yo, SLOTS + t - 1)
                for c in range(2):
                    last = pe.matmul(bank[:, 5 + b % 2, 0:D], hbT[b % 2][0:K1, c * P:(c + 1) * P],
                                     w2s[:, bass.ds(e * 2 * D + c * D, D)], start=(c == 0), stop=(c == 1))
                last.then_inc(e_o, 1)

            pe.wait_ge(ld_w1, 96 * E)
            pe.wait_ge(w2_scaled, E + 1)
            run_slots(pe, SLOTS, NB, [(1, slot_hidden(1, w13s, 2 * H1)), (0, slot_turn(1)), (3, slot_turn_act),
                                      (4, slot_out1)], experts)


def kernel(**inputs):
    import numpy as np
    import concourse.bacc as bacc
    from concourse.bass_utils import run_bass_kernel_spmd

    a = {k: np.ascontiguousarray(v) for k, v in inputs.items()}
    T, D = a["L0_attn_inputs"].shape[1:]
    NH, DH = 16, 64
    qkvb = a["L1_attn_W_qkvb"].reshape(NH, 3 * DH + 1, D)
    blocks = [qkvb[:, k * DH:(k + 1) * DH].reshape(NH * DH, D) for k in range(3)] + [qkvb[:, 3 * DH]]
    f = "L1_ffn_"
    arrays = {
        "x": a["L0_attn_inputs"].reshape(T, D), "WQ": a["L0_attn_WQ"], "WK": a["L0_attn_WK"], "WV": a["L0_attn_WV"],
        "Wr0": a["L0_ffn_Wr"], "br0": a["L0_ffn_br"], "W1": a["L0_ffn_W1"], "b1": a["L0_ffn_b1"],
        "W2": a["L0_ffn_W2"], "b2": a["L0_ffn_b2"],
        "c01": np.stack([a["L0_c"].reshape(D), a["L1_c"].reshape(D)], axis=1),
        "wmod0": a["L0_wmod"], "wmod1": a["L1_wmod"],
        "WqkvbT": np.concatenate(blocks, axis=0).T, "WoT": a["L1_attn_W_o"].T,
        "ln_g": a["L1_attn_ln_g"], "ln_b": a["L1_attn_ln_b"],
        "Wr1": a[f + "gate_w"], "br1": a[f + "gate_b"], "w1": a[f + "w1"], "b1e": a[f + "b1"],
        "w3": a[f + "w3"], "b3e": a[f + "b3"], "w2": a[f + "w2"], "b2e": a[f + "b2"],
        "sw1": a[f + "sw1"], "sb1": a[f + "sb1"], "sw3": a[f + "sw3"], "sb3": a[f + "sb3"],
        "sw2": a[f + "sw2"], "sb2": a[f + "sb2"],
    }
    nc = bacc.Bacc("TRN2", target_bir_lowering=False, num_devices=1)
    feed, args = {}, {}
    for name, v in arrays.items():
        v = np.ascontiguousarray(v)
        feed[f"in_{name}"] = v
        args[name] = nc.dram_tensor(f"in_{name}", v.shape, mybir.dt.from_np(v.dtype), kind="ExternalInput").ap()
    args["out"] = nc.dram_tensor("out_x", (T, D), F32, kind="ExternalOutput").ap()
    build(nc, **args)
    r = run_bass_kernel_spmd(nc, [feed], core_ids=[0])
    return r.results[0]["out_x"].reshape(1, T, D)
```
